# Optimizing a Trainium2 kernel written in Bass

```python
import numpy as np
import jax
import jax.numpy as jnp

def _softmax(x, axis=-1):
    return jax.nn.softmax(x, axis=axis)

def _gelu(x):
    return jax.nn.gelu(x, approximate=True)

def _silu(x):
    return jax.nn.silu(x)

def _sigmoid(x):
    return jax.nn.sigmoid(x)

def _layernorm(x, axis=-1, eps=1e-05):
    m = jnp.mean(x, axis=axis, keepdims=True)
    v = jnp.var(x, axis=axis, keepdims=True)
    return (x - m) / jnp.sqrt(v + eps)

def _scatter_add(tgt, idx, src, axis=0):
    return tgt.at[idx].add(src)

def _segment_sum(src, seg, n):
    return jax.ops.segment_sum(src, seg, n)
kernel_name = 'mk_conv_attn_hybrid_d4_conv_nchw256_r4_712b72'

def setup_inputs(seed: int=0):
    np.random.seed(seed)
    _w = jnp.asarray

    def _rec_inputs():
        import jax
        import jax.numpy as jnp
        _gk = jax.random.key(seed)
        x = -0.000125 + 0.9999 * jax.random.normal(jax.random.fold_in(_gk, 1), (32, 64, 16, 16), jnp.float32)
        return x
    x = _rec_inputs()

    def _L0_conv_setup():
        import jax, jax.numpy as jnp
        import numpy as np
        B, C, H, Wd = (32, 64, 16, 16)
        key = jax.random.key(seed)
        k1, k2, k3 = jax.random.split(key, 3)
        x = jax.random.normal(k1, (B, C, H, Wd), dtype=jnp.float32)
        W = jax.random.normal(k2, (C, 4), dtype=jnp.float32) * 0.5
        b = jax.random.normal(k3, (C,), dtype=jnp.float32) * 0.1
        return {'x': x, 'W': W, 'b': b}
    _L0_conv_all = _L0_conv_setup()
    _L0_conv_in = {k: v for k, v in _L0_conv_all.items() if k in ('W', 'b')}
    del _L0_conv_all

    def _L1_conv_setup():
        import jax, jax.numpy as jnp
        import numpy as np
        from jax import lax
        NUM_HEADS = 8
        FOCUSING_FACTOR = 3.0
        KERNEL_SIZE = 5
        key = jax.random.key(seed)
        ks = jax.random.split(key, 9)
        B, C, H, W = (16, 64, 16, 16)
        s = 0.02
        return {'x': jax.random.normal(ks[0], (B, C, H, W), dtype=jnp.float32), 'Wq': jax.random.normal(ks[1], (C, C), dtype=jnp.float32) * s, 'bq': jax.random.normal(ks[2], (C,), dtype=jnp.float32) * s, 'Wkv': jax.random.normal(ks[3], (2 * C, C), dtype=jnp.float32) * s, 'bkv': jax.random.normal(ks[4], (2 * C,), dtype=jnp.float32) * s, 'Wproj': jax.random.normal(ks[5], (C, C), dtype=jnp.float32) * s, 'bproj': jax.random.normal(ks[6], (C,), dtype=jnp.float32) * s, 'dwc_w': jax.random.normal(ks[7], (C // NUM_HEADS, 1, KERNEL_SIZE, KERNEL_SIZE), dtype=jnp.float32) * s, 'dwc_b': jax.random.normal(ks[8], (C // NUM_HEADS,), dtype=jnp.float32) * s, 'scale_param': jnp.zeros((1, 1, C), dtype=jnp.float32)}
    _L1_conv_all = _L1_conv_setup()
    _L1_conv_in = {k: v for k, v in _L1_conv_all.items() if k in ('Wq', 'bq', 'Wkv', 'bkv', 'Wproj', 'bproj', 'dwc_w', 'dwc_b', 'scale_param')}
    del _L1_conv_all

    def _L2_attn_setup():
        import jax, jax.numpy as jnp
        import numpy as np
        T, N, D = (128, 256, 64)

        def _causal_attend(H, e):
            n = H.shape[1]
            m0 = jnp.full((n,), -jnp.inf, dtype=H.dtype)
            s0 = jnp.zeros((n,), dtype=H.dtype)
            num0 = jnp.zeros((n, H.shape[2]), dtype=H.dtype)

            def step(carry, inp):
                m, s, num = carry
                e_t, h_t = inp
                m_new = jnp.maximum(m, e_t)
                alpha = jnp.exp(m - m_new)
                p = jnp.exp(e_t - m_new)
                s_new = s * alpha + p
                num_new = num * alpha[:, None] + p[:, None] * h_t
                c_t = num_new / s_new[:, None]
                return ((m_new, s_new, num_new), c_t)
            _, C = jax.lax.scan(step, (m0, s0, num0), (e, H))
            return C
        key = jax.random.key(seed)
        k1, k2, k3, k4 = jax.random.split(key, 4)
        scale = 1.0 / np.sqrt(D)
        return {'H': jax.random.normal(k1, (T, N, D), dtype=jnp.float32), 'fc_w': jax.random.normal(k2, (D, D), dtype=jnp.float32) * scale, 'fc_b': jax.random.normal(k3, (D,), dtype=jnp.float32) * scale, 'score_w': jax.random.normal(k4, (D,), dtype=jnp.float32) * scale}
    _L2_attn_all = _L2_attn_setup()
    _L2_attn_in = {k: v for k, v in _L2_attn_all.items() if k in ('fc_w', 'fc_b', 'score_w')}
    del _L2_attn_all

    def _L2_ffn_setup():
        import jax, jax.numpy as jnp
        import numpy as np
        D_MODEL = 64
        N_EXPERTS = 16
        HIDDEN = 128
        SCALE = 0.02
        key = jax.random.key(seed)
        ks = jax.random.split(key, 5)
        x = jax.random.normal(ks[0], (4, 2048, D_MODEL), dtype=jnp.float32)
        gate_w = jax.random.normal(ks[1], (D_MODEL, N_EXPERTS), dtype=jnp.float32) * SCALE
        gate_b = jnp.zeros((N_EXPERTS,), dtype=jnp.float32)
        w1 = jax.random.normal(ks[2], (N_EXPERTS, D_MODEL, HIDDEN), dtype=jnp.float32) * SCALE
        w2 = jax.random.normal(ks[3], (N_EXPERTS, D_MODEL, HIDDEN), dtype=jnp.float32) * SCALE
        w3 = jax.random.normal(ks[4], (N_EXPERTS, HIDDEN, D_MODEL), dtype=jnp.float32) * SCALE
        return {'x': x, 'gate_w': gate_w, 'gate_b': gate_b, 'w1': w1, 'w2': w2, 'w3': w3}
    _L2_ffn_all = _L2_ffn_setup()
    _L2_ffn_in = {k: v for k, v in _L2_ffn_all.items() if k in ('gate_w', 'gate_b', 'w1', 'w2', 'w3')}
    del _L2_ffn_all

    def _L3_attn_setup():
        import jax, jax.numpy as jnp
        import numpy as np
        B, N, DIM, H, R = (8, 1024, 64, 8, 32)
        key = jax.random.key(seed)
        k0, k1, k2, k3 = jax.random.split(key, 4)
        x = jax.random.normal(k0, (B, N, DIM), jnp.float32)
        qkv_w = jax.random.normal(k1, (DIM, 2 * H * DIM), jnp.float32) * 0.02
        qkv_b = jnp.zeros((2 * H * DIM,), jnp.float32)
        lunchbox = jax.random.normal(k2, (DIM, R), jnp.float32) * (1.0 / np.sqrt(DIM))
        proj_w = jax.random.normal(k3, (H * DIM, DIM), jnp.float32) * 0.02
        proj_b = jnp.zeros((DIM,), jnp.float32)
        return dict(x=x, qkv_w=qkv_w, qkv_b=qkv_b, lunchbox=lunchbox, proj_w=proj_w, proj_b=proj_b)
    _L3_attn_all = _L3_attn_setup()
    _L3_attn_in = {k: v for k, v in _L3_attn_all.items() if k in ('qkv_w', 'qkv_b', 'lunchbox', 'proj_w', 'proj_b')}
    del _L3_attn_all

    def _L3_ffn_setup():
        import jax, jax.numpy as jnp
        import numpy as np
        D_MODEL = 64
        N_EXPERTS = 16
        HIDDEN = 128
        SCALE = 0.02
        key = jax.random.key(seed)
        ks = jax.random.split(key, 5)
        x = jax.random.normal(ks[0], (4, 2048, D_MODEL), dtype=jnp.float32)
        gate_w = jax.random.normal(ks[1], (D_MODEL, N_EXPERTS), dtype=jnp.float32) * SCALE
        gate_b = jnp.zeros((N_EXPERTS,), dtype=jnp.float32)
        w1 = jax.random.normal(ks[2], (N_EXPERTS, D_MODEL, HIDDEN), dtype=jnp.float32) * SCALE
        w2 = jax.random.normal(ks[3], (N_EXPERTS, D_MODEL, HIDDEN), dtype=jnp.float32) * SCALE
        w3 = jax.random.normal(ks[4], (N_EXPERTS, HIDDEN, D_MODEL), dtype=jnp.float32) * SCALE
        return {'x': x, 'gate_w': gate_w, 'gate_b': gate_b, 'w1': w1, 'w2': w2, 'w3': w3}
    _L3_ffn_all = _L3_ffn_setup()
    _L3_ffn_in = {k: v for k, v in _L3_ffn_all.items() if k in ('gate_w', 'gate_b', 'w1', 'w2', 'w3')}
    del _L3_ffn_all
    return {'x': x, 'L0_conv_W': _L0_conv_in['W'], 'L0_conv_b': _L0_conv_in['b'], 'L1_conv_Wq': _L1_conv_in['Wq'], 'L1_conv_bq': _L1_conv_in['bq'], 'L1_conv_Wkv': _L1_conv_in['Wkv'], 'L1_conv_bkv': _L1_conv_in['bkv'], 'L1_conv_Wproj': _L1_conv_in['Wproj'], 'L1_conv_bproj': _L1_conv_in['bproj'], 'L1_conv_dwc_w': _L1_conv_in['dwc_w'], 'L1_conv_dwc_b': _L1_conv_in['dwc_b'], 'L1_conv_scale_param': _L1_conv_in['scale_param'], 'L2_attn_fc_w': _L2_attn_in['fc_w'], 'L2_attn_fc_b': _L2_attn_in['fc_b'], 'L2_attn_score_w': _L2_attn_in['score_w'], 'L2_ffn_gate_w': _L2_ffn_in['gate_w'], 'L2_ffn_gate_b': _L2_ffn_in['gate_b'], 'L2_ffn_w1': _L2_ffn_in['w1'], 'L2_ffn_w2': _L2_ffn_in['w2'], 'L2_ffn_w3': _L2_ffn_in['w3'], 'L3_attn_qkv_w': _L3_attn_in['qkv_w'], 'L3_attn_qkv_b': _L3_attn_in['qkv_b'], 'L3_attn_lunchbox': _L3_attn_in['lunchbox'], 'L3_attn_proj_w': _L3_attn_in['proj_w'], 'L3_attn_proj_b': _L3_attn_in['proj_b'], 'L3_ffn_gate_w': _L3_ffn_in['gate_w'], 'L3_ffn_gate_b': _L3_ffn_in['gate_b'], 'L3_ffn_w1': _L3_ffn_in['w1'], 'L3_ffn_w2': _L3_ffn_in['w2'], 'L3_ffn_w3': _L3_ffn_in['w3']}

def reference(x, L0_conv_W, L0_conv_b, L1_conv_Wq, L1_conv_bq, L1_conv_Wkv, L1_conv_bkv, L1_conv_Wproj, L1_conv_bproj, L1_conv_dwc_w, L1_conv_dwc_b, L1_conv_scale_param, L2_attn_fc_w, L2_attn_fc_b, L2_attn_score_w, L2_ffn_gate_w, L2_ffn_gate_b, L2_ffn_w1, L2_ffn_w2, L2_ffn_w3, L3_attn_qkv_w, L3_attn_qkv_b, L3_attn_lunchbox, L3_attn_proj_w, L3_attn_proj_b, L3_ffn_gate_w, L3_ffn_gate_b, L3_ffn_w1, L3_ffn_w2, L3_ffn_w3):
    import jax
    import jax.numpy as jnp

    def _L0_conv_ref(x, W, b):
        import jax, jax.numpy as jnp
        import numpy as np
        B, C, H, Wd = (32, 64, 16, 16)
        batch, ch, h, w = x.shape
        jj = (jnp.arange(w, dtype=x.dtype) / (w - 1))[None, :]
        ii = (jnp.arange(h, dtype=x.dtype) / (h - 1))[:, None]
        pos = jnp.stack([jnp.broadcast_to(jj, (h, w)), jnp.broadcast_to(ii, (h, w)), jnp.broadcast_to(1.0 - jj, (h, w)), jnp.broadcast_to(1.0 - ii, (h, w))], axis=-1)
        pe = pos @ W.T + b
        pe = jnp.broadcast_to(pe[None], (batch, h, w, ch)).reshape(batch, ch, h, w)
        return x + pe

    def _L1_conv_ref(x, Wq, bq, Wkv, bkv, Wproj, bproj, dwc_w, dwc_b, scale_param):
        import jax, jax.numpy as jnp
        import numpy as np
        from jax import lax
        NUM_HEADS = 8
        FOCUSING_FACTOR = 3.0
        KERNEL_SIZE = 5
        B, C, H, W = x.shape
        nh = NUM_HEADS
        hd = C // nh
        N = H * W
        num = int(round(N ** 0.5))
        xt = x.reshape(B, C, N).transpose(0, 2, 1)
        q = xt @ Wq.T + bq
        kv = xt @ Wkv.T + bkv
        k, v = (kv[..., :C], kv[..., C:])
        scale = jax.nn.softplus(scale_param)
        q = (jax.nn.relu(q) + 1e-06) / scale
        k = (jax.nn.relu(k) + 1e-06) / scale
        q_norm = jnp.linalg.norm(q, axis=-1, keepdims=True)
        k_norm = jnp.linalg.norm(k, axis=-1, keepdims=True)
        q = q ** FOCUSING_FACTOR
        k = k ** FOCUSING_FACTOR
        q = q / jnp.linalg.norm(q, axis=-1, keepdims=True) * q_norm
        k = k / jnp.linalg.norm(k, axis=-1, keepdims=True) * k_norm

        def split_heads(t):
            return t.reshape(B, N, nh, hd).transpose(0, 2, 1, 3).reshape(B * nh, N, hd)
        q, k, v = (split_heads(q), split_heads(k), split_heads(v))
        z = 1.0 / (jnp.einsum('bic,bc->bi', q, k.sum(axis=1)) + 1e-06)
        kv_state = jnp.einsum('bjc,bjd->bcd', k, v)
        out = jnp.einsum('bic,bcd->bid', q, kv_state) * z[..., None]
        fm = v.transpose(0, 2, 1).reshape(B * nh, hd, num, num)
        fm = lax.conv_general_dilated(fm, dwc_w, window_strides=(1, 1), padding=[(KERNEL_SIZE // 2, KERNEL_SIZE // 2)] * 2, dimension_numbers=('NCHW', 'OIHW', 'NCHW'), feature_group_count=hd) + dwc_b[None, :, None, None]
        fm = fm.reshape(B * nh, hd, N).transpose(0, 2, 1)
        out = out + fm
        out = out.reshape(B, nh, N, hd).transpose(0, 2, 1, 3).reshape(B, N, C)
        out = out @ Wproj.T + bproj
        return out.transpose(0, 2, 1).reshape(B, C, H, W)

    def _L2_attn_ref(H, fc_w, fc_b, score_w):
        import jax, jax.numpy as jnp
        import numpy as np
        T, N, D = (128, 256, 64)

        def _causal_attend(H, e):
            n = H.shape[1]
            m0 = jnp.full((n,), -jnp.inf, dtype=H.dtype)
            s0 = jnp.zeros((n,), dtype=H.dtype)
            num0 = jnp.zeros((n, H.shape[2]), dtype=H.dtype)

            def step(carry, inp):
                m, s, num = carry
                e_t, h_t = inp
                m_new = jnp.maximum(m, e_t)
                alpha = jnp.exp(m - m_new)
                p = jnp.exp(e_t - m_new)
                s_new = s * alpha + p
                num_new = num * alpha[:, None] + p[:, None] * h_t
                c_t = num_new / s_new[:, None]
                return ((m_new, s_new, num_new), c_t)
            _, C = jax.lax.scan(step, (m0, s0, num0), (e, H))
            return C
        Q = jnp.tanh(jnp.einsum('tnd,ed->tne', H, fc_w) + fc_b)
        e = jnp.einsum('tne,e->tn', Q, score_w)
        return _causal_attend(H, e)

    def _L2_ffn_ref(x, gate_w, gate_b, w1, w2, w3):
        import jax, jax.numpy as jnp
        import numpy as np
        D_MODEL = 64
        N_EXPERTS = 16
        HIDDEN = 128
        SCALE = 0.02
        n_experts = w1.shape[0]
        logits = jnp.einsum('bsd,de->bse', x, gate_w) + gate_b
        probs = jax.nn.softmax(logits, axis=-1)
        top_probs, top_idx = jax.lax.top_k(probs, 2)
        top_probs = top_probs / jnp.sum(top_probs, axis=-1, keepdims=True)
        dispatch = jnp.sum(jax.nn.one_hot(top_idx, n_experts, dtype=x.dtype) * top_probs[..., None], axis=-2)
        h1 = jnp.einsum('bsd,edh->bseh', x, w1)
        h2 = jnp.einsum('bsd,edh->bseh', x, w2)
        hidden = jax.nn.silu(h1) * h2
        expert_out = jnp.einsum('bseh,eho->bseo', hidden, w3)
        return jnp.einsum('bseo,bse->bso', expert_out, dispatch)

    def _L3_attn_ref(x, qkv_w, qkv_b, lunchbox, proj_w, proj_b):
        import jax, jax.numpy as jnp
        import numpy as np
        B, N, DIM, H, R = (8, 1024, 64, 8, 32)
        Bsz, Nseq, C = x.shape
        D, Rr = lunchbox.shape
        Hh = qkv_w.shape[1] // (2 * D)
        scale = max(D, Rr) ** (-0.5)
        h = x @ qkv_w + qkv_b
        h = jnp.transpose(h, (0, 2, 1)).reshape(Bsz, 2, Hh, D, Nseq)
        q, v = (h[:, 0], h[:, 1])
        attn = jnp.einsum('bhdn,dr->bhrd', q, lunchbox) * scale
        res = jnp.einsum('bhrd,bhdn->bhnd', attn, v)
        out = res.reshape(Bsz, Nseq, Hh * D) @ proj_w + proj_b
        return out

    def _L3_ffn_ref(x, gate_w, gate_b, w1, w2, w3):
        import jax, jax.numpy as jnp
        import numpy as np
        D_MODEL = 64
        N_EXPERTS = 16
        HIDDEN = 128
        SCALE = 0.02
        n_experts = w1.shape[0]
        logits = jnp.einsum('bsd,de->bse', x, gate_w) + gate_b
        probs = jax.nn.softmax(logits, axis=-1)
        top_probs, top_idx = jax.lax.top_k(probs, 2)
        top_probs = top_probs / jnp.sum(top_probs, axis=-1, keepdims=True)
        dispatch = jnp.sum(jax.nn.one_hot(top_idx, n_experts, dtype=x.dtype) * top_probs[..., None], axis=-2)
        h1 = jnp.einsum('bsd,edh->bseh', x, w1)
        h2 = jnp.einsum('bsd,edh->bseh', x, w2)
        hidden = jax.nn.silu(h1) * h2
        expert_out = jnp.einsum('bseh,eho->bseo', hidden, w3)
        return jnp.einsum('bseo,bse->bso', expert_out, dispatch)

    def _gn(v, G=32, eps=1e-05):
        B_, C_, H_, W_ = v.shape
        g = v.reshape(B_, G, C_ // G, H_, W_)
        m = jnp.mean(g, axis=(2, 3, 4), keepdims=True)
        s = jnp.var(g, axis=(2, 3, 4), keepdims=True)
        return ((g - m) / jnp.sqrt(s + eps)).reshape(v.shape)

    def _ln_c(v, eps=1e-06):
        m = jnp.mean(v, axis=1, keepdims=True)
        s = jnp.var(v, axis=1, keepdims=True)
        return (v - m) / jnp.sqrt(s + eps)

    def _ln_t(v, eps=1e-05):
        m = jnp.mean(v, axis=-1, keepdims=True)
        s = jnp.var(v, axis=-1, keepdims=True)
        return (v - m) / jnp.sqrt(s + eps)

    def _to_tokens(v):
        B_, C_, H_, W_ = v.shape
        return v.reshape(B_, C_, H_ * W_).transpose(0, 2, 1)

    def _from_tokens(t, like):
        B_, C_, H_, W_ = like.shape
        return t.transpose(0, 2, 1).reshape(B_, C_, H_, W_)
    x = _L0_conv_ref(x, L0_conv_W, L0_conv_b)
    x = x + _L1_conv_ref(_gn(x), L1_conv_Wq, L1_conv_bq, L1_conv_Wkv, L1_conv_bkv, L1_conv_Wproj, L1_conv_bproj, L1_conv_dwc_w, L1_conv_dwc_b, L1_conv_scale_param)
    t = _to_tokens(x)
    t = t + _L2_attn_ref(_ln_t(t), L2_attn_fc_w, L2_attn_fc_b, L2_attn_score_w)
    t = t + _L2_ffn_ref(_ln_t(t), L2_ffn_gate_w, L2_ffn_gate_b, L2_ffn_w1, L2_ffn_w2, L2_ffn_w3)
    t = t + _L3_attn_ref(_ln_t(t), L3_attn_qkv_w, L3_attn_qkv_b, L3_attn_lunchbox, L3_attn_proj_w, L3_attn_proj_b)
    t = t + _L3_ffn_ref(_ln_t(t), L3_ffn_gate_w, L3_ffn_gate_b, L3_ffn_w1, L3_ffn_w2, L3_ffn_w3)
    x = _from_tokens(t, x)
    return x

_drawn_inputs = setup_inputs


def setup_inputs(seed=0):
    import zlib

    import numpy as np

    out = dict(_drawn_inputs(seed))
    spreads = {'L1_conv_scale_param': (0.0, 0.8),
     'L2_ffn_gate_b': (0.0, 0.8),
     'L3_attn_qkv_b': (0.0, 0.1),
     'L3_attn_proj_b': (0.0, 0.1),
     'L3_ffn_gate_b': (0.0, 0.8)}
    factors = {'L1_conv_Wq': 8.0,
     'L1_conv_bq': 8.0,
     'L1_conv_Wkv': 7.624,
     'L1_conv_bkv': 8.0,
     'L1_conv_Wproj': 5.241,
     'L1_conv_dwc_w': 8.0,
     'L1_conv_dwc_b': 8.0,
     'L2_attn_fc_b': 6.207,
     'L2_ffn_gate_w': 8.0,
     'L2_ffn_w1': 8.0,
     'L2_ffn_w2': 8.0,
     'L2_ffn_w3': 8.0,
     'L3_ffn_gate_w': 8.0,
     'L3_ffn_w1': 8.0,
     'L3_ffn_w2': 8.0,
     'L3_ffn_w3': 8.0}
    for name, (base, spread) in spreads.items():
        noise = np.random.default_rng([zlib.crc32(name.encode()), seed]).standard_normal(out[name].shape)
        drawn = base * np.exp(spread * noise) if base else spread * noise
        out[name] = jnp.asarray(drawn.astype(out[name].dtype))
    for name, factor in factors.items():
        out[name] = (out[name] * factor).astype(out[name].dtype)
    return out
```

```python
from contextlib import ExitStack

import numpy as np

import concourse.bass as bass
from concourse import mybir

F32 = mybir.dt.float32
F32R = mybir.dt.float32r
ALU = mybir.AluOpType
ACT = mybir.ActivationFunctionType
AX = mybir.AxisListType

B, C, HH, WW = 32, 64, 16, 16
N = HH * WW
P = 128
Q = B // 2
NT = Q * 2 * 2
NH, HD = 8, C // 8
KS = 5
E, HID = 16, 128
H3 = 8
G = 4
QG = Q // G
BANK = 512
BIG = 1e38


def counter(eng, sem):
    n = [0]

    def then(ins):
        n[0] += 1
        ins.then_inc(sem, 1)
        eng.wait_ge(sem, n[0])
    return then


def bcast(ap, shape):
    return ap.to_broadcast(shape)


def stage_norm(nc, sem, A, K, Xc, xn, wqkv, wproj, T):
    with ExitStack() as st:
        def sb(name, shape, dt=F32):
            return st.enter_context(nc.sbuf_tensor(name, shape, dt))
        ps = st.enter_context(nc.psum_tensor("n_ps", [P, 8, BANK], F32))
        posw = sb("n_posw", [5, C])
        w1 = sb("n_w1", [P, 2, C])
        w2 = sb("n_w2", [P, 2, C])
        taps = sb("n_taps", [KS * KS, HD])
        selx = sb("n_selx", [KS * KS, WW, KS * WW])
        sely = sb("n_sely", [KS * WW, 2, 31 * 8])
        pos = sb("n_pos", [5, 4, P])
        pairs = sb("n_pairs", [P, P])
        rowk = sb("n_rowk", [KS * WW, HD, 2, 8])
        stats = sb("n_stats", [P, Q, 6])
        mv = sb("n_mv", [P, Q, 2])
        gm = sb("n_gm", [P, Q, 2])
        dm = sb("n_dm", [P, Q])
        vg = sb("n_vg", [P, Q])
        sd = sb("n_sd", [P, Q])
        rs = sb("n_rs", [P, Q])
        nmr = sb("n_nmr", [P, Q])
        small, big_w, x_in = sem("n_small"), sem("n_bigw"), [sem(f"n_x{g}") for g in range(G)]
        pe_ready, mv_ready, gm_ready, var_ready, sd_ready = (
            sem("n_pe"), sem("n_mv"), sem("n_gm"), sem("n_var"), sem("n_sd"))
        wt_ready, rowk_ps, rowk_sb, band_ps, band_sb = (
            sem("n_wt"), sem("n_rkp"), sem("n_rks"), sem("n_bp"), sem("n_bs"))
        own_v, zeroed, own_s = sem("n_ownv"), sem("n_zero"), sem("n_owns")
        x_v = A["x"].rearrange("(q b) c y w -> (b c) q (y w)", b=2)

        with nc.Block() as block:
            @block.sync
            def _(sp):
                for g in range(G):
                    sp.dma_start(Xc[:, g * QG:(g + 1) * QG, :], x_v[:, g * QG:(g + 1) * QG, :]).then_inc(x_in[g], 16)

            @block.gpsimd
            def _(pool):
                pool.memset(wqkv[:], 0.0).then_inc(zeroed, 1)
                pool.memset(wproj[:], 0.0).then_inc(zeroed, 1)

            @block.scalar
            def _(act):
                act.dma_start(pos[:], A["k_pos"]).then_inc(small, 16)
                act.dma_start(posw[0:4, :], A["L0_conv_W"].rearrange("c k -> k c"), allow_slow_non_contiguous=True).then_inc(small, 16)
                act.dma_start(posw[4:5, :], A["L0_conv_b"].rearrange("(a c) -> a c", a=1)).then_inc(small, 16)
                act.dma_start(pairs[:], A["k_pairs"]).then_inc(big_w, 16)
                act.dma_start(K["ident"][:], A["k_ident"]).then_inc(big_w, 16)
                for half in range(2):
                    act.dma_start(w1[0:C, half, :], A["L1_conv_Wq"]).then_inc(big_w, 16)
                    act.dma_start(w1[C:P, half, :], A["L1_conv_Wkv"][0:C, :]).then_inc(big_w, 16)
                    act.dma_start(w2[0:C, half, :], A["L1_conv_Wkv"][C:2 * C, :]).then_inc(big_w, 16)
                    act.dma_start(w2[C:P, half, :], A["L1_conv_Wproj"]).then_inc(big_w, 16)
                act.dma_start(taps[:], A["L1_conv_dwc_w"].rearrange("d a y x -> (a y x) d"),
                              allow_slow_non_contiguous=True).then_inc(big_w, 16)
                act.dma_start(selx[:], A["k_selx"]).then_inc(big_w, 16)
                act.dma_start(sely[:], A["k_sely"]).then_inc(big_w, 16)
                act.wait_ge(var_ready, 1)
                act.activation(sd[:], vg[:], ACT.Sqrt).then_inc(sd_ready, 1)
                for k in range(8):
                    act.wait_ge(band_ps, k + 1)
                    pj, i4 = k // 4, (k % 4) * 4
                    for u in range(4):
                        ins = act.copy(T[:, pj, :, (i4 + u) * 8:(i4 + u) * 8 + 8],
                                       ps[:, 4 + k % 2, u * P:(u + 1) * P].rearrange("p (a b) -> p a b", b=8))
                    ins.then_inc(band_sb, 1)

            @block.tensor
            def _(pe):
                pe.wait_ge(small, 48)
                for j in range(4):
                    ins = pe.matmul(ps[:, 0, j * C:(j + 1) * C], pos[:, j, :], posw[:], start=True, stop=True)
                ins.then_inc(pe_ready, 1)
                pe.wait_ge(big_w, 16 * 13)
                pe.transpose(ps[:, 1, 0:P], w1[:].rearrange("p a c -> p (a c)"), K["ident"][:])
                pe.transpose(ps[:, 1, P:2 * P], w2[:].rearrange("p a c -> p (a c)"), K["ident"][:]).then_inc(wt_ready, 1)
                for ix in range(WW):
                    ins = pe.matmul(ps[0:KS * WW, 2, ix * 8:ix * 8 + 8], selx[:, ix, :], taps[:], start=True, stop=True)
                ins.then_inc(rowk_ps, 1)
                pe.wait_ge(mv_ready, 1)
                pe.matmul(ps[:, 3, 0:2 * Q], pairs[:], mv[:].rearrange("p q k -> p (q k)"),
                          start=True, stop=True).then_inc(gm_ready, 1)
                pe.wait_ge(rowk_sb, 1)
                for k in range(8):
                    pj, i4 = k // 4, (k % 4) * 4
                    if k >= 2:
                        pe.wait_ge(band_sb, k - 1)
                    for u in range(4):
                        s0 = (HH - 1 - (i4 + u)) * 8
                        ins = pe.matmul(ps[:, 4 + k % 2, u * P:(u + 1) * P], sely[:, pj, s0:s0 + P],
                                        rowk[:].rearrange("k d a b -> k (d a b)"), start=True, stop=True)
                    ins.then_inc(band_ps, 1)

            @block.vector
            def _(dve):
                then = counter(dve, own_v)
                dve.wait_ge(pe_ready, 1)
                for g in range(G):
                    dve.wait_ge(x_in[g], 16)
                    xg = Xc[:, g * QG:(g + 1) * QG, :]
                    then(dve.tensor_tensor(xg, xg, ps[:, 0, 0:N].unsqueeze(1).to_broadcast([P, QG, N]), ALU.add))
                    for q in range(g * QG, (g + 1) * QG):
                        ins = dve.bn_stats(stats[:, q, :], Xc[:, q, :])
                then(ins)
                for q in range(Q):
                    ins = dve.bn_aggr(mv[:, q, :], stats[:, q, :])
                ins.then_inc(mv_ready, 1)
                dve.wait_ge(wt_ready, 1)
                dve.wait_ge(zeroed, 2)
                for b2 in range(2):
                    rows = slice(b2 * C, b2 * C + C)
                    for k in range(3):
                        dve.tensor_copy(wqkv[rows, k, b2, :], ps[rows, 1, k * C:(k + 1) * C])
                    dve.tensor_copy(wproj[rows, b2, :], ps[rows, 1, 3 * C:4 * C])
                dve.wait_ge(rowk_ps, 1)
                dve.tensor_copy(rowk[:], ps[0:KS * WW, 2, 0:P].rearrange("k (b a d) -> k d a b", a=2, d=8)
                                ).then_inc(rowk_sb, 1)
                dve.wait_ge(gm_ready, 1)
                then(dve.tensor_copy(gm[:].rearrange("p q k -> p (q k)"), ps[:, 3, 0:2 * Q]))
                then(dve.tensor_tensor(dm[:], mv[:, :, 0], gm[:, :, 0], ALU.subtract))
                then(dve.tensor_tensor(dm[:], dm[:], dm[:], ALU.mult))
                then(dve.tensor_tensor(vg[:], dm[:], gm[:, :, 1], ALU.add))
                dve.tensor_scalar(vg[:], vg[:], 1e-5, None, ALU.add).then_inc(var_ready, 1)
                dve.wait_ge(sd_ready, 1)
                then(dve.reciprocal(rs[:], sd[:]))
                then(dve.scalar_tensor_tensor(out=nmr[:], in0=gm[:, :, 0], scalar=-1.0, in1=rs[:],
                                              op0=ALU.mult, op1=ALU.mult))
                for q in range(Q):
                    dve.tensor_scalar(xn[:, q, :], Xc[:, q, :], rs[:, q:q + 1], nmr[:, q:q + 1], ALU.mult, ALU.add)


def stage_qkv(nc, sem, A, xn, wqkv, QKf, V):
    with ExitStack() as st:
        def sb(name, shape, dt=F32):
            return st.enter_context(nc.sbuf_tensor(name, shape, dt))
        ps = st.enter_context(nc.psum_tensor("q_ps", [P, 4, BANK], F32))
        QK = sb("q_qk", [P, Q, 2, 4 * C])
        S = sb("q_sq", [P, Q, 2, 4 * C])
        bias = sb("q_bias", [P, 3, C])
        bias2 = sb("q_bias2", [P, 3, 2, C])
        sp_ = sb("q_sp", [P, 8, C])
        n2 = sb("q_n2", [P, Q * 2 * 4])
        n6 = sb("q_n6", [P, Q * 2 * 4])
        loaded, own_v = sem("q_loaded"), sem("q_own")
        exp_in, exp_out, ln_in, ln_out = sem("q_ei"), sem("q_eo"), sem("q_li"), sem("q_lo")
        mm, evac = sem("q_mm"), sem("q_evac")
        scaled, squared, cubed, sixth, norms, roots = (
            sem("q_scaled"), sem("q_squared"), sem("q_cubed"), sem("q_sixth"), sem("q_norms"), sem("q_roots"))

        def part(t, g):
            return t[:, g * QG:(g + 1) * QG].rearrange("p q a c -> p (q a c)")

        with nc.Block() as block:
            @block.sync
            def _(sp):
                for k, src in enumerate((A["L1_conv_bq"][0:C], A["L1_conv_bkv"][0:C], A["L1_conv_bkv"][C:2 * C])):
                    sp.dma_start(bias[:, k, :], src.rearrange("(a c) -> a c", a=1).to_broadcast([P, C])).then_inc(loaded, 16)
                sp.dma_start(sp_[:, 0, :], A["L1_conv_scale_param"].rearrange("a b c -> (a b) c").to_broadcast([P, C])
                             ).then_inc(loaded, 16)

            @block.tensor
            def _(pe):
                for i in range(2 * Q):
                    if i >= 4:
                        pe.wait_ge(evac, i - 3)
                    pe.matmul(ps[:, i % 4, 0:6 * C], xn[:, i // 2, i % 2:N:2],
                              wqkv[:].rearrange("p k b c -> p (k b c)"), start=True, stop=True).then_inc(mm, 1)

            @block.scalar
            def _(act):
                act.wait_ge(exp_in, 1)
                act.activation(sp_[:, 2, :], sp_[:, 1, :], ACT.Exp).then_inc(exp_out, 1)
                act.wait_ge(ln_in, 1)
                act.activation(sp_[:, 5, :], sp_[:, 3, :], ACT.Ln).then_inc(ln_out, 1)
                for g in range(G):
                    act.wait_ge(scaled, g + 1)
                    act.activation(part(S, g), part(QK, g), ACT.Square).then_inc(squared, 1)
                for g in range(G):
                    act.wait_ge(cubed, g + 1)
                    act.activation(part(S, g), part(QKf, g), ACT.Square).then_inc(sixth, 1)
                act.wait_ge(norms, 1)
                act.activation(n2[:], n2[:], ACT.Sqrt)
                act.activation(n6[:], n6[:], ACT.Sqrt).then_inc(roots, 1)

            @block.vector
            def _(dve):
                then = counter(dve, own_v)
                dve.wait_ge(loaded, 64)
                then(dve.tensor_copy(bias2[:], bias[:].unsqueeze(2).to_broadcast([P, 3, 2, C])))
                then(dve.tensor_scalar(sp_[:, 4, :], sp_[:, 0, :], -1.0, None, ALU.mult))
                dve.tensor_tensor(sp_[:, 1, :], sp_[:, 0, :], sp_[:, 4, :], ALU.min).then_inc(exp_in, 1)
                dve.wait_ge(exp_out, 1)
                dve.tensor_scalar(sp_[:, 3, :], sp_[:, 2, :], 1.0, None, ALU.add).then_inc(ln_in, 1)
                dve.wait_ge(ln_in, 1)
                then(dve.tensor_scalar(sp_[:, 4, :], sp_[:, 3, :], -1.0, None, ALU.add))
                then(dve.tensor_scalar(sp_[:, 6, :], sp_[:, 4, :], 0.0, None, ALU.is_equal))
                dve.wait_ge(ln_out, 1)
                then(dve.tensor_tensor(sp_[:, 5, :], sp_[:, 5, :], sp_[:, 6, :], ALU.add))
                then(dve.tensor_tensor(sp_[:, 4, :], sp_[:, 4, :], sp_[:, 6, :], ALU.add))
                then(dve.reciprocal(sp_[:, 7, :], sp_[:, 4, :]))
                then(dve.tensor_tensor(sp_[:, 5, :], sp_[:, 5, :], sp_[:, 2, :], ALU.mult))
                then(dve.tensor_tensor(sp_[:, 5, :], sp_[:, 5, :], sp_[:, 7, :], ALU.mult))
                then(dve.scalar_tensor_tensor(out=sp_[:, 6, :], in0=sp_[:, 0, :], scalar=0.0, in1=sp_[:, 5, :],
                                              op0=ALU.max, op1=ALU.add))
                then(dve.reciprocal(sp_[:, 7, :], sp_[:, 6, :]))
                dve.memset(V[:, :, :, 2 * C:2 * C + 4], 1.0)
                bqk = bias2[:, 0:2].rearrange("p k b c -> p (k b c)")
                bv = bias2[:, 2].rearrange("p b c -> p (b c)")
                for g in range(G):
                    for i in range(g * 2 * QG, (g + 1) * 2 * QG):
                        dve.wait_ge(mm, i + 1)
                        dve.tensor_tensor(QK[:, i // 2, i % 2, :], ps[:, i % 4, 0:4 * C], bqk, ALU.add)
                        ins = dve.tensor_tensor(V[:, i // 2, i % 2, 0:2 * C], ps[:, i % 4, 4 * C:6 * C], bv, ALU.add)
                        ins.then_inc(evac, 1)
                    dve.wait_ge(evac, (g + 1) * 2 * QG)
                    then(dve.tensor_scalar(part(QK, g), part(QK, g), 0.0, 1e-6, ALU.max, ALU.add))
                    v = part(QK, g).rearrange("p (r c) -> p r c", c=C)
                    dve.tensor_tensor(v, v, sp_[:, 7:8, :].to_broadcast([P, QG * 8, C]), ALU.mult).then_inc(scaled, 1)
                for g in range(G):
                    r = slice(g * QG * 8, (g + 1) * QG * 8)
                    dve.wait_ge(squared, g + 1)
                    dve.tensor_reduce(n2[:, r], part(S, g).rearrange("p (r c) -> p r c", c=C), AX.X, ALU.add)
                    dve.tensor_tensor(part(QKf, g), part(S, g), part(QK, g), ALU.mult).then_inc(cubed, 1)
                for g in range(G):
                    r = slice(g * QG * 8, (g + 1) * QG * 8)
                    dve.wait_ge(sixth, g + 1)
                    ins = dve.tensor_reduce(n6[:, r], part(S, g).rearrange("p (r c) -> p r c", c=C), AX.X, ALU.add)
                ins.then_inc(norms, 1)
                dve.wait_ge(roots, 1)
                then(dve.reciprocal(n6[:], n6[:]))
                then(dve.tensor_tensor(n2[:], n2[:], n6[:], ALU.mult))
                for g in range(G):
                    r = slice(g * QG * 8, (g + 1) * QG * 8)
                    v = part(QKf, g).rearrange("p (r c) -> p r c", c=C)
                    dve.tensor_tensor(v, v, n2[:, r].unsqueeze(2).to_broadcast([P, QG * 8, C]), ALU.mult)


def stage_attend(nc, sem, A, K, Xc, QKf, V, T, wproj, X):
    with ExitStack() as st:
        def sb(name, shape, dt=F32):
            return st.enter_context(nc.sbuf_tensor(name, shape, dt))
        ps = st.enter_context(nc.psum_tensor("a_ps", [P, 8, BANK], F32))
        FM = sb("a_fm", [P, Q, 2, 2 * C])
        QT = sb("a_qt", [P, Q, 2, P])
        mask = sb("a_mask", [P, P])
        BD = sb("a_bd", [P, Q, 2, P])
        rz = sb("a_rz", [P, 2, N])
        y = sb("a_y", [P, 2, N])
        oT = sb("a_ot", [P, 2, N])
        dwb = sb("a_dwb", [P, 1])
        bp = sb("a_bp", [P, 2, C])
        loaded, own_v = sem("a_loaded"), sem("a_own")
        conv_mm, conv_ev, qt_mm, qt_ev, kv_mm, kv_ev = (
            sem("a_cm"), sem("a_ce"), sem("a_qm"), sem("a_qe"), sem("a_km"), sem("a_ke"))
        nd_mm, fm_mm, o_ready, pr_mm, pr_ev = sem("a_nm"), sem("a_fmm"), sem("a_or"), sem("a_pm"), sem("a_pe")

        with nc.Block() as block:
            @block.sync
            def _(sp):
                sp.dma_start(mask[:], A["k_mask"]).then_inc(loaded, 16)
                db = A["L1_conv_dwc_b"].rearrange("(d a) -> d a", a=1)
                for r in range(2 * NH):
                    sp.dma_start(dwb[r * HD:(r + 1) * HD, :], db).then_inc(loaded, 16)
                for b2 in range(2):
                    sp.dma_start(bp[:, b2, :], A["L1_conv_bproj"].rearrange("(a c) -> a c", a=1).to_broadcast([P, C])
                                 ).then_inc(loaded, 16)

            @block.tensor
            def _(pe):
                def kv(q):
                    if q >= 2:
                        pe.wait_ge(kv_ev, q - 1)
                    for par in range(2):
                        ins = pe.matmul(ps[:, 4 + q % 2, 0:2 * C + 1], QKf[:, q, par, 2 * C:4 * C],
                                        V[:, q, par, 0:2 * C + 1], start=(par == 0), stop=(par == 1))
                    ins.then_inc(kv_mm, 1)

                def qt(k):
                    if k >= 2:
                        pe.wait_ge(qt_ev, k - 1)
                    for u in range(4):
                        ins = pe.transpose(ps[:, 2 + k % 2, u * P:(u + 1) * P], QKf[:, 2 * k + u // 2, u % 2, 0:2 * C],
                                           K["ident"][:])
                    ins.then_inc(qt_mm, 1)

                def conv(k):
                    d, pi = k // 2, k % 2
                    if k >= 2:
                        pe.wait_ge(conv_ev, k - 1)
                    for pj in range(2):
                        ins = pe.matmul(ps[:, k % 2, 0:B * NH], T[:, pj, 2 * d + pi, :],
                                        V[:, :, pj, d:2 * C:HD], start=(pj == 0), stop=(pj == 1))
                    ins.then_inc(conv_mm, 1)

                for q in range(Q):
                    kv(q)
                    conv(q)
                    if q % 2 == 1:
                        qt(q // 2)

                def numden(q):
                    if q == 0:
                        pe.wait_ge(conv_ev, 2 * HD)
                        pe.wait_ge(kv_ev, Q)
                        pe.wait_ge(qt_ev, Q // 2)
                    if q >= 2:
                        pe.wait_ge(o_ready, q - 1)
                    for k in range(2):
                        ins = pe.matmul(ps[:, q % 2, k * N:(k + 1) * N], BD[:, q, k, :],
                                        QT[:, q].rearrange("p a n -> p (a n)"), start=True, stop=True)
                    ins.then_inc(nd_mm, 1)
                    for par in range(2):
                        ins = pe.transpose(ps[:, 2 + q % 2, par * P:(par + 1) * P], FM[:, q, par, :], K["ident"][:])
                    ins.then_inc(fm_mm, 1)

                def project(q):
                    pe.wait_ge(o_ready, q + 1)
                    if q >= 2:
                        pe.wait_ge(pr_ev, q - 1)
                    for par in range(2):
                        o = ps[:, 6 + q % 2, par * P:(par + 1) * P]
                        pe.matmul(o, oT[:, q % 2, par * P:(par + 1) * P], wproj[:].rearrange("p b c -> p (b c)"),
                                  start=True, stop=False)
                        ins = pe.matmul(o, Xc[:, q, par:N:2], K["ident"][:], start=False, stop=True)
                    ins.then_inc(pr_mm, 1)

                numden(0)
                for q in range(Q):
                    if q + 1 < Q:
                        numden(q + 1)
                    project(q)

            @block.scalar
            def _(act):
                for q in range(Q):
                    d, pi = q // 2, q % 2
                    act.wait_ge(conv_mm, q + 1)
                    act.copy(FM[:, :, pi, d:2 * C:HD], ps[:, q % 2, 0:B * NH].rearrange("p (q h) -> p q h", q=Q)
                             ).then_inc(conv_ev, 1)
                    if q % 2 == 1:
                        k = q // 2
                        act.wait_ge(qt_mm, k + 1)
                        act.copy(QT[:, 2 * k:2 * k + 2].rearrange("p a b n -> p (a b n)"), ps[:, 2 + k % 2, :]
                                 ).then_inc(qt_ev, 1)

            @block.vector
            def _(dve):
                then = counter(dve, own_v)
                dve.wait_ge(loaded, 16 * (3 + 2 * NH))
                for q in range(Q):
                    dve.wait_ge(kv_mm, q + 1)
                    dve.tensor_tensor(BD[:, q, 0, :], ps[:, 4 + q % 2, 0:P], mask[:], ALU.mult)
                    dve.tensor_tensor(BD[:, q, 1, :], mask[:], ps[:, 4 + q % 2, P:P + 1].to_broadcast([P, P]), ALU.mult
                                      ).then_inc(kv_ev, 1)
                for q in range(Q):
                    dve.wait_ge(nd_mm, q + 1)
                    num, den = ps[:, q % 2, 0:N], ps[:, q % 2, N:2 * N]
                    then(dve.tensor_scalar(rz[:, q % 2, :], den, 1e-6, None, ALU.add))
                    then(dve.reciprocal(rz[:, q % 2, :], rz[:, q % 2, :]))
                    then(dve.tensor_tensor(y[:, q % 2, :], num, rz[:, q % 2, :], ALU.mult))
                    dve.wait_ge(fm_mm, q + 1)
                    if q >= 2:
                        dve.wait_ge(pr_mm, q - 1)
                    dve.scalar_tensor_tensor(out=oT[:, q % 2, :], in0=ps[:, 2 + q % 2, 0:N], scalar=dwb[:],
                                             in1=y[:, q % 2, :], op0=ALU.add, op1=ALU.add).then_inc(o_ready, 1)
                    if q >= 1:
                        r = q - 1
                        dve.wait_ge(pr_mm, r + 1)
                        dve.tensor_tensor(X[:, r], ps[:, 6 + r % 2, 0:2 * P].rearrange("p (a n) -> p a n", a=2),
                                          bp[:].rearrange("p b c -> p (b c)").unsqueeze(1).to_broadcast([P, 2, P]),
                                          ALU.add).then_inc(pr_ev, 1)
                r = Q - 1
                dve.wait_ge(pr_mm, r + 1)
                dve.tensor_tensor(X[:, r], ps[:, 6 + r % 2, 0:2 * P].rearrange("p (a n) -> p a n", a=2),
                                  bp[:].rearrange("p b c -> p (b c)").unsqueeze(1).to_broadcast([P, 2, P]),
                                  ALU.add).then_inc(pr_ev, 1)


class LayerNorm:

    def __init__(self, nc, sem, st, tag, X, out, done):
        self.X, self.out, self.done = X, out, done
        self.xm = st.enter_context(nc.sbuf_tensor(tag + "xm", [P, Q, 2, 2 * C], F32))
        self.sq = st.enter_context(nc.sbuf_tensor(tag + "sq", [P, Q, 2, 2 * C], F32))
        self.s1 = st.enter_context(nc.sbuf_tensor(tag + "s1", [P, NT], F32))
        self.r = st.enter_context(nc.sbuf_tensor(tag + "r", [P, NT], F32))
        self.centered, self.squared, self.var, self.sd = (sem(tag + n) for n in ("cen", "sqd", "var", "sd"))

    def flat(self, t, g):
        return t[:, g * QG:(g + 1) * QG].rearrange("p q a c -> p (q a c)")

    def rows(self, t, g):
        return self.flat(t, g).rearrange("p (r c) -> p r c", c=C)

    def scalar(self, act):
        for g in range(G):
            act.wait_ge(self.centered, g + 1)
            act.activation(self.flat(self.sq, g), self.flat(self.xm, g), ACT.Square).then_inc(self.squared, 1)
        act.wait_ge(self.var, 1)
        act.activation(self.s1[:], self.s1[:], ACT.Sqrt).then_inc(self.sd, 1)

    def vector(self, dve, then):
        k = NT // G
        for g in range(G):
            s = self.s1[:, g * k:(g + 1) * k]
            then(dve.tensor_reduce(s, self.rows(self.X, g), AX.X, ALU.add))
            then(dve.tensor_scalar(s, s, -1.0 / C, None, ALU.mult))
            dve.tensor_tensor(self.rows(self.xm, g), self.rows(self.X, g), s.unsqueeze(2).to_broadcast([P, k, C]),
                              ALU.add).then_inc(self.centered, 1)
        for g in range(G):
            dve.wait_ge(self.squared, g + 1)
            ins = dve.tensor_reduce(self.s1[:, g * k:(g + 1) * k], self.rows(self.sq, g), AX.X, ALU.add)
        then(ins)
        dve.tensor_scalar(self.s1[:], self.s1[:], 1.0 / C, 1e-5, ALU.mult, ALU.add).then_inc(self.var, 1)
        dve.wait_ge(self.sd, 1)
        then(dve.reciprocal(self.r[:], self.s1[:]))
        for g in range(G):
            for o, i, r in self.out(g):
                ins = dve.tensor_tensor(o, i, r, ALU.mult)
            ins.then_inc(self.done, 1)


def plain_norm_out(ln_of, xn):
    def out(g):
        ln, k = ln_of(), NT // G
        return [(ln.rows(ln.xm if xn is None else xn, g), ln.rows(ln.xm, g), ln.r[:, g * k:(g + 1) * k].unsqueeze(2).to_broadcast([P, k, C]))]
    return out


def stage_pool(nc, sem, A, K, X):
    with ExitStack() as st:
        def sb(name, shape, dt=F32):
            return st.enter_context(nc.sbuf_tensor(name, shape, dt))
        ps = st.enter_context(nc.psum_tensor("p_ps", [P, 8, BANK], F32))
        H = sb("p_h", [P, Q, 2, 2 * C])
        HT = sb("p_ht", [P, Q * 2, P])
        QT = sb("p_qt", [P, Q * 2, P])
        AE = sb("p_ae", [P, 2, C * B])
        BH = sb("p_bh", [P, 2, C * B])
        wf = sb("p_wf", [C, 2, C])
        wbd = sb("p_wbd", [P, 2, C])
        fb = sb("p_fb", [P, 1])
        sw = sb("p_sw", [P, 2])
        e = sb("p_e", [P, 2, B])
        m = sb("p_m", [P, 2, B + 1])
        dd = sb("p_d", [P, 2, 2, B])
        ex = sb("p_ex", [P, 2, 2, B])
        s = sb("p_s", [P, 2, B + 1])
        rs = sb("p_rs", [P, 2, B])
        co = sb("p_co", [P, 2, 2, B])
        loaded, own_v, zeroed = sem("p_loaded"), sem("p_own"), sem("p_zero")
        normed, ht_mm, ht_ev, w_mm, w_ev, fc_mm, tanh_done, e_mm = (
            sem("p_" + n) for n in ("normed", "htm", "hte", "wm", "we", "fc", "tanh", "em"))
        exp_in, exp_out, a_ready, spread = (sem("p_" + n) for n in ("xi", "xo", "ar", "sp"))
        ln = LayerNorm(nc, sem, st, "p_", X, plain_norm_out(lambda: ln, H), normed)

        def by_batch(t, par):
            return t[:, :, par, :].rearrange("p q (b c) -> p c q b", b=2)

        with nc.Block() as block:
            @block.sync
            def _(sp):
                for k in range(2):
                    sp.dma_start(wf[:, k, :], A["L2_attn_fc_w"]).then_inc(loaded, 16)
                    sp.dma_start(fb[k * C:(k + 1) * C, :], A["L2_attn_fc_b"].rearrange("(c a) -> c a", a=1)
                                 ).then_inc(loaded, 16)
                sp.wait_ge(zeroed, 1)
                for k in range(2):
                    sp.dma_start(sw[k * C:(k + 1) * C, k:k + 1], A["L2_attn_score_w"].rearrange("(c a) -> c a", a=1)
                                 ).then_inc(loaded, 16)

            @block.gpsimd
            def _(pool):
                pool.memset(sw[:], 0.0).then_inc(zeroed, 1)
                pool.memset(wbd[:], 0.0).then_inc(zeroed, 1)

            @block.tensor
            def _(pe):
                pe.wait_ge(loaded, 96)
                pe.transpose(ps[:, 7, 0:C], wf[:].rearrange("p a c -> p (a c)"), K["ident"][0:C, 0:C]).then_inc(w_mm, 1)
                for k in range(Q // 2):
                    pe.wait_ge(normed, k * 2 // QG + 1)
                    if k >= 2:
                        pe.wait_ge(ht_ev, k - 1)
                    for u in range(4):
                        ins = pe.transpose(ps[:, k % 2, u * P:(u + 1) * P], H[:, 2 * k + u // 2, u % 2, :], K["ident"][:])
                    ins.then_inc(ht_mm, 1)
                pe.wait_ge(w_ev, 2)
                for k in range(Q // 2):
                    pe.wait_ge(ht_ev, k + 1)
                    if k >= 2:
                        pe.wait_ge(tanh_done, k - 1)
                    pe.matmul(ps[:, 2 + k % 2, :], wbd[:].rearrange("p b c -> p (b c)"),
                              HT[:, 4 * k:4 * k + 4].rearrange("p a n -> p (a n)"), start=True, stop=True
                              ).then_inc(fc_mm, 1)
                for k in range(2 * Q):
                    pe.wait_ge(tanh_done, k // 4 + 1)
                    ins = pe.matmul(ps[:, 4, 2 * k:2 * k + 2], QT[:, k, :], sw[:], start=True, stop=True)
                ins.then_inc(e_mm, 1)

            @block.scalar
            def _(act):
                ln.scalar(act)
                for k in range(Q // 2):
                    act.wait_ge(ht_mm, k + 1)
                    act.copy(HT[:, 4 * k:4 * k + 4].rearrange("p a n -> p (a n)"), ps[:, k % 2, :]).then_inc(ht_ev, 1)
                for k in range(Q // 2):
                    act.wait_ge(fc_mm, k + 1)
                    act.activation(QT[:, 4 * k:4 * k + 4].rearrange("p a n -> p (a n)"), ps[:, 2 + k % 2, :],
                                   ACT.Tanh, bias=fb[:]).then_inc(tanh_done, 1)
                act.wait_ge(exp_in, 2)
                act.activation(ex[:], dd[:], ACT.Exp).then_inc(exp_out, 1)
                act.wait_ge(a_ready, 1)
                for par in range(2):
                    act.copy(AE[:, par].rearrange("p (c b) -> p c b", b=B),
                             co[:, par, 0:1, :].to_broadcast([P, C, B])).then_inc(spread, 1)

            @block.vector
            def _(dve):
                then = counter(dve, own_v)
                ln.vector(dve, then)
                dve.wait_ge(w_mm, 1)
                dve.wait_ge(zeroed, 2)
                for b2 in range(2):
                    rows = slice(b2 * C, b2 * C + C)
                    dve.tensor_copy(wbd[rows, b2, :], ps[rows, 7, 0:C]).then_inc(w_ev, 1)
                dve.memset(m[:, :, 0:1], -3e38)
                dve.memset(s[:, :, 0:1], 0.0)
                dve.wait_ge(e_mm, 1)
                then(dve.tensor_copy(e[:].rearrange("p a (q b) -> p a q b", b=2),
                                     ps[:, 4, 0:NT].rearrange("p (q a b) -> p a q b", a=2, b=2)))
                for par in range(2):
                    ins = dve.tensor_tensor_scan(m[:, par, 1:B + 1], e[:, par], e[:, par], -3e38, ALU.max, ALU.max)
                then(ins)
                dve.tensor_tensor(dd[:, :, 0, :], m[:, :, 0:B], m[:, :, 1:B + 1], ALU.subtract).then_inc(exp_in, 1)
                dve.tensor_tensor(dd[:, :, 1, :], e[:], m[:, :, 1:B + 1], ALU.subtract).then_inc(exp_in, 1)
                dve.wait_ge(exp_out, 1)
                for par in range(2):
                    ins = dve.tensor_tensor_scan(s[:, par, 1:B + 1], ex[:, par, 0], ex[:, par, 1], 0.0,
                                                 ALU.mult, ALU.add)
                then(ins)
                then(dve.reciprocal(rs[:], s[:, :, 1:B + 1]))
                dve.tensor_tensor(co[:, :, 1, :], ex[:, :, 1, :], rs[:], ALU.mult)
                then(dve.tensor_tensor(co[:, :, 0, :], ex[:, :, 0, :], rs[:], ALU.mult))
                dve.tensor_tensor(co[:, :, 0, :], co[:, :, 0, :], s[:, :, 0:B], ALU.mult).then_inc(a_ready, 1)
                for par in range(2):
                    cb = co[:, par, 1, :].rearrange("p (q b) -> p q b", b=2).unsqueeze(1).to_broadcast([P, C, Q, 2])
                    ins = dve.tensor_tensor(BH[:, par].rearrange("p (c q b) -> p c q b", q=Q, b=2),
                                            by_batch(H, par), cb, ALU.mult)
                then(ins)
                for par in range(2):
                    dve.wait_ge(spread, par + 1)
                    ins = dve.tensor_tensor_scan(BH[:, par], AE[:, par], BH[:, par], 0.0, ALU.mult, ALU.add)
                then(ins)
                for par in range(2):
                    dve.tensor_tensor(by_batch(X, par), by_batch(X, par),
                                      BH[:, par].rearrange("p (c q b) -> p c q b", q=Q, b=2), ALU.add)


def stage_route(nc, sem, A, K, X, L, XS, DT, W1, W2, W3, tag):
    with ExitStack() as st:
        def sb(name, shape, dt=F32):
            return st.enter_context(nc.sbuf_tensor(tag + name, shape, dt))
        ps = st.enter_context(nc.psum_tensor(tag + "r_ps", [P, 8, BANK], F32))
        HL = sb("hl", [P, 2, QG * 4, 2, C], F32R)
        raw = sb("raw", [P, E, HID])
        gw = sb("gw", [P, E])
        gb = sb("gb", [P, E])
        lg = sb("lg", [P, NT, E])
        key = sb("key", [P, NT, E])
        one1 = sb("one1", [P, NT, E])
        mx = sb("mx", [P, 6, NT])
        DD = sb("dd", [P, NT, 2, E], F32R)
        g_loaded, w_loaded, own_v, own_p, normed = (sem(tag + n) for n in ("gl", "wl", "ov", "op", "nm"))
        hi, hl, tr_mm, tr_ev, lg_mm, exp_in, exp_out, dd_done, dt_mm, dt_ev, raw_free, zeroed = (
            sem(tag + n) for n in ("hi", "lo", "tm", "te", "lm", "xi", "xo", "ddd", "dm", "de", "rf", "z"))
        ln = LayerNorm(nc, sem, st, tag, X, plain_norm_out(lambda: ln, None), normed)
        xn = ln.xm
        TG = QG * 4

        with nc.Block() as block:
            @block.sync
            def _(sp):
                for k in range(2):
                    sp.dma_start(gw[k * C:(k + 1) * C, :], A[L + "_gate_w"]).then_inc(g_loaded, 16)
                sp.dma_start(gb[:], A[L + "_gate_b"].rearrange("(a c) -> a c", a=1).to_broadcast([P, E])).then_inc(g_loaded, 16)
                for n, w in enumerate(("_w1", "_w2")):
                    if n:
                        sp.wait_ge(raw_free, n)
                    for k in range(2):
                        sp.dma_start(raw[k * C:(k + 1) * C], A[L + w].rearrange("e d h -> d e h")).then_inc(w_loaded, 16)
                sp.wait_ge(raw_free, 2)
                sp.dma_start(raw[:].rearrange("p e h -> p (e h)")[:, 0:E * C].rearrange("p (e c) -> p e c", c=C),
                             A[L + "_w3"].rearrange("e h o -> h e o")).then_inc(w_loaded, 16)

            @block.gpsimd
            def _(pool):
                then = counter(pool, own_p)
                pool.memset(DT[:].bitcast(F32), 0.0).then_inc(zeroed, 1)
                for n, W in enumerate((W1, W2)):
                    pool.wait_ge(w_loaded, 32 * (n + 1))
                    then(pool.tensor_copy(W[:, 0], raw[:]))
                    pool.tensor_tensor(W[:, 1], raw[:], W[:, 0].bitcast(F32), ALU.subtract).then_inc(raw_free, 1)
                pool.wait_ge(w_loaded, 80)
                r3 = raw[:].rearrange("p e h -> p (e h)")[:, 0:E * C].rearrange("p (e c) -> p e c", c=C)
                then(pool.tensor_copy(W3[:, :, 0, :], r3))
                pool.tensor_tensor(W3[:, :, 1, :], r3, W3[:, :, 0, :].bitcast(F32), ALU.subtract)

            @block.tensor
            def _(pe):
                pe.wait_ge(g_loaded, 48)
                for k in range(NT // 4):
                    g, kk = k // (TG // 4), k % (TG // 4)
                    pe.wait_ge(hl, g + 1)
                    if k >= 2:
                        pe.wait_ge(tr_ev, k - 1)
                    for u in range(4):
                        ins = pe.transpose(ps[:, k % 2, u * P:(u + 1) * P],
                                           HL[:, g % 2, 4 * kk + u].rearrange("p a c -> p (a c)").bitcast(F32),
                                           K["ident"][:])
                    ins.then_inc(tr_mm, 1)
                for t in range(NT):
                    if t % 4 == 0:
                        pe.wait_ge(tr_ev, t // 4 + 1)
                    ins = pe.matmul(ps[:, 2 + t // 32, (t % 32) * E:(t % 32) * E + E], XS[:, t, :].bitcast(F32), gw[:],
                                    start=True, stop=True)
                ins.then_inc(lg_mm, 1)
                pe.wait_ge(dd_done, 2)
                for k in range(Q):
                    ins = pe.transpose(ps[:, 4 + k // 4, (k % 4) * P:(k % 4) * P + P],
                                       DD[:, 4 * k:4 * k + 4].rearrange("p t a e -> p (t a e)").bitcast(F32),
                                       K["ident"][:])
                    if k % 4 == 3:
                        ins.then_inc(dt_mm, 1)

            @block.scalar
            def _(act):
                ln.scalar(act)
                for g in range(G):
                    act.wait_ge(normed, g + 1)
                    if g >= 2:
                        act.wait_ge(tr_mm, (g - 1) * TG // 4)
                    act.copy(HL[:, g % 2, :, 0, :], ln.rows(xn, g)).then_inc(hi, 1)
                    if g >= 1:
                        for k in range((g - 1) * TG // 4, g * TG // 4):
                            act.wait_ge(tr_mm, k + 1)
                            act.copy(XS[:, 4 * k:4 * k + 4].rearrange("p t n -> p (t n)"), ps[:, k % 2, :]).then_inc(tr_ev, 1)
                for k in range((G - 1) * TG // 4, G * TG // 4):
                    act.wait_ge(tr_mm, k + 1)
                    act.copy(XS[:, 4 * k:4 * k + 4].rearrange("p t n -> p (t n)"), ps[:, k % 2, :]).then_inc(tr_ev, 1)
                act.wait_ge(exp_in, 1)
                act.activation(mx[:, 3], mx[:, 2], ACT.Exp).then_inc(exp_out, 1)
                for k in range(4):
                    act.wait_ge(dt_mm, k + 1)
                    act.wait_ge(zeroed, 1)
                    for u in range(4):
                        act.copy(DT[0:32, 16 * k + u:16 * (k + 1):4, :],
                                 ps[32 * u:32 * u + 32, 4 + k, :].rearrange("p (c n) -> p c n", n=P)).then_inc(dt_ev, 1)

            @block.vector
            def _(dve):
                then = counter(dve, own_v)
                ln.vector(dve, then)
                for g in range(G):
                    dve.wait_ge(hi, g + 1)
                    dve.tensor_tensor(HL[:, g % 2, :, 1, :], ln.rows(xn, g), HL[:, g % 2, :, 0, :].bitcast(F32),
                                      ALU.subtract).then_inc(hl, 1)
                full = [P, NT, E]

                def wide(k):
                    return mx[:, k].unsqueeze(2).to_broadcast(full)
                iota = K["iota"][:].unsqueeze(1).to_broadcast(full)
                dve.wait_ge(lg_mm, 1)
                for k in range(2):
                    ins = dve.tensor_tensor(lg[:, 32 * k:32 * k + 32, :], ps[:, 2 + k, :].rearrange("p (t e) -> p t e", e=E),
                                            gb[:].unsqueeze(1).to_broadcast([P, 32, E]), ALU.add)
                then(ins)
                for k, one in ((0, one1), (1, key)):
                    then(dve.tensor_reduce(mx[:, k], lg[:], AX.X, ALU.max))
                    then(dve.tensor_tensor(key[:], lg[:], wide(k), ALU.is_equal))
                    then(dve.scalar_tensor_tensor(out=key[:], in0=key[:], scalar=-64.0, in1=iota,
                                                  op0=ALU.mult, op1=ALU.add))
                    then(dve.tensor_reduce(mx[:, 5], key[:], AX.X, ALU.min))
                    then(dve.tensor_tensor(one[:], key[:], wide(5), ALU.is_equal))
                    if k == 0:
                        then(dve.scalar_tensor_tensor(out=lg[:], in0=one1[:], scalar=-BIG, in1=lg[:],
                                                      op0=ALU.mult, op1=ALU.add))
                dve.tensor_tensor(mx[:, 2], mx[:, 1], mx[:, 0], ALU.subtract).then_inc(exp_in, 1)
                dve.wait_ge(exp_out, 1)
                then(dve.tensor_scalar(mx[:, 4], mx[:, 3], 1.0, None, ALU.add))
                then(dve.reciprocal(mx[:, 4], mx[:, 4]))
                then(dve.tensor_tensor(mx[:, 5], mx[:, 3], mx[:, 4], ALU.mult))
                dve.tensor_tensor(one1[:], one1[:], wide(4), ALU.mult)
                then(dve.tensor_tensor(key[:], key[:], wide(5), ALU.mult))
                then(dve.tensor_tensor(lg[:], one1[:], key[:], ALU.add))
                dve.tensor_copy(DD[:, :, 0, :], lg[:]).then_inc(dd_done, 1)
                dve.wait_ge(dd_done, 1)
                dve.tensor_tensor(DD[:, :, 1, :], lg[:], DD[:, :, 0, :].bitcast(F32), ALU.subtract).then_inc(dd_done, 1)


def stage_experts(nc, sem, K, X, XS, DT, W1, W2, W3, tag):
    LEAD = 4
    SKEW = 2
    NB = 4
    TOK = 4 * P
    with ExitStack() as st:
        def sb(name, shape, dt=F32):
            return st.enter_context(nc.sbuf_tensor(tag + name, shape, dt))

        def pb(name, shape):
            return st.enter_context(nc.psum_tensor(tag + name, shape, F32))
        h1, h2, share = pb("h1", [P, 2, BANK]), pb("h2", [P, 2, BANK]), pb("sh", [P, 2, BANK])
        acc, back = pb("acc", [P, BANK]), pb("back", [P, BANK])
        gate = sb("gate", [P, NB, TOK])
        prod = sb("prod", [P, 2, TOK])
        hid = sb("hid", [P, NB, TOK])
        hid_hi = sb("hidh", [P, NB, TOK], F32R)
        hid_lo = sb("hidl", [P, NB, TOK], F32R)
        outT = sb("outT", [P, TOK])
        h1_done, h2_done, share_done, acc_done, back_done = (sem(tag + n) for n in ("ph1", "ph2", "psh", "pac", "pbk"))
        w3_done = sem(tag + "pw3")
        silu_done, hi_done, outT_done, prod_done, hid_done, lo_done = (
            sem(tag + n) for n in ("asi", "ahi", "aot", "vpr", "vhi", "plo"))

        def chunks(eng, body):
            body(0, True, False)
            with eng.Fori(1, Q - 1) as q:
                body(q, False, False)
            body(Q - 1, False, True)

        with nc.Block() as block:
            @block.tensor
            def _(pe):
                def up(q, e, fresh):
                    u = q * E + e
                    x = XS[:, bass.ts(q, 4), :].rearrange("p t n -> p (t n)")
                    if not fresh:
                        pe.wait_ge(silu_done, u - 1)
                    pe.matmul(h1[:, e % 2], W1[:, 0, e], x, start=True, stop=False)
                    pe.matmul(h1[:, e % 2], W1[:, 1, e], x, start=False, stop=True).then_inc(h1_done, 1)
                    if not fresh:
                        pe.wait_ge(prod_done, u - 1)
                    pe.matmul(h2[:, e % 2], W2[:, 0, e], x, start=True, stop=False)
                    pe.matmul(h2[:, e % 2], W2[:, 1, e], x, start=False, stop=True).then_inc(h2_done, 1)

                def spread(q, e, fresh):
                    u = q * E + e
                    d = DT[:, bass.ts(q, 4), :].rearrange("p t n -> p (t n)")
                    if not fresh:
                        pe.wait_ge(hid_done, u - 1)
                    pe.matmul(share[:, e % 2], K["pick"][:, e, :], d, start=True, stop=True).then_inc(share_done, 1)

                def down(q, e, first):
                    u = q * E + e
                    if e == 0 and not first:
                        pe.wait_ge(outT_done, q)
                    pe.wait_ge(hi_done, u + 1)
                    pe.matmul(acc[:], W3[:, e].rearrange("p a c -> p (a c)"), hid_hi[:, e % NB], start=(e == 0), stop=False)
                    pe.wait_ge(lo_done, u + 1)
                    pe.matmul(acc[:], W3[:, e].rearrange("p a c -> p (a c)"), hid_lo[:, e % NB], start=False,
                              stop=(e == E - 1)).then_inc(w3_done, 1)

                def turn(q):
                    pe.wait_ge(outT_done, q + 1)
                    for t in range(4):
                        ins = pe.matmul(back[:, t * C:(t + 1) * C], outT[:, t * P:(t + 1) * P], K["fold"][:],
                                        start=True, stop=True)
                    ins.then_inc(back_done, 1)

                def body(q, first, last):
                    for e in range(E):
                        if e + LEAD < E:
                            up(q, e + LEAD, False)
                        elif not last:
                            up(q + 1, e + LEAD - E, False)
                        if e + LEAD - 1 < E:
                            spread(q, e + LEAD - 1, False)
                        elif not last:
                            spread(q + 1, e + LEAD - 1 - E, False)
                        down(q, e, first)
                        if e == 2 and not first:
                            turn(q - 1)

                for e in range(LEAD):
                    up(0, e, e < 2)
                    if e:
                        spread(0, e - 1, e < 3)
                chunks(pe, body)
                turn(Q - 1)

            @block.scalar
            def _(act):
                def silu(q, e, fresh):
                    u = q * E + e
                    act.wait_ge(h1_done, u + 1)
                    if not fresh:
                        act.wait_ge(prod_done, u + 1 - NB)
                    act.activation(gate[:, e % NB], h1[:, e % 2], ACT.Silu).then_inc(silu_done, 1)

                def high(q, e, fresh):
                    u = q * E + e
                    act.wait_ge(hid_done, u + 1)
                    if not fresh:
                        act.wait_ge(w3_done, u + 1 - NB)
                    act.copy(hid_hi[:, e % NB], hid[:, e % NB]).then_inc(hi_done, 1)

                def body(q, first, last):
                    for e in range(E):
                        if e + SKEW < E:
                            silu(q, e + SKEW, first and e + SKEW < NB)
                        elif not last:
                            silu(q + 1, e + SKEW - E, False)
                        high(q, e, first and e < NB)
                        if e == 1 and not first:
                            out(q - 1)

                def out(q):
                    act.wait_ge(w3_done, (q + 1) * E)
                    act.copy(outT[:], acc[:]).then_inc(outT_done, 1)

                for e in range(SKEW):
                    silu(0, e, True)
                chunks(act, body)
                out(Q - 1)

            @block.vector
            def _(dve):
                def product(q, e, fresh):
                    u = q * E + e
                    dve.wait_ge(silu_done, u + 1)
                    dve.wait_ge(h2_done, u + 1)
                    if not fresh:
                        dve.wait_ge(hid_done, u - 1)
                    dve.tensor_tensor(prod[:, e % 2], gate[:, e % NB], h2[:, e % 2], ALU.mult).then_inc(prod_done, 1)

                def shared(q, e, fresh):
                    u = q * E + e
                    dve.wait_ge(prod_done, u + 1)
                    dve.wait_ge(share_done, u + 1)
                    if not fresh:
                        dve.wait_ge(lo_done, u + 1 - NB)
                    dve.tensor_tensor(hid[:, e % NB], prod[:, e % 2], share[:, e % 2], ALU.mult).then_inc(hid_done, 1)

                def residual(q):
                    dve.wait_ge(back_done, q + 1)
                    x = X[:, bass.ts(q, 1)].rearrange("p q a c -> p (q a c)")
                    dve.tensor_tensor(x, x, back[:, 0:4 * C], ALU.add)

                def body(q, first, last):
                    for e in range(E):
                        if e + 1 < E:
                            product(q, e + 1, first and e + 1 < 2)
                        elif not last:
                            product(q + 1, 0, False)
                        shared(q, e, first and e < NB)
                        if e == 5 and not first:
                            residual(q - 1)

                product(0, 0, True)
                chunks(dve, body)
                residual(Q - 1)

            @block.gpsimd
            def _(pool):
                def low(q, e, fresh):
                    u = q * E + e
                    pool.wait_ge(hi_done, u + 1)
                    if not fresh:
                        pool.wait_ge(w3_done, u + 1 - NB)
                    pool.tensor_tensor(hid_lo[:, e % NB], hid[:, e % NB], hid_hi[:, e % NB].bitcast(F32),
                                       ALU.subtract).then_inc(lo_done, 1)

                def body(q, first, last):
                    for e in range(E):
                        low(q, e, first and e < NB)
                chunks(pool, body)


def stage_linear(nc, sem, A, K, X):
    SCALE = 1.0 / 8.0
    BC = 4
    NC3 = B // BC
    with ExitStack() as st:
        def sb(name, shape, dt=F32):
            return st.enter_context(nc.sbuf_tensor("l_" + name, shape, dt))
        ps = st.enter_context(nc.psum_tensor("l_ps", [P, 8, BANK], F32))
        xn = sb("xn", [P, B, 2, C])
        xT = sb("xT", [P, B, P])
        sx = sb("sx", [P, B])
        wraw = sb("wraw", [P, 2 * H3, C])
        wv = sb("wv", [P, H3, 2, C])
        wq = sb("wq", [P, H3, 2, C])
        pw = sb("pw", [P, 4, C])
        pbias = sb("pbias", [C, 1])
        bq = sb("bq", [P, H3])
        bv = sb("bv", [P, H3])
        lb = sb("lb", [P, 32])
        ls = sb("ls", [P, 1])
        gain = sb("gain", [P, H3, B])
        vg = sb("vg", [P, 2, H3, BC * P])
        oT = sb("oT", [C, 2, BC, 2, H3, 16])
        loaded, own_v, own_p, normed, zeroed, w_ready = (sem("l_" + n) for n in ("ld", "ov", "op", "nm", "z", "wr"))
        xt_mm, xt_ev, g_mm, g_ready, sx_ready = (sem("l_" + n) for n in ("xm", "xe", "gm", "gr", "sx"))
        v_mm, v_ev, o_mm, o_ev, t_mm, t_ev = (sem("l_" + n) for n in ("vm", "ve", "om", "oe", "tm", "te"))

        def out(g):
            k = NT // G
            pairs = []
            for par in range(2):
                src = ln.xm[:, g * QG:(g + 1) * QG, par, :].rearrange("p q (b c) -> p q b c", b=2)
                dst = xn[:, g * 2 * QG:(g + 1) * 2 * QG, par, :].rearrange("p (q b) c -> p q b c", b=2)
                r = ln.r[:, g * k:(g + 1) * k].rearrange("p (q a b) -> p q a b", a=2, b=2)[:, :, par, :]
                pairs.append((dst, src, r.unsqueeze(3).to_broadcast([P, QG, 2, C])))
            return pairs
        ln = LayerNorm(nc, sem, st, "l_", X, out, normed)

        with nc.Block() as block:
            @block.sync
            def _(sp):
                for k in range(2):
                    rows = slice(k * C, (k + 1) * C)
                    sp.dma_start(wraw[rows].rearrange("p a c -> p (a c)"), A["L3_attn_qkv_w"]).then_inc(loaded, 16)
                    bias = A["L3_attn_qkv_b"].rearrange("(s h d) -> s d h", s=2, d=C)
                    sp.dma_start(bq[rows], bias[0], allow_slow_non_contiguous=True).then_inc(loaded, 16)
                    sp.dma_start(bv[rows], bias[1], allow_slow_non_contiguous=True).then_inc(loaded, 16)
                    sp.dma_start(lb[rows], A["L3_attn_lunchbox"]).then_inc(loaded, 16)
                sp.dma_start(pw[:], A["L3_attn_proj_w"].rearrange("(j p) o -> p j o", p=P)).then_inc(loaded, 16)
                sp.dma_start(pbias[:], A["L3_attn_proj_b"].rearrange("(o a) -> o a", a=1)).then_inc(loaded, 16)

            @block.gpsimd
            def _(pool):
                then = counter(pool, own_p)
                then(pool.memset(wv[:], 0.0))
                pool.wait_ge(loaded, 160)
                for k in range(2):
                    rows = slice(k * C, (k + 1) * C)
                    pool.tensor_copy(wv[rows, :, k, :], wraw[rows, H3:2 * H3, :]).then_inc(w_ready, 1)
                pool.wait_ge(w_ready, 2)
                pool.tensor_copy(wq[:], wraw[:, 0:H3, :].unsqueeze(2).to_broadcast([P, H3, 2, C])).then_inc(w_ready, 1)

            @block.tensor
            def _(pe):
                for k in range(NC3):
                    pe.wait_ge(normed, k // 2 + 1)
                    if k >= 2:
                        pe.wait_ge(xt_ev, k - 1)
                    for u in range(4):
                        ins = pe.transpose(ps[:, k % 2, u * P:(u + 1) * P],
                                           xn[:, 4 * k + u].rearrange("p a c -> p (a c)"), K["ident"][:])
                    ins.then_inc(xt_mm, 1)
                pe.wait_ge(w_ready, 3)
                pe.wait_ge(sx_ready, 1)
                for h in range(H3):
                    ins = pe.matmul(ps[:, 2, h * B:(h + 1) * B], wq[:, h].rearrange("p a c -> p (a c)"), sx[:],
                                    start=True, stop=True)
                ins.then_inc(g_mm, 1)

                def values(k):
                    for h in range(H3):
                        n = k * H3 + h
                        if n >= 2:
                            pe.wait_ge(v_ev, n - 1)
                        else:
                            pe.wait_ge(xt_ev, NC3)
                        pe.matmul(ps[:, n % 2, :], wv[:, h].rearrange("p a c -> p (a c)"),
                                  xT[:, BC * k:BC * (k + 1)].rearrange("p b n -> p (b n)"), start=True, stop=True
                                  ).then_inc(v_mm, 1)

                def project(k):
                    v = vg[:, k % 2].rearrange("p h n -> p (h n)")
                    pe.wait_ge(v_ev, (k + 1) * H3)
                    if k >= 2:
                        pe.wait_ge(o_ev, 4 * (k - 1))
                    for half in range(2):
                        o = ps[0:C, 3 + 2 * (k % 2) + half, :]
                        for jj in range(4):
                            ins = pe.matmul(o, pw[:, jj, :], v[:, half * 2048 + jj:(half + 1) * 2048:4],
                                            start=(jj == 0), stop=(jj == 3))
                        ins.then_inc(o_mm, 1)

                def turn(k):
                    pe.wait_ge(o_ev, 4 * (k + 1))
                    if k >= 1:
                        pe.wait_ge(t_ev, 2 * k)
                    for b in range(BC):
                        for par in range(2):
                            ins = pe.transpose(ps[:, 7, (2 * b + par) * C:(2 * b + par + 1) * C],
                                               oT[:, k % 2, b, par].rearrange("p h m -> p (h m)"), K["ident"][0:C, 0:C])
                    ins.then_inc(t_mm, 1)

                values(0)
                for k in range(NC3):
                    if k + 1 < NC3:
                        values(k + 1)
                    project(k)
                    if k >= 1:
                        turn(k - 1)
                turn(NC3 - 1)

            @block.scalar
            def _(act):
                ln.scalar(act)
                for k in range(NC3):
                    act.wait_ge(xt_mm, k + 1)
                    act.copy(xT[:, 4 * k:4 * k + 4].rearrange("p b n -> p (b n)"), ps[:, k % 2, :]).then_inc(xt_ev, 1)
                for k in range(NC3):
                    for half in range(2):
                        act.wait_ge(o_mm, 2 * k + half + 1)
                        if k >= 2:
                            act.wait_ge(t_mm, k - 1)
                        src = ps[0:C, 3 + 2 * (k % 2) + half, :].rearrange("p (h b m a) -> p a h b m", h=4, b=BC, a=2)
                        for par in range(2):
                            act.activation(oT[:, k % 2, :, par, 4 * half:4 * half + 4, :].rearrange("p b h m -> p h b m"),
                                           src[:, par], ACT.Identity, bias=pbias[:]).then_inc(o_ev, 1)

            @block.vector
            def _(dve):
                then = counter(dve, own_v)
                ln.vector(dve, then)
                dve.wait_ge(loaded, 160)
                then(dve.tensor_reduce(ls[:], lb[:], AX.X, ALU.add))
                then(dve.tensor_scalar(ls[:], ls[:], SCALE, None, ALU.mult))
                then(dve.tensor_scalar(bq[:], bq[:], float(N), None, ALU.mult))
                dve.wait_ge(xt_ev, NC3)
                dve.tensor_reduce(sx[:], xT[:], AX.X, ALU.add).then_inc(sx_ready, 1)
                dve.wait_ge(g_mm, 1)
                then(dve.tensor_tensor(gain[:], ps[:, 2, 0:H3 * B].rearrange("p (h b) -> p h b", b=B),
                                       bq[:].unsqueeze(2).to_broadcast([P, H3, B]), ALU.add))
                then(dve.tensor_scalar(gain[:], gain[:], ls[:], None, ALU.mult))

                def residual(k):
                    dve.wait_ge(t_mm, k + 1)
                    for u in range(2):
                        x = X[:, 2 * k + u].rearrange("p a (b c) -> p a b c", b=2)
                        t = ps[:, 7, u * 4 * C:(u + 1) * 4 * C].rearrange("p (b a c) -> p a b c", b=2, a=2)
                        dve.tensor_tensor(x, x, t, ALU.add).then_inc(t_ev, 1)

                for k in range(NC3):
                    for h in range(H3):
                        n = k * H3 + h
                        dve.wait_ge(v_mm, n + 1)
                        if k >= 2:
                            dve.wait_ge(o_mm, 2 * (k - 1))
                        dve.scalar_tensor_tensor(
                            out=vg[:, k % 2, h].rearrange("p (b n) -> p b n", b=BC),
                            in0=ps[:, n % 2, :].rearrange("p (b n) -> p b n", b=BC), scalar=bv[:, h:h + 1],
                            in1=gain[:, h, BC * k:BC * (k + 1)].unsqueeze(2).to_broadcast([P, BC, P]),
                            op0=ALU.add, op1=ALU.mult).then_inc(v_ev, 1)
                    if k >= 2:
                        residual(k - 2)
                residual(NC3 - 2)
                residual(NC3 - 1)


def stage_out(nc, sem, K, X, out):
    with ExitStack() as st:
        ps = st.enter_context(nc.psum_tensor("o_ps", [P, 4, BANK], F32))
        Y = st.enter_context(nc.sbuf_tensor("o_y", [P, Q, N], F32))
        mm, ev, stored = sem("o_mm"), sem("o_ev"), sem("o_st")
        out_v = out.rearrange("(q b) c y w -> (b c) q (y w)", b=2)
        with nc.Block() as block:
            @block.tensor
            def _(pe):
                for k in range(Q // 2):
                    if k >= 4:
                        pe.wait_ge(ev, k - 3)
                    for u in range(4):
                        ins = pe.transpose(ps[:, k % 4, u * P:(u + 1) * P], X[:, 2 * k + u // 2, u % 2, :], K["ident"][:])
                    ins.then_inc(mm, 1)

            def move(eng, copy, k):
                eng.wait_ge(mm, k + 1)
                copy(Y[:, 2 * k:2 * k + 2].rearrange("p q (n a) -> p q a n", a=2),
                     ps[:, k % 4, :].rearrange("p (q a n) -> p q a n", q=2, a=2)).then_inc(ev, 1)

            @block.vector
            def _(dve):
                for k in range(Q // 2):
                    move(dve, dve.tensor_copy, k)

            @block.sync
            def _(sp):
                for g in range(G):
                    sp.wait_ge(ev, 2 * (g + 1))
                    sp.dma_start(out_v[:, g * QG:(g + 1) * QG, :], Y[:, g * QG:(g + 1) * QG, :]).then_inc(stored, 16)
                sp.wait_ge(stored, 16 * G)


def stage_constants(nc, sem, A, K):
    with ExitStack() as st:
        raw = st.enter_context(nc.sbuf_tensor("c_raw", [P, E, P], F32))
        loaded = sem("c_loaded")
        with nc.Block() as block:
            @block.sync
            def _(sp):
                sp.dma_start(raw[:], A["k_pick"]).then_inc(loaded, 16)
                sp.dma_start(K["fold"][:], A["k_fold"]).then_inc(loaded, 16)
                sp.dma_start(K["iota"][:], A["k_iota"]).then_inc(loaded, 16)

            @block.gpsimd
            def _(pool):
                pool.wait_ge(loaded, 48)
                pool.tensor_copy(K["pick"][:], raw[:])


def build(nc, A, out):
    with ExitStack() as ctx:
        def sb(name, shape, dt=F32):
            return ctx.enter_context(nc.sbuf_tensor(name, shape, dt))

        def sem(name):
            return ctx.enter_context(nc.semaphore(name))
        X = sb("X", [P, Q, 2, 2 * C])
        K = {"ident": sb("ident", [P, P])}
        with ExitStack() as st:
            def tmp(name, shape, dt=F32):
                return st.enter_context(nc.sbuf_tensor(name, shape, dt))
            Xc = tmp("Xc", [P, Q, N])
            wproj = tmp("wproj", [P, 2, C])
            T = tmp("T", [P, 2, 2 * HD, P])
            V = tmp("V", [P, Q, 2, 2 * C + 4])
            QKf = tmp("QKf", [P, Q, 2, 4 * C])
            with nc.sbuf_tensor("xn0", [P, Q, N], F32) as xn, nc.sbuf_tensor("wqkv", [P, 3, 2, C], F32) as wqkv:
                stage_norm(nc, sem, A, K, Xc, xn, wqkv, wproj, T)
                stage_qkv(nc, sem, A, xn, wqkv, QKf, V)
            stage_attend(nc, sem, A, K, Xc, QKf, V, T, wproj, X)
        K["pick"] = sb("pick", [P, E, P], F32R)
        K["fold"] = sb("fold", [P, C])
        K["iota"] = sb("iota", [P, E])
        stage_constants(nc, sem, A, K)
        stage_pool(nc, sem, A, K, X)
        for L in ("L2_ffn", "L3_ffn"):
            with ExitStack() as st:
                used = []

                def ffn_sem(name):
                    used.append(nc.alloc_semaphore(name=name))
                    return used[-1]
                def tmp(name, shape, dt=F32):
                    return st.enter_context(nc.sbuf_tensor(L + name, shape, dt))
                XS = tmp("XS", [P, NT, P], F32R)
                DT = tmp("DT", [P, NT, P], F32R)
                W1 = tmp("W1", [P, 2, E, HID], F32R)
                W2 = tmp("W2", [P, 2, E, HID], F32R)
                W3 = tmp("W3", [P, E, 2, C], F32R)
                stage_route(nc, ffn_sem, A, K, X, L, XS, DT, W1, W2, W3, L + "r_")
                stage_experts(nc, ffn_sem, K, X, XS, DT, W1, W2, W3, L + "e_")
                nc.clear_and_free_semaphores(used)
                nc.all_engine_barrier()
            if L == "L2_ffn":
                stage_linear(nc, sem, A, K, X)
        stage_out(nc, sem, K, X, out)


def shape_constants():
    pos = np.zeros((5, 4, P), np.float32)
    for r in range(P):
        for j in range(4):
            n = (r % C) * 4 + j
            jj, ii = np.float32(n % WW) / np.float32(WW - 1), np.float32(n // WW) / np.float32(HH - 1)
            pos[:, j, r] = (jj, ii, np.float32(1) - jj, np.float32(1) - ii, 1)
    pairs = np.kron(np.eye(P // 2), np.full((2, 2), 0.5)).astype(np.float32)
    mask = np.kron(np.eye(P // HD), np.ones((HD, HD))).astype(np.float32)
    selx = np.zeros((KS, KS, WW, KS, WW), np.float32)
    for dy in range(KS):
        for ix in range(WW):
            for jx in range(WW):
                if 0 <= jx - ix + KS // 2 < KS:
                    selx[dy, jx - ix + KS // 2, ix, dy, jx] = 1
    sely = np.zeros((KS, WW, 2, 2 * HH - 1, WW // 2), np.float32)
    for dy in range(KS):
        for jx in range(WW):
            sely[dy, jx, jx % 2, dy - KS // 2 + HH - 1, jx // 2] = 1
    pick = np.zeros((P, E, P), np.float32)
    for e in range(E):
        pick[e, e, :] = pick[E + e, e, :] = 1
    return {
        "k_pos": pos, "k_pairs": pairs, "k_mask": mask, "k_ident": np.eye(P, dtype=np.float32),
        "k_selx": selx.reshape(KS * KS, WW, KS * WW), "k_sely": sely.reshape(KS * WW, 2, -1),
        "k_pick": pick, "k_fold": np.concatenate([np.eye(C), np.eye(C)]).astype(np.float32),
        "k_iota": np.tile(np.arange(E, dtype=np.float32), (P, 1)),
    }


_INS = ['x', 'L0_conv_W', 'L0_conv_b', 'L1_conv_Wq', 'L1_conv_bq', 'L1_conv_Wkv', 'L1_conv_bkv', 'L1_conv_Wproj',
        'L1_conv_bproj', 'L1_conv_dwc_w', 'L1_conv_dwc_b', 'L1_conv_scale_param', 'L2_attn_fc_w', 'L2_attn_fc_b',
        'L2_attn_score_w', 'L2_ffn_gate_w', 'L2_ffn_gate_b', 'L2_ffn_w1', 'L2_ffn_w2', 'L2_ffn_w3', 'L3_attn_qkv_w',
        'L3_attn_qkv_b', 'L3_attn_lunchbox', 'L3_attn_proj_w', 'L3_attn_proj_b', 'L3_ffn_gate_w', 'L3_ffn_gate_b',
        'L3_ffn_w1', 'L3_ffn_w2', 'L3_ffn_w3']


def kernel(**inputs):
    import concourse.bacc as bacc
    from concourse.bass_utils import run_bass_kernel_spmd

    nc = bacc.Bacc("TRN2", target_bir_lowering=False, num_devices=1)
    arrays, A = {}, {}
    for name, a in [(n, inputs[n]) for n in _INS] + list(shape_constants().items()):
        a = np.ascontiguousarray(a)
        arrays[f"in_{name}"] = a
        A[name] = nc.dram_tensor(f"in_{name}", a.shape, mybir.dt.from_np(a.dtype), kind="ExternalInput").ap()
    out = nc.dram_tensor("out_x", (B, C, HH, WW), F32, kind="ExternalOutput").ap()
    build(nc, A, out)
    r = run_bass_kernel_spmd(nc, [arrays], core_ids=[0])
    return r.results[0]["out_x"]
```

```python
from contextlib import ExitStack

import numpy as np

import concourse.bass as bass
from concourse import mybir

F32 = mybir.dt.float32
F32R = mybir.dt.float32r
ALU = mybir.AluOpType
ACT = mybir.ActivationFunctionType
AX = mybir.AxisListType

B, C, HH, WW = 32, 64, 16, 16
N = HH * WW
P = 128
Q = B // 2
NT = Q * 2 * 2
NH, HD = 8, C // 8
KS = 5
E, HID = 16, 128
H3 = 8
G = 4
QG = Q // G
BANK = 512
BIG = 1e38


def counter(eng, sem):
    n = [0]

    def then(ins):
        n[0] += 1
        ins.then_inc(sem, 1)
        eng.wait_ge(sem, n[0])
    return then


def bcast(ap, shape):
    return ap.to_broadcast(shape)


def stage_norm(nc, sem, A, K, Xc, xn, wqkv, brow, wproj, rowk, epsv):
    with ExitStack() as st:
        def sb(name, shape, dt=F32):
            return st.enter_context(nc.sbuf_tensor(name, shape, dt))
        ps = st.enter_context(nc.psum_tensor("n_ps", [P, 8, BANK], F32))
        posw = sb("n_posw", [5, C])
        w1 = sb("n_w1", [P, 2, C])
        w2 = sb("n_w2", [P, 2, C])
        taps = sb("n_taps", [KS * KS, HD])
        selx = sb("n_selx", [KS * KS, WW, KS * WW])
        pos = sb("n_pos", [5, 4, P])
        pairs = sb("n_pairs", [P, P])
        stats = sb("n_stats", [P, Q, 6])
        mv = sb("n_mv", [P, Q, 2])
        gm = sb("n_gm", [P, Q, 2])
        dm = sb("n_dm", [P, Q])
        vg = sb("n_vg", [P, Q])
        sd = sb("n_sd", [P, Q])
        rs = sb("n_rs", [P, Q])
        nmr = sb("n_nmr", [P, Q])
        sp_ = sb("n_sp", [P, 8, C])
        small, big_w, x_in = sem("n_small"), sem("n_bigw"), [sem(f"n_x{g}") for g in range(G)]
        pe_ready, mv_ready, gm_ready, var_ready, sd_ready = (
            sem("n_pe"), sem("n_mv"), sem("n_gm"), sem("n_var"), sem("n_sd"))
        scale_in, bias_in, exp_in, exp_out, ln_in, ln_out = (sem("n_" + n) for n in ("sc", "bi", "ei", "eo", "li", "lo"))
        wt_ready, rowk_ps, later = sem("n_wt"), sem("n_rkp"), sem("n_later")
        own_v, own_p, zeroed = sem("n_ownv"), sem("n_ownp"), sem("n_zero")
        x_v = A["x"].rearrange("(q b) c y w -> (b c) q (y w)", b=2)

        with nc.Block() as block:
            @block.sync
            def _(sp):
                sp.dma_start(sp_[:, 0, :], A["L1_conv_scale_param"].rearrange("a b c -> (a b) c").to_broadcast([P, C])
                             ).then_inc(scale_in, 16)
                for g in range(G):
                    sp.dma_start(Xc[:, g * QG:(g + 1) * QG, :], x_v[:, g * QG:(g + 1) * QG, :]).then_inc(x_in[g], 16)
                sp.wait_ge(zeroed, 1)
                for k, src in enumerate((A["L1_conv_bq"][0:C], A["L1_conv_bkv"][0:C], A["L1_conv_bkv"][C:2 * C])):
                    for b2 in range(2):
                        sp.dma_start(brow[0:1, k, b2, :], src.rearrange("(a c) -> a c", a=1)).then_inc(bias_in, 16)
                for name in ("fold", "iota", "fill", "reset", "upper"):
                    sp.dma_start(K[name][:], A["k_" + name]).then_inc(later, 16)
                sp.wait_ge(later, 80)

            @block.gpsimd
            def _(pool):
                then = counter(pool, own_p)
                pool.memset(brow[:], 0.0).then_inc(zeroed, 1)
                pool.memset(wqkv[:], 0.0).then_inc(zeroed, 1)
                pool.memset(wproj[:], 0.0).then_inc(zeroed, 1)
                pool.memset(K["ones"][:], 1.0)
                then(pool.memset(K["row0"][:], 0.0))
                pool.memset(K["row0"][0:1, :], 1.0)

            @block.scalar
            def _(act):
                act.dma_start(pos[:], A["k_pos"]).then_inc(small, 16)
                act.dma_start(posw[0:4, :], A["L0_conv_W"].rearrange("c k -> k c"), allow_slow_non_contiguous=True
                              ).then_inc(small, 16)
                act.dma_start(posw[4:5, :], A["L0_conv_b"].rearrange("(a c) -> a c", a=1)).then_inc(small, 16)
                act.dma_start(pairs[:], A["k_pairs"]).then_inc(big_w, 16)
                act.dma_start(K["ident"][:], A["k_ident"]).then_inc(big_w, 16)
                for half in range(2):
                    act.dma_start(w1[0:C, half, :], A["L1_conv_Wq"]).then_inc(big_w, 16)
                    act.dma_start(w1[C:P, half, :], A["L1_conv_Wkv"][0:C, :]).then_inc(big_w, 16)
                    act.dma_start(w2[0:C, half, :], A["L1_conv_Wkv"][C:2 * C, :]).then_inc(big_w, 16)
                    act.dma_start(w2[C:P, half, :], A["L1_conv_Wproj"]).then_inc(big_w, 16)
                act.dma_start(taps[:], A["L1_conv_dwc_w"].rearrange("d a y x -> (a y x) d"),
                              allow_slow_non_contiguous=True).then_inc(big_w, 16)
                act.dma_start(selx[:], A["k_selx"]).then_inc(big_w, 16)
                act.wait_ge(exp_in, 1)
                act.activation(sp_[:, 2, :], sp_[:, 1, :], ACT.Exp).then_inc(exp_out, 1)
                act.wait_ge(ln_in, 1)
                act.activation(sp_[:, 5, :], sp_[:, 3, :], ACT.Ln).then_inc(ln_out, 1)
                act.wait_ge(var_ready, 1)
                act.activation(sd[:], vg[:], ACT.Sqrt).then_inc(sd_ready, 1)

            @block.tensor
            def _(pe):
                pe.wait_ge(small, 48)
                for j in range(4):
                    ins = pe.matmul(ps[:, 0, j * C:(j + 1) * C], pos[:, j, :], posw[:], start=True, stop=True)
                ins.then_inc(pe_ready, 1)
                pe.wait_ge(big_w, 16 * 12)
                pe.transpose(ps[:, 1, 0:P], w1[:].rearrange("p a c -> p (a c)"), K["ident"][:])
                pe.transpose(ps[:, 1, P:2 * P], w2[:].rearrange("p a c -> p (a c)"), K["ident"][:]).then_inc(wt_ready, 1)
                for ix in range(WW):
                    ins = pe.matmul(ps[0:KS * WW, 2, ix * 8:ix * 8 + 8], selx[:, ix, :], taps[:], start=True, stop=True)
                ins.then_inc(rowk_ps, 1)
                pe.wait_ge(mv_ready, 1)
                pe.matmul(ps[:, 3, 0:2 * Q], pairs[:], mv[:].rearrange("p q k -> p (q k)"),
                          start=True, stop=True).then_inc(gm_ready, 1)

            @block.vector
            def _(dve):
                then = counter(dve, own_v)
                dve.wait_ge(scale_in, 16)
                then(dve.tensor_scalar(sp_[:, 4, :], sp_[:, 0, :], -1.0, None, ALU.mult))
                dve.tensor_tensor(sp_[:, 1, :], sp_[:, 0, :], sp_[:, 4, :], ALU.min).then_inc(exp_in, 1)
                dve.wait_ge(exp_out, 1)
                dve.tensor_scalar(sp_[:, 3, :], sp_[:, 2, :], 1.0, None, ALU.add).then_inc(ln_in, 1)
                dve.wait_ge(ln_in, 1)
                then(dve.tensor_scalar(sp_[:, 4, :], sp_[:, 3, :], -1.0, None, ALU.add))
                then(dve.tensor_scalar(sp_[:, 6, :], sp_[:, 4, :], 0.0, None, ALU.is_equal))
                dve.wait_ge(ln_out, 1)
                then(dve.tensor_tensor(sp_[:, 5, :], sp_[:, 5, :], sp_[:, 6, :], ALU.add))
                then(dve.tensor_tensor(sp_[:, 4, :], sp_[:, 4, :], sp_[:, 6, :], ALU.add))
                then(dve.reciprocal(sp_[:, 7, :], sp_[:, 4, :]))
                then(dve.tensor_tensor(sp_[:, 5, :], sp_[:, 5, :], sp_[:, 2, :], ALU.mult))
                then(dve.tensor_tensor(sp_[:, 5, :], sp_[:, 5, :], sp_[:, 7, :], ALU.mult))
                then(dve.scalar_tensor_tensor(out=sp_[:, 6, :], in0=sp_[:, 0, :], scalar=0.0, in1=sp_[:, 5, :],
                                              op0=ALU.max, op1=ALU.add))
                then(dve.reciprocal(sp_[:, 7, :], sp_[:, 6, :]))
                dve.tensor_scalar(epsv[:], sp_[:, 7, :], 1e-6, None, ALU.mult)
                dve.wait_ge(pe_ready, 1)
                for g in range(G):
                    dve.wait_ge(x_in[g], 16)
                    xg = Xc[:, g * QG:(g + 1) * QG, :]
                    then(dve.tensor_tensor(xg, xg, ps[:, 0, 0:N].unsqueeze(1).to_broadcast([P, QG, N]), ALU.add))
                    for q in range(g * QG, (g + 1) * QG):
                        ins = dve.bn_stats(stats[:, q, :], Xc[:, q, :])
                then(ins)
                for q in range(Q):
                    ins = dve.bn_aggr(mv[:, q, :], stats[:, q, :])
                ins.then_inc(mv_ready, 1)
                dve.wait_ge(gm_ready, 1)
                then(dve.tensor_copy(gm[:].rearrange("p q k -> p (q k)"), ps[:, 3, 0:2 * Q]))
                then(dve.tensor_tensor(dm[:], mv[:, :, 0], gm[:, :, 0], ALU.subtract))
                then(dve.tensor_tensor(dm[:], dm[:], dm[:], ALU.mult))
                then(dve.tensor_tensor(vg[:], dm[:], gm[:, :, 1], ALU.add))
                dve.tensor_scalar(vg[:], vg[:], 1e-5, None, ALU.add).then_inc(var_ready, 1)
                dve.wait_ge(wt_ready, 1)
                dve.wait_ge(zeroed, 3)
                for b2 in range(2):
                    rows = slice(b2 * C, b2 * C + C)
                    for k in range(2):
                        dve.tensor_tensor(wqkv[rows, k, b2, :], ps[rows, 1, k * C:(k + 1) * C], sp_[rows, 7, :], ALU.mult)
                    dve.tensor_copy(wqkv[rows, 2, b2, :], ps[rows, 1, 2 * C:3 * C])
                    dve.tensor_copy(wproj[rows, b2, :], ps[rows, 1, 3 * C:4 * C])
                dve.wait_ge(bias_in, 96)
                b4 = brow[0:1, 0:2].rearrange("p k b c -> p (k b) c")
                dve.tensor_tensor(b4, b4, sp_[0:1, 7:8, :].to_broadcast([1, 4, C]), ALU.mult)
                dve.wait_ge(rowk_ps, 1)
                dve.tensor_copy(rowk[:], ps[0:KS * WW, 2, 0:P].rearrange("k (b a d) -> k d a b", a=2, d=8))
                dve.wait_ge(sd_ready, 1)
                then(dve.reciprocal(rs[:], sd[:]))
                then(dve.scalar_tensor_tensor(out=nmr[:], in0=gm[:, :, 0], scalar=-1.0, in1=rs[:],
                                              op0=ALU.mult, op1=ALU.mult))
                for q in range(Q):
                    dve.tensor_scalar(xn[:, q, :], Xc[:, q, :], rs[:, q:q + 1], nmr[:, q:q + 1], ALU.mult, ALU.add)


def stage_qkv(nc, sem, A, K, xn, wqkv, brow, rowk, epsv, QKf, V, FM, S):
    with ExitStack() as st:
        def sb(name, shape, dt=F32):
            return st.enter_context(nc.sbuf_tensor(name, shape, dt))
        ps = st.enter_context(nc.psum_tensor("q_ps", [P, 8, BANK], F32))
        QK = sb("q_qk", [P, Q, 2, 4 * C])
        S6 = sb("q_s6", [P, 2, QG * 2 * 4 * C])
        T = sb("q_t", [P, 2, 2 * HD, P])
        sely = sb("q_sely", [KS * WW, 2, 31 * 8])
        dwb = sb("q_dwb", [P, HD])
        n2 = sb("q_n2", [P, Q * 2 * 4])
        n6 = sb("q_n6", [P, Q * 2 * 4])
        loaded, own_v = sem("q_loaded"), sem("q_own")
        mm, qk_ev, v_ev, ones = sem("q_mm"), sem("q_evac"), sem("q_vev"), sem("q_ones")
        grp_ready, squared, cubed, sixth, norms, roots = (
            sem("q_grp"), sem("q_squared"), sem("q_cubed"), sem("q_sixth"), sem("q_norms"), sem("q_roots"))
        band_ps, band_sb, conv_mm, conv_ev, s_free, f_ready = (sem("q_" + n) for n in ("bp", "bs", "cm", "ce", "sf", "fr"))
        NT2 = 2 * Q

        def part(t, g):
            return t[:, g * QG:(g + 1) * QG].rearrange("p q a c -> p (q a c)")

        def rows(ap):
            return ap.rearrange("p (r c) -> p r c", c=C)

        with nc.Block() as block:
            @block.sync
            def _(sp):
                sp.dma_start(sely[:], A["k_sely"]).then_inc(loaded, 16)
                sp.dma_start(dwb[:], A["L1_conv_dwc_b"].rearrange("(a d) -> a d", a=1).to_broadcast([P, HD])
                             ).then_inc(loaded, 16)

            @block.tensor
            def _(pe):
                for i in range(NT2):
                    if i >= 8 and i % 2 == 0:
                        pe.wait_ge(qk_ev, i // 2 - 3)
                    if i >= 8 and i % 4 == 0:
                        pe.wait_ge(v_ev, i // 4 - 1)
                    for bank, c0, k in ((i // 2 % 4, i % 2 * 4 * C, slice(0, 2)), (4 + i // 4 % 2, i % 4 * 2 * C, slice(2, 3))):
                        w, b = (t[:, k].rearrange("p k b c -> p (k b c)") for t in (wqkv, brow))
                        o = ps[:, bank, c0:c0 + (k.stop - k.start) * 2 * C]
                        pe.matmul(o, xn[:, i // 2, i % 2:N:2], w, start=True, stop=False)
                        ins = pe.matmul(o, K["row0"][:], b, start=False, stop=True)
                    if i % 2 == 1:
                        ins.then_inc(mm, 1)
                pe.wait_ge(loaded, 32)
                for k in range(8):
                    pj, i4 = k // 4, (k % 4) * 4
                    if k >= 2:
                        pe.wait_ge(band_sb, k - 1)
                    for u in range(4):
                        s0 = (HH - 1 - (i4 + u)) * 8
                        ins = pe.matmul(ps[:, 6 + k % 2, u * P:(u + 1) * P], sely[:, pj, s0:s0 + P],
                                        rowk[:].rearrange("k d a b -> k (d a b)"), start=True, stop=True)
                    ins.then_inc(band_ps, 1)
                pe.wait_ge(v_ev, Q // 2)
                pe.wait_ge(band_sb, 8)
                for k in range(2 * HD):
                    d, pi = k // 2, k % 2
                    if k >= 2:
                        pe.wait_ge(conv_ev, k - 1)
                    for pj in range(2):
                        ins = pe.matmul(ps[:, 4 + k % 2, 0:B * NH], T[:, pj, 2 * d + pi, :],
                                        V[:, :, pj, d:2 * C:HD], start=(pj == 0), stop=(pj == 1))
                    ins.then_inc(conv_mm, 1)

            @block.scalar
            def _(act):
                def square(g):
                    if g >= 2:
                        act.wait_ge(cubed, g - 1)
                        act.wait_ge(norms, 2 * (g - 2) + 1)
                    act.activation(S[:, g % 2], part(QK, g), ACT.Square).then_inc(squared, 1)

                def sixths(g):
                    act.wait_ge(cubed, g + 1)
                    if g >= 2:
                        act.wait_ge(norms, 2 * (g - 2) + 2)
                    act.activation(S6[:, g % 2], part(QKf, g), ACT.Square).then_inc(sixth, 1)

                def root(g):
                    act.wait_ge(norms, 2 * g + 2)
                    r = slice(g * QG * 8, (g + 1) * QG * 8)
                    act.activation(n2[:, r], n2[:, r], ACT.Sqrt).then_inc(roots, 1)
                    act.activation(n6[:, r], n6[:, r], ACT.Sqrt).then_inc(roots, 1)

                def bands(k):
                    pj, i4 = k // 4, (k % 4) * 4
                    act.wait_ge(band_ps, k + 1)
                    act.copy(T[:, pj, :, i4 * 8:(i4 + 4) * 8].rearrange("p a (u b) -> p u a b", b=8),
                             ps[:, 6 + k % 2, :].rearrange("p (u a b) -> p u a b", u=4, b=8)).then_inc(band_sb, 1)

                def conv(k):
                    d, pi = k // 2, k % 2
                    act.wait_ge(conv_mm, k + 1)
                    act.activation(FM[:, :, pi, d:2 * C:HD], ps[:, 4 + k % 2, 0:B * NH].rearrange("p (q h) -> p q h", q=Q),
                                   ACT.Identity, bias=dwb[:, d:d + 1]).then_inc(conv_ev, 1)

                for g in range(G):
                    for j in range(g * QG // 2, (g + 1) * QG // 2):
                        act.wait_ge(mm, 2 * j + 2)
                        act.copy(V[:, 2 * j:2 * j + 2, :, 0:2 * C],
                                 ps[:, 4 + j % 2, :].rearrange("p (q a c) -> p q a c", q=2, a=2)).then_inc(v_ev, 1)
                    act.wait_ge(qk_ev, (g + 1) * QG)
                    square(g)
                    if g >= 1:
                        sixths(g - 1)
                    if g >= 2:
                        root(g - 2)
                act.wait_ge(loaded, 32)
                bands(0)
                bands(1)
                sixths(G - 1)
                bands(2)
                bands(3)
                root(G - 2)
                for k in range(4, 8):
                    bands(k)
                root(G - 1)
                for k in range(2 * HD):
                    conv(k)

            def scale(eng, g, k0):
                eng.wait_ge(f_ready, g + 1)
                eng.wait_ge(sixth, g + 1)
                v = QKf[:, g * QG:(g + 1) * QG].rearrange("p q a (k c) -> p (q a) k c", c=C)[:, :, k0:k0 + 2]
                f = n2[:, g * QG * 8:(g + 1) * QG * 8].rearrange("p (r k) -> p r k", k=4)[:, :, k0:k0 + 2]
                eng.tensor_tensor(v, v, f.unsqueeze(3).to_broadcast([P, 2 * QG, 2, C]), ALU.mult)

            @block.gpsimd
            def _(pool):
                pool.memset(V[:, :, :, 2 * C:2 * C + 4], 1.0)
                for g in range(G + 1):
                    if g < G:
                        pool.wait_ge(squared, g + 1)
                        pool.tensor_tensor(part(QKf, g), S[:, g % 2], part(QK, g), ALU.mult).then_inc(cubed, 1)
                    if g >= 1:
                        scale(pool, g - 1, 2)

            @block.vector
            def _(dve):
                then = counter(dve, own_v)
                for g in range(G + 3):
                    if g < G:
                        for q in range(g * QG, (g + 1) * QG):
                            dve.wait_ge(mm, q + 1)
                            dve.scalar_tensor_tensor(out=rows(QK[:, q].rearrange("p a c -> p (a c)")), in0=rows(ps[:, q % 4, :]),
                                                     scalar=0.0, in1=epsv[:].unsqueeze(1).to_broadcast([P, 8, C]),
                                                     op0=ALU.max, op1=ALU.add).then_inc(qk_ev, 1)
                    if 0 <= g - 1 < G:
                        r = slice((g - 1) * QG * 8, g * QG * 8)
                        dve.wait_ge(squared, g)
                        dve.tensor_reduce(n2[:, r], rows(S[:, (g - 1) % 2]), AX.X, ALU.add).then_inc(norms, 1)
                        dve.wait_ge(sixth, g)
                        dve.tensor_reduce(n6[:, r], rows(S6[:, (g - 1) % 2]), AX.X, ALU.add).then_inc(norms, 1)
                    if 0 <= g - 2 < G:
                        r = slice((g - 2) * QG * 8, (g - 1) * QG * 8)
                        dve.wait_ge(roots, 2 * (g - 1))
                        then(dve.reciprocal(n6[:, r], n6[:, r]))
                        dve.tensor_tensor(n2[:, r], n2[:, r], n6[:, r], ALU.mult).then_inc(f_ready, 1)
                        scale(dve, g - 2, 0)


def stage_attend(nc, sem, A, K, Xc, QKf, V, FM, wproj, X, WR, XD, zeros, zeroed):
    with ExitStack() as st:
        def sb(name, shape, dt=F32):
            return st.enter_context(nc.sbuf_tensor(name, shape, dt))
        ps = st.enter_context(nc.psum_tensor("a_ps", [P, 8, BANK], F32))
        W = P + 2 * NH
        QT = sb("a_qt", [P, Q, 2, P])
        mask = sb("a_mask", [P, P])
        BD = sb("a_bd", [P, Q, W])
        z = sb("a_z", [P, 2, 2, 2 * NH])
        y = sb("a_y", [P, 2, 2, P])
        yf = sb("a_yf", [P, 2, 2, P])
        oT = sb("a_ot", [P, 2, 2, P])
        bp = sb("a_bp", [P, 2, C])
        loaded, own_v = sem("a_loaded"), sem("a_own")
        qt_mm, qt_ev, kv_mm, kv_ev = (sem("a_qm"), sem("a_qe"), sem("a_km"), sem("a_ke"))
        nd_mm, y_ready, yf_ready, t_mm, o_ready, pr_mm, pr_ev = (
            sem("a_" + n) for n in ("nm", "yr", "yf", "tm", "or", "pm", "pe"))
        w_loaded, zeros_set = sem("a_wl"), sem("a_zs")

        with nc.Block() as block:
            @block.sync
            def _(sp):
                sp.dma_start(mask[:], A["k_mask"]).then_inc(loaded, 16)
                for b2 in range(2):
                    sp.dma_start(bp[:, b2, :], A["L1_conv_bproj"].rearrange("(a c) -> a c", a=1).to_broadcast([P, C])
                                 ).then_inc(loaded, 16)
                sp.wait_ge(zeros_set, 1)
                for part in range(PARTS):
                    rows = XD[part].rearrange("(p a b) c -> p a (b c)", p=P, b=4)
                    sp.dma_start(rows, zeros[:].unsqueeze(1).to_broadcast(rows.shape)).then_inc(zeroed, 16)
                load_weights(sp, A, "L2_ffn", WR, w_loaded)

            @block.tensor
            def _(pe):
                def kv(q):
                    if q >= 2:
                        pe.wait_ge(kv_ev, q - 1)
                    for par in range(2):
                        ins = pe.matmul(ps[:, 4 + q % 2, 0:2 * C + 1], QKf[:, q, par, 2 * C:4 * C],
                                        V[:, q, par, 0:2 * C + 1], start=(par == 0), stop=(par == 1))
                    ins.then_inc(kv_mm, 1)

                def qt(k):
                    if k >= 2:
                        pe.wait_ge(qt_ev, k - 1)
                    for u in range(4):
                        ins = pe.transpose(ps[:, 2 + k % 2, u * P:(u + 1) * P], QKf[:, 2 * k + u // 2, u % 2, 0:2 * C],
                                           K["ident"][:])
                    ins.then_inc(qt_mm, 1)

                for q in range(Q):
                    kv(q)
                    if q % 2 == 1:
                        qt(q // 2)

                def numden(q):
                    pe.wait_ge(kv_ev, q + 1)
                    pe.wait_ge(qt_ev, q // 2 + 1)
                    if q >= 2:
                        pe.wait_ge(y_ready, q - 1)
                    for par in range(2):
                        ins = pe.matmul(ps[:, q % 2, par * W:(par + 1) * W], QT[:, q, par, :], BD[:, q, :],
                                        start=True, stop=True)
                    ins.then_inc(nd_mm, 1)

                def turn(q):
                    if q == 0:
                        pe.wait_ge(qt_ev, Q // 2)
                    if q >= 2:
                        pe.wait_ge(o_ready, q - 1)
                    pe.wait_ge(yf_ready, q + 1)
                    for par in range(2):
                        ins = pe.transpose(ps[:, 2 + q % 2, par * P:(par + 1) * P], yf[:, q % 2, par], K["ident"][:])
                    ins.then_inc(t_mm, 1)

                def project(q):
                    if q >= 2:
                        pe.wait_ge(pr_ev, q - 1)
                    pe.wait_ge(o_ready, q + 1)
                    for par in range(2):
                        o = ps[:, 6 + q % 2, par * P:(par + 1) * P]
                        pe.matmul(o, Xc[:, q, par:N:2], K["ident"][:], start=True, stop=False)
                        ins = pe.matmul(o, oT[:, q % 2, par], wproj[:].rearrange("p b c -> p (b c)"),
                                        start=False, stop=True)
                    ins.then_inc(pr_mm, 1)

                for i in range(Q + 3):
                    if i < Q:
                        numden(i)
                    if 0 <= i - 2 < Q:
                        turn(i - 2)
                    if 0 <= i - 3 < Q:
                        project(i - 3)

            @block.scalar
            def _(act):
                for k in range(Q // 2):
                    act.wait_ge(qt_mm, k + 1)
                    act.copy(QT[:, 2 * k:2 * k + 2].rearrange("p a b n -> p (a b n)"), ps[:, 2 + k % 2, :]
                             ).then_inc(qt_ev, 1)
                for q in range(Q):
                    act.wait_ge(t_mm, q + 1)
                    if q >= 2:
                        act.wait_ge(pr_mm, q - 1)
                    act.copy(oT[:, q % 2].rearrange("p a n -> p (a n)"), ps[:, 2 + q % 2, 0:2 * P]).then_inc(o_ready, 1)

            @block.gpsimd
            def _(pool):
                pool.memset(zeros[:], 0.0).then_inc(zeros_set, 1)
                for q in range(Q):
                    pool.wait_ge(y_ready, q + 1)
                    if q >= 2:
                        pool.wait_ge(t_mm, q - 1)
                    pool.tensor_tensor(yf[:, q % 2], y[:, q % 2], FM[:, q], ALU.add).then_inc(yf_ready, 1)

            @block.vector
            def _(dve):
                then = counter(dve, own_v)
                dve.wait_ge(loaded, 48)
                for q in range(Q):
                    dve.wait_ge(kv_mm, q + 1)
                    dve.tensor_tensor(BD[:, q, 0:P], ps[:, 4 + q % 2, 0:P], mask[:], ALU.mult)
                    dve.tensor_tensor(BD[:, q, P:W], mask[:, 0:P:HD], ps[:, 4 + q % 2, P:P + 1].to_broadcast([P, 2 * NH]),
                                      ALU.mult).then_inc(kv_ev, 1)

                def out(q):
                    dve.wait_ge(pr_mm, q + 1)
                    dve.tensor_tensor(X[:, q], ps[:, 6 + q % 2, 0:2 * P].rearrange("p (a n) -> p a n", a=2),
                                      bp[:].rearrange("p b c -> p (b c)").unsqueeze(1).to_broadcast([P, 2, P]),
                                      ALU.add).then_inc(pr_ev, 1)

                for q in range(Q):
                    dve.wait_ge(nd_mm, q + 1)
                    nd = ps[:, q % 2, 0:2 * W].rearrange("p (a w) -> p a w", w=W)
                    then(dve.tensor_scalar(z[:, q % 2], nd[:, :, P:W], 1e-6, None, ALU.add))
                    then(dve.reciprocal(z[:, q % 2], z[:, q % 2]))
                    if q >= 2:
                        dve.wait_ge(yf_ready, q - 1)
                    dve.tensor_tensor(y[:, q % 2].rearrange("p a (h d) -> p a h d", d=HD),
                                      nd[:, :, 0:P].rearrange("p a (h d) -> p a h d", d=HD),
                                      z[:, q % 2].unsqueeze(3).to_broadcast([P, 2, 2 * NH, HD]),
                                      ALU.mult).then_inc(y_ready, 1)
                    if q >= 4:
                        out(q - 4)
                for q in range(Q - 4, Q):
                    out(q)


class LayerNorm:

    def __init__(self, nc, sem, st, tag, X, out, done, room=None):
        self.X, self.out, self.done = X, out, done
        if room:
            self.xm, self.sq = room
        else:
            self.xm = st.enter_context(nc.sbuf_tensor(tag + "xm", [P, Q, 2, 2 * C], F32))[:]
            self.sq = st.enter_context(nc.sbuf_tensor(tag + "sq", [P, 2, QG * 4 * C], F32))[:]
        self.mean = st.enter_context(nc.sbuf_tensor(tag + "s1", [P, NT], F32))
        self.var = st.enter_context(nc.sbuf_tensor(tag + "s2", [P, NT], F32))
        self.r = st.enter_context(nc.sbuf_tensor(tag + "r", [P, NT], F32))
        self.mean_done, self.centered, self.squared, self.var_done, self.sd_done = (
            sem(tag + n) for n in ("mea", "cen", "sqd", "var", "sd"))

    def flat(self, t, g):
        return t[:, g * QG:(g + 1) * QG].rearrange("p q a c -> p (q a c)")

    def rows(self, t, g):
        return self.flat(t, g).rearrange("p (r c) -> p r c", c=C)

    def cols(self, t, g):
        return t[:, g * NT // G:(g + 1) * NT // G]

    def pool(self, pool):
        for g in range(G):
            pool.wait_ge(self.mean_done, g + 1)
            pool.tensor_tensor(self.rows(self.xm, g), self.rows(self.X, g),
                               self.cols(self.mean, g).unsqueeze(2).to_broadcast([P, NT // G, C]),
                               ALU.add).then_inc(self.centered, 1)

    def square(self, act, g):
        act.wait_ge(self.centered, g + 1)
        if g >= 2:
            act.wait_ge(self.var_done, g - 1)
        act.activation(self.sq[:, g % 2], self.flat(self.xm, g), ACT.Square).then_inc(self.squared, 1)

    def root(self, act, g):
        act.wait_ge(self.var_done, g + 1)
        act.activation(self.cols(self.var, g), self.cols(self.var, g), ACT.Sqrt).then_inc(self.sd_done, 1)

    def scalar(self, act):
        for g in range(G + 1):
            if g < G:
                self.square(act, g)
            if g >= 1:
                self.root(act, g - 1)

    def sum(self, dve, then, g):
        s = self.cols(self.mean, g)
        then(dve.tensor_reduce(s, self.rows(self.X, g), AX.X, ALU.add))
        dve.tensor_scalar(s, s, -1.0 / C, None, ALU.mult).then_inc(self.mean_done, 1)

    def variance(self, dve, then, g):
        s = self.cols(self.var, g)
        dve.wait_ge(self.squared, g + 1)
        then(dve.tensor_reduce(s, self.sq[:, g % 2].rearrange("p (r c) -> p r c", c=C), AX.X, ALU.add))
        dve.tensor_scalar(s, s, 1.0 / C, 1e-5, ALU.mult, ALU.add).then_inc(self.var_done, 1)

    def normalize(self, dve, then, g):
        dve.wait_ge(self.sd_done, g + 1)
        then(dve.reciprocal(self.cols(self.r, g), self.cols(self.var, g)))
        for o, i, r in self.out(g):
            ins = dve.tensor_tensor(o, i, r, ALU.mult)
        ins.then_inc(self.done, 1)

    def vector(self, dve, then):
        for g in range(G + 3):
            if g < G:
                self.sum(dve, then, g)
            if 0 <= g - 2 < G:
                self.variance(dve, then, g - 2)
            if 0 <= g - 3 < G:
                self.normalize(dve, then, g - 3)


def load_weights(sp, A, L, WR, loaded):
    for k in range(2):
        for n, w in enumerate(("_w1", "_w2")):
            sp.dma_start(WR[k * C:(k + 1) * C, :, n * HID:(n + 1) * HID], A[L + w].rearrange("e d h -> d e h")
                         ).then_inc(loaded, 16)
    sp.dma_start(WR[:, :, 2 * HID:WC], A[L + "_w3"].rearrange("e h o -> h e o")).then_inc(loaded, 16)
    sp.wait_ge(loaded, 80)


def plain_norm_out(ln_of, xn):
    def out(g):
        ln, k = ln_of(), NT // G
        return [(ln.rows(ln.xm if xn is None else xn, g), ln.rows(ln.xm, g), ln.r[:, g * k:(g + 1) * k].unsqueeze(2).to_broadcast([P, k, C]))]
    return out


def stage_pool(nc, sem, A, K, X):
    with ExitStack() as st:
        def sb(name, shape, dt=F32):
            return st.enter_context(nc.sbuf_tensor(name, shape, dt))
        ps = st.enter_context(nc.psum_tensor("p_ps", [P, 8, BANK], F32))
        H = sb("p_h", [P, Q, 2, 2 * C])
        HT = sb("p_ht", [P, Q * 2, P])
        QT = sb("p_qt", [P, Q * 2, P])
        AE = sb("p_ae", [P, 2, C * B])
        BH = sb("p_bh", [P, 2, C * B])
        wf = sb("p_wf", [C, 2, C])
        wbd = sb("p_wbd", [P, 2, C])
        fb = sb("p_fb", [P, 1])
        sw = sb("p_sw", [P, 2])
        e = sb("p_e", [P, 2, B])
        m = sb("p_m", [P, 2, B + 1])
        dd = sb("p_d", [P, 2, 2, B])
        ex = sb("p_ex", [P, 2, 2, B])
        s = sb("p_s", [P, 2, B + 1])
        rs = sb("p_rs", [P, 2, B])
        co = sb("p_co", [P, 2, 2, B])
        loaded, own_v, zeroed = sem("p_loaded"), sem("p_own"), sem("p_zero")
        normed, ht_mm, ht_ev, w_mm, w_ev, fc_mm, tanh_done, e_mm = (
            sem("p_" + n) for n in ("normed", "htm", "hte", "wm", "we", "fc", "tanh", "em"))
        exp_in, exp_out, a_ready, spread = (sem("p_" + n) for n in ("xi", "xo", "ar", "sp"))
        ln = LayerNorm(nc, sem, st, "p_", X, plain_norm_out(lambda: ln, H), normed)

        def by_batch(t, par):
            return t[:, :, par, :].rearrange("p q (b c) -> p c q b", b=2)

        with nc.Block() as block:
            @block.sync
            def _(sp):
                for k in range(2):
                    sp.dma_start(wf[:, k, :], A["L2_attn_fc_w"]).then_inc(loaded, 16)
                    sp.dma_start(fb[k * C:(k + 1) * C, :], A["L2_attn_fc_b"].rearrange("(c a) -> c a", a=1)
                                 ).then_inc(loaded, 16)
                sp.wait_ge(zeroed, 1)
                for k in range(2):
                    sp.dma_start(sw[k * C:(k + 1) * C, k:k + 1], A["L2_attn_score_w"].rearrange("(c a) -> c a", a=1)
                                 ).then_inc(loaded, 16)

            @block.gpsimd
            def _(pool):
                pool.memset(sw[:], 0.0).then_inc(zeroed, 1)
                pool.memset(wbd[:], 0.0).then_inc(zeroed, 1)
                ln.pool(pool)

            @block.tensor
            def _(pe):
                pe.wait_ge(loaded, 96)
                pe.transpose(ps[:, 7, 0:C], wf[:].rearrange("p a c -> p (a c)"), K["ident"][0:C, 0:C]).then_inc(w_mm, 1)
                for k in range(Q // 2):
                    pe.wait_ge(normed, k * 2 // QG + 1)
                    if k >= 2:
                        pe.wait_ge(ht_ev, k - 1)
                    for u in range(4):
                        ins = pe.transpose(ps[:, k % 2, u * P:(u + 1) * P], H[:, 2 * k + u // 2, u % 2, :], K["ident"][:])
                    ins.then_inc(ht_mm, 1)
                pe.wait_ge(w_ev, 2)
                for k in range(Q // 2):
                    pe.wait_ge(ht_ev, k + 1)
                    if k >= 2:
                        pe.wait_ge(tanh_done, k - 1)
                    pe.matmul(ps[:, 2 + k % 2, :], wbd[:].rearrange("p b c -> p (b c)"),
                              HT[:, 4 * k:4 * k + 4].rearrange("p a n -> p (a n)"), start=True, stop=True
                              ).then_inc(fc_mm, 1)
                for k in range(2 * Q):
                    pe.wait_ge(tanh_done, k // 4 + 1)
                    ins = pe.matmul(ps[:, 4, 2 * k:2 * k + 2], QT[:, k, :], sw[:], start=True, stop=True)
                ins.then_inc(e_mm, 1)

            @block.scalar
            def _(act):
                ln.scalar(act)
                for k in range(Q // 2):
                    act.wait_ge(ht_mm, k + 1)
                    act.copy(HT[:, 4 * k:4 * k + 4].rearrange("p a n -> p (a n)"), ps[:, k % 2, :]).then_inc(ht_ev, 1)
                for k in range(Q // 2):
                    act.wait_ge(fc_mm, k + 1)
                    act.activation(QT[:, 4 * k:4 * k + 4].rearrange("p a n -> p (a n)"), ps[:, 2 + k % 2, :],
                                   ACT.Tanh, bias=fb[:]).then_inc(tanh_done, 1)
                act.wait_ge(exp_in, 2)
                act.activation(ex[:], dd[:], ACT.Exp).then_inc(exp_out, 1)
                act.wait_ge(a_ready, 1)
                for par in range(2):
                    act.copy(AE[:, par].rearrange("p (c b) -> p c b", b=B),
                             co[:, par, 0:1, :].to_broadcast([P, C, B])).then_inc(spread, 1)

            @block.vector
            def _(dve):
                then = counter(dve, own_v)
                ln.vector(dve, then)
                dve.wait_ge(w_mm, 1)
                dve.wait_ge(zeroed, 2)
                for b2 in range(2):
                    rows = slice(b2 * C, b2 * C + C)
                    dve.tensor_copy(wbd[rows, b2, :], ps[rows, 7, 0:C]).then_inc(w_ev, 1)
                dve.memset(m[:, :, 0:1], -3e38)
                dve.memset(s[:, :, 0:1], 0.0)
                dve.wait_ge(e_mm, 1)
                then(dve.tensor_copy(e[:].rearrange("p a (q b) -> p a q b", b=2),
                                     ps[:, 4, 0:NT].rearrange("p (q a b) -> p a q b", a=2, b=2)))
                for par in range(2):
                    ins = dve.tensor_tensor_scan(m[:, par, 1:B + 1], e[:, par], e[:, par], -3e38, ALU.max, ALU.max)
                then(ins)
                dve.tensor_tensor(dd[:, :, 0, :], m[:, :, 0:B], m[:, :, 1:B + 1], ALU.subtract).then_inc(exp_in, 1)
                dve.tensor_tensor(dd[:, :, 1, :], e[:], m[:, :, 1:B + 1], ALU.subtract).then_inc(exp_in, 1)
                dve.wait_ge(exp_out, 1)
                for par in range(2):
                    ins = dve.tensor_tensor_scan(s[:, par, 1:B + 1], ex[:, par, 0], ex[:, par, 1], 0.0,
                                                 ALU.mult, ALU.add)
                then(ins)
                then(dve.reciprocal(rs[:], s[:, :, 1:B + 1]))
                dve.tensor_tensor(co[:, :, 1, :], ex[:, :, 1, :], rs[:], ALU.mult)
                then(dve.tensor_tensor(co[:, :, 0, :], ex[:, :, 0, :], rs[:], ALU.mult))
                dve.tensor_tensor(co[:, :, 0, :], co[:, :, 0, :], s[:, :, 0:B], ALU.mult).then_inc(a_ready, 1)
                for par in range(2):
                    cb = co[:, par, 1, :].rearrange("p (q b) -> p q b", b=2).unsqueeze(1).to_broadcast([P, C, Q, 2])
                    ins = dve.tensor_tensor(BH[:, par].rearrange("p (c q b) -> p c q b", q=Q, b=2),
                                            by_batch(H, par), cb, ALU.mult)
                then(ins)
                for par in range(2):
                    dve.wait_ge(spread, par + 1)
                    ins = dve.tensor_tensor_scan(BH[:, par], AE[:, par], BH[:, par], 0.0, ALU.mult, ALU.add)
                then(ins)
                for par in range(2):
                    dve.tensor_tensor(by_batch(X, par), by_batch(X, par),
                                      BH[:, par].rearrange("p (c q b) -> p c q b", q=Q, b=2), ALU.add)


BS = 512
PARTS = 2
TH = NT // PARTS
NBLK = 2 * TH * P // BS + E - 1
WC = 2 * HID + C


class Mixture:

    def __init__(self, nc, sem, st, A, K, X, L, WR, XD, YD):
        def sb(name, shape, dt=F32):
            return st.enter_context(nc.sbuf_tensor(L + name, shape, dt))

        self.nc, self.A, self.K, self.X, self.L, self.WR, self.XD, self.YD = nc, A, K, X, L, WR, XD, YD
        self.ps = st.enter_context(nc.psum_tensor(L + "ps", [P, 8, BANK], F32))
        self.HL = sb("hl", [P, NT, 2, C])
        self.XS = sb("xs", [P, 4, 4 * P])
        self.gw, self.gb = sb("gw", [P, E]), sb("gb", [P, E])
        self.lg, self.key, self.one1 = sb("lg", [P, TH, E]), sb("key", [P, TH, E]), sb("one1", [P, TH, E])
        self.mx = sb("mx", [P, PARTS, 6, TH])
        self.tot, self.cum, self.off = sb("tot", [P, E, TH]), sb("cum", [P, E, TH]), sb("off", [P, E, TH])
        self.nbk = sb("nbk", [P, E, TH * P // BS])
        self.blk = sb("blk", [P, 4, E])
        self.own = sb("own", [P, NBLK, E])
        self.ownf = sb("ownf", [P, NBLK])
        self.slotf = sb("slotf", [P, TH])
        self.owner = sb("owner", [P, PARTS, NBLK], mybir.dt.int32)
        self.slot = sb("slot", [P, PARTS, 2, TH], mybir.dt.int32)
        self.xb = sb("xb", [P, 4, 4, P])
        self.xt = sb("xt", [P, 2, BS], F32R)
        self.wb = sb("wb", [P, 4, WC])
        self.wr = sb("wr", [P, 4, 2, WC], F32R)
        self.gate = sb("gate", [P, 2, BS])
        self.hid = sb("hid", [P, 2, BS])
        self.hh = sb("hh", [P, 2, BS], F32R)
        self.hlo = sb("hlo", [P, 2, BS], F32R)
        self.yb = sb("yb", [P, 4, 4 * C])
        self.GY = sb("gy", [P, 2, NT, C])

        def sems(*names):
            return [sem(L + n) for n in names]
        self.g_loaded, self.own_v, self.normed = sems("gl", "ov", "nm")
        self.hi, self.lo, self.tr_mm, self.tr_ev, self.lg_mm, self.exp_in, self.exp_out = sems(
            "hi", "lo", "tm", "te", "lm", "xi", "xo")
        self.counted, self.ranked, self.owned, self.slotted = sems("cn", "rk", "ow", "sl")
        self.scattered = sems(*(f"sc{h}" for h in range(PARTS)))
        self.x_in, self.w_in, self.stored = (sems(*(f"{n}{j}" for j in range(4))) for n in ("xl", "wl", "ys"))
        self.turned, self.xt_out, self.up1, self.up2, self.down = sems("bt", "bx", "b1", "b2", "bd")
        self.w_hi, self.w_lo, self.silu, self.prod, self.h_hi, self.h_lo, self.y_out = sems(
            "wh", "wo", "si", "pr", "hh_", "ho", "yo")
        self.gathered = sems(*(f"ga{j}" for j in range(PARTS * 4)))
        self.ln = LayerNorm(nc, sem, st, L, X, plain_norm_out(lambda: self.ln, None), self.normed)

    def free(self, eng, sem, part, n, depth):
        if isinstance(n, int) and n < depth:
            if part:
                eng.wait_ge(sem, part * NBLK)
        else:
            eng.wait_ge(sem, part * NBLK + n - depth + 1)

    def steps(self, eng, body):
        for n in range(8):
            body(n, n % 4, n // 4)
        last = (NBLK - 3) // 4
        with eng.Fori(2, last) as i:
            for j in range(4):
                body(i * 4 + j, j, i)
        for n in range(4 * last, NBLK):
            body(n, n % 4, n // 4)

    def filled(self, part, j, i):
        return 16 * (part * ((NBLK + 3 - j % 4) // 4) + i + j // 4 + 1)

    def sync(self, sp):
        for k in range(2):
            sp.dma_start(self.gw[k * C:(k + 1) * C, :], self.A[self.L + "_gate_w"]).then_inc(self.g_loaded, 16)
        sp.dma_start(self.gb[:], self.A[self.L + "_gate_b"].rearrange("(a c) -> a c", a=1).to_broadcast([P, E])
                     ).then_inc(self.g_loaded, 16)
        for part in range(PARTS):
            def fetch(n, j, i):
                self.free(sp, self.turned, part, n, 4)
                rows = self.XD[part].rearrange("(b p s) c -> b p (s c)", p=P, s=4)
                sp.dma_start(self.xb[:, j].rearrange("p s c -> p (s c)"),
                             rows[bass.ds(n, 1)].rearrange("b p c -> p (b c)")).then_inc(self.x_in[j], 16)
                self.free(sp, self.w_lo, part, n, 4)
                e = sp.value_load(self.owner[0:1, part, bass.ds(n, 1)], min_val=0, max_val=E - 1)
                sp.dma_start(self.wb[:, j:j + 1], self.WR[:, bass.ds(e, 1)]).then_inc(self.w_in[j], 16)
            sp.wait_ge(self.owned, part + 1)
            sp.wait_ge(self.scattered[part], 16 * 2 * TH)
            self.steps(sp, fetch)

    def pool(self, pool, zeroed):
        self.ln.pool(pool)
        pool.wait_ge(*zeroed)
        for part in range(PARTS):
            pool.wait_ge(self.slotted, 2 * part + 2)
            for t in range(TH):
                for k in range(2):
                    pool.indirect_dma_start(self.XD[part], bass.IndirectOffsetOnAxis(self.slot[:, part, k, t:t + 1], 0),
                                            self.HL[:, part * TH + t].rearrange("p a c -> p (a c)"), None
                                            ).then_inc(self.scattered[part], 16)
        for part in range(PARTS):
            for j in range(4):
                pool.wait_ge(self.stored[j], 16 * (part + 1) * ((NBLK + 3 - j) // 4))
            for t in range(TH):
                for k in range(2):
                    pool.indirect_dma_start(self.GY[:, k, part * TH + t], None, self.YD[part],
                                            bass.IndirectOffsetOnAxis(self.slot[:, part, k, t:t + 1], 0)
                                            ).then_inc(self.gathered[part * 4 + t // (TH // 4)], 16)

    def tensor(self, pe):
        ps, K = self.ps, self.K
        TG, KG = NT // G, NT // G // 4
        pe.wait_ge(self.g_loaded, 48)
        for g in range(G):
            pe.wait_ge(self.lo, g + 1)
            for k in range(g * KG, (g + 1) * KG):
                if k >= 2:
                    pe.wait_ge(self.tr_ev, k - 1)
                for u in range(4):
                    ins = pe.transpose(ps[:, k % 2, u * P:(u + 1) * P],
                                       self.HL[:, 4 * k + u].rearrange("p a c -> p (a c)"), K["ident"][:])
                ins.then_inc(self.tr_mm, 1)
            for t in range(g * TG, (g + 1) * TG):
                pe.wait_ge(self.tr_ev, t // 4 + 1)
                ins = pe.matmul(ps[:, 2 + t // TH, (t % TH) * E:(t % TH) * E + E],
                                self.XS[:, t // 4 % 4, t % 4 * P:(t % 4 + 1) * P], self.gw[:], start=True, stop=True)
                if t % 4 == 3:
                    ins.then_inc(self.lg_mm, 1)
        for part in range(PARTS):
            pe.wait_ge(self.counted, part + 1)
            if part:
                pe.wait_ge(self.slotted, 2 * part)
            m = self.tot[:].rearrange("p e t -> p (e t)")
            pe.matmul(ps[:, 4, :], K["upper"][:], m, start=True, stop=True)
            pe.matmul(ps[:, 5, :], K["ones"][:], m, start=True, stop=True).then_inc(self.ranked, 1)
        pe.wait_ge(self.slotted, 2 * PARTS)
        for part in range(PARTS):
            def turn(n, j, i):
                self.free(pe, self.xt_out, part, n, 2)
                pe.wait_ge(self.x_in[j % 4], self.filled(part, j, i))
                for s in range(4):
                    ins = pe.transpose(ps[:, j % 2, s * P:(s + 1) * P], self.xb[:, j % 4, s], K["ident"][:])
                ins.then_inc(self.turned, 1)

            def up(n, j):
                count = part * NBLK + n + 1
                pe.wait_ge(self.xt_out, count)
                pe.wait_ge(self.w_lo, count)
                self.free(pe, self.silu, part, n, 2)
                x = self.xt[:, j % 2]
                for bank, c0, done in ((2, 0, self.up1), (4, HID, self.up2)):
                    if bank == 4:
                        self.free(pe, self.prod, part, n, 2)
                    o = ps[:, bank + j % 2]
                    pe.matmul(o, self.wr[:, j % 4, 0, c0:c0 + HID], x, start=True, stop=False)
                    pe.matmul(o, self.wr[:, j % 4, 1, c0:c0 + HID], x, start=False, stop=True).then_inc(done, 1)

            def down(n, j):
                self.free(pe, self.y_out, part, n, 2)
                pe.wait_ge(self.h_lo, part * NBLK + n + 1)
                for s in range(4):
                    o = ps[:, 6 + j % 2, s * P:(s + 1) * P].rearrange("p (a c) -> p a c", a=2)
                    for k, h in enumerate((self.hh, self.hlo)):
                        ins = pe.matmul(o, h[:, j % 2, s * P:(s + 1) * P], self.wr[:, j % 4, :, 2 * HID:WC],
                                        start=(k == 0), stop=(k == 1))
                ins.then_inc(self.down, 1)

            def step(n, j, i):
                if not isinstance(n, int) or n + 3 < NBLK:
                    turn(n + 3, j + 3, i)
                if not isinstance(n, int) or n + 2 < NBLK:
                    up(n + 2, j + 2)
                down(n, j)
            for n in range(3):
                turn(n, n, 0)
            for n in range(2):
                up(n, n)
            self.steps(pe, step)

    def scalar(self, act):
        ln, ps = self.ln, self.ps
        KG = NT // G // 4

        def high(g):
            act.wait_ge(self.normed, g + 1)
            act.copy(self.HL[:, g * 4 * KG:(g + 1) * 4 * KG, 0, :].bitcast(F32R), ln.rows(ln.xm, g)).then_inc(self.hi, 1)

        def channel_major(g):
            for k in range(g * KG, (g + 1) * KG):
                act.wait_ge(self.tr_mm, k + 1)
                if k >= 4:
                    act.wait_ge(self.lg_mm, k - 3)
                act.copy(self.XS[:, k % 4], ps[:, k % 2, :]).then_inc(self.tr_ev, 1)

        for g in range(G + 2):
            if g < G:
                ln.square(act, g)
            if 0 <= g - 1 < G:
                ln.root(act, g - 1)
            if 0 <= g - 2 < G:
                high(g - 2)
            if 0 <= g - 3 < G:
                channel_major(g - 3)
        channel_major(G - 1)
        for part in range(PARTS):
            act.wait_ge(self.exp_in, part + 1)
            act.activation(self.mx[:, part, 3], self.mx[:, part, 2], ACT.Exp).then_inc(self.exp_out, 1)
        for part in range(PARTS):
            def weights(n, j, i):
                act.wait_ge(self.w_in[j % 4], self.filled(part, j, i))
                self.free(act, self.down, part, n, 4)
                act.copy(self.wr[:, j % 4, 0], self.wb[:, j % 4]).then_inc(self.w_hi, 1)

            def tokens(n, j):
                act.wait_ge(self.turned, part * NBLK + n + 1)
                self.free(act, self.up2, part, n, 2)
                act.copy(self.xt[:, j % 2], ps[:, j % 2, :]).then_inc(self.xt_out, 1)

            def silu(n, j):
                act.wait_ge(self.up1, part * NBLK + n + 1)
                self.free(act, self.prod, part, n, 2)
                act.activation(self.gate[:, j % 2], ps[:, 2 + j % 2, :], ACT.Silu).then_inc(self.silu, 1)

            def halve(n, j):
                act.wait_ge(self.prod, part * NBLK + n + 1)
                self.free(act, self.down, part, n, 2)
                act.copy(self.hh[:, j % 2], self.hid[:, j % 2]).then_inc(self.h_hi, 1)

            def store(n, j):
                act.wait_ge(self.y_out, part * NBLK + n + 1)
                rows = self.YD[part].rearrange("(b p s) c -> b p (s c)", p=P, s=4)
                act.dma_start(rows[bass.ds(n, 1)].rearrange("b p c -> p (b c)"), self.yb[:, j % 4]).then_inc(self.stored[j % 4], 16)

            def step(n, j, i):
                peeled = isinstance(n, int)
                if not peeled or n + 3 < NBLK:
                    weights(n + 3, j + 3, i)
                    tokens(n + 3, j + 3)
                if not peeled or n + 2 < NBLK:
                    silu(n + 2, j + 2)
                if not peeled or n + 1 < NBLK:
                    halve(n + 1, j + 1)
                if not peeled or n >= 1:
                    store(n - 1, j + 3)
            for n in range(3):
                weights(n, n, 0)
                tokens(n, n)
            for n in range(2):
                silu(n, n)
            halve(0, 0)
            self.steps(act, step)
            store(NBLK - 1, (NBLK - 1) % 4)

    def vector(self, dve):
        nc, ln, ps, K, mx = self.nc, self.ln, self.ps, self.K, self.mx
        then = counter(dve, self.own_v)
        full = [P, TH, E]
        lg, key, one1, blk = self.lg, self.key, self.one1, self.blk
        iota = K["iota"][:, 0:E].unsqueeze(1).to_broadcast(full)
        TG = NT // G

        def low(g):
            dve.wait_ge(self.hi, g + 1)
            hl = self.HL[:, g * TG:(g + 1) * TG]
            dve.tensor_tensor(hl[:, :, 1, :], ln.rows(ln.xm, g), hl[:, :, 0, :], ALU.subtract).then_inc(self.lo, 1)

        def by_tile(t):
            return t.rearrange("p e t -> p t e")

        def route(part):
            m = mx[:, part]

            def wide(k):
                return m[:, k].unsqueeze(2).to_broadcast(full)
            dve.wait_ge(self.lg_mm, (part + 1) * TH // 4)
            then(dve.tensor_tensor(lg[:], ps[:, 2 + part, :].rearrange("p (t e) -> p t e", e=E),
                                   self.gb[:].unsqueeze(1).to_broadcast(full), ALU.add))
            for k, one in ((0, one1), (1, key)):
                then(dve.tensor_reduce(m[:, k], lg[:], AX.X, ALU.max))
                then(dve.tensor_tensor(key[:], lg[:], wide(k), ALU.is_equal))
                then(dve.scalar_tensor_tensor(out=key[:], in0=key[:], scalar=-64.0, in1=iota,
                                              op0=ALU.mult, op1=ALU.add))
                then(dve.tensor_reduce(m[:, 5], key[:], AX.X, ALU.min))
                if k == 1:
                    dve.tensor_tensor(m[:, 2], m[:, 1], m[:, 0], ALU.subtract).then_inc(self.exp_in, 1)
                then(dve.tensor_tensor(one[:], key[:], wide(5), ALU.is_equal))
                if k == 0:
                    then(dve.scalar_tensor_tensor(out=lg[:], in0=one1[:], scalar=-BIG, in1=lg[:],
                                                  op0=ALU.mult, op1=ALU.add))
            dve.tensor_tensor(by_tile(self.tot[:]), one1[:], key[:], ALU.add).then_inc(self.counted, 1)
            dve.wait_ge(self.exp_out, part + 1)
            then(dve.tensor_scalar(m[:, 4], m[:, 3], 1.0, None, ALU.add))
            then(dve.reciprocal(m[:, 4], m[:, 4]))
            then(dve.tensor_tensor(m[:, 5], m[:, 3], m[:, 4], ALU.mult))
            dve.wait_ge(self.ranked, part + 1)
            flat = "p e t -> p (e t)"
            then(dve.tensor_copy(self.off[:].rearrange(flat), ps[:, 5, :]))
            then(dve.tensor_tensor_scan(self.cum[:].rearrange(flat), K["reset"][:], self.off[:].rearrange(flat), 0.0,
                                        ALU.mult, ALU.add))
            n_e = self.cum[:, :, TH - 1:TH]
            nb = self.nbk.shape[2]
            then(dve.tensor_tensor(self.nbk[:], n_e.to_broadcast([P, E, nb]),
                                   K["fill"][:, 0:nb].unsqueeze(1).to_broadcast([P, E, nb]), ALU.is_gt))
            then(dve.tensor_reduce(blk[:, 0], self.nbk[:], AX.X, ALU.add))
            then(dve.tensor_tensor_scan(blk[:, 1], K["ones"][:, 0:E], blk[:, 0], 0.0, ALU.mult, ALU.add))
            then(dve.tensor_tensor(blk[:, 2], blk[:, 1], blk[:, 0], ALU.subtract))
            then(dve.tensor_scalar(blk[:, 3], blk[:, 2], float(BS), None, ALU.mult))
            wide_b = [P, NBLK, E]
            then(dve.tensor_tensor(self.own[:], blk[:, 1].unsqueeze(1).to_broadcast(wide_b),
                                   K["iota"][:, 0:NBLK].unsqueeze(2).to_broadcast(wide_b), ALU.is_le))
            then(dve.tensor_reduce(self.ownf[:], self.own[:], AX.X, ALU.add))
            then(dve.tensor_scalar(self.ownf[:], self.ownf[:], float(E - 1), None, ALU.min))
            dve.tensor_copy(self.owner[:, part], self.ownf[:]).then_inc(self.owned, 1)
            then(dve.tensor_tensor(self.off[:], self.cum[:], self.off[:], ALU.subtract))
            then(dve.tensor_tensor(self.off[:], self.off[:], blk[:, 3].unsqueeze(2).to_broadcast([P, E, TH]), ALU.add))
            then(dve.tensor_tensor(self.off[:].rearrange(flat), self.off[:].rearrange(flat), ps[:, 4, :], ALU.add))
            for k, one in ((0, one1), (1, key)):
                then(dve.tensor_tensor(lg[:], one[:], by_tile(self.off[:]), ALU.mult))
                then(dve.tensor_reduce(self.slotf[:], lg[:], AX.X, ALU.add))
                dve.tensor_copy(self.slot[:, part, k], self.slotf[:]).then_inc(self.slotted, 1)
                dve.wait_ge(self.slotted, 2 * part + k + 1)

        for g in range(G + 4):
            if g < G:
                ln.sum(dve, then, g)
            if 0 <= g - 1 < G:
                ln.variance(dve, then, g - 1)
            if 0 <= g - 3 < G:
                low(g - 3)
            if 0 <= g - 2 < G:
                ln.normalize(dve, then, g - 2)
            if g == 6:
                route(0)
        for part in range(1, PARTS):
            route(part)

        for part in range(PARTS):
            def weights(n, j):
                dve.wait_ge(self.w_hi, part * NBLK + n + 1)
                dve.tensor_tensor(self.wr[:, j % 4, 1], self.wb[:, j % 4], self.wr[:, j % 4, 0].bitcast(F32),
                                  ALU.subtract).then_inc(self.w_lo, 1)

            def product(n, j):
                dve.wait_ge(self.silu, part * NBLK + n + 1)
                dve.wait_ge(self.up2, part * NBLK + n + 1)
                self.free(dve, self.h_lo, part, n, 2)
                dve.tensor_tensor(self.hid[:, j % 2], self.gate[:, j % 2], ps[:, 4 + j % 2, :], ALU.mult
                                  ).then_inc(self.prod, 1)

            def rest(n, j):
                dve.wait_ge(self.h_hi, part * NBLK + n + 1)
                dve.tensor_tensor(self.hlo[:, j % 2], self.hid[:, j % 2], self.hh[:, j % 2].bitcast(F32),
                                  ALU.subtract).then_inc(self.h_lo, 1)

            def result(n, j, i):
                dve.wait_ge(self.down, part * NBLK + n + 1)
                if not isinstance(n, int) or n >= 4:
                    dve.wait_ge(self.stored[j % 4], self.filled(part, j, i) - 16)
                elif part:
                    dve.wait_ge(self.stored[j % 4], 16 * ((NBLK + 3 - j) // 4))
                y = ps[:, 6 + j % 2, :].rearrange("p (s a c) -> p s c a", s=4, a=2)
                dve.tensor_reduce(self.yb[:, j % 4].rearrange("p (s c) -> p s c", c=C), y, AX.X, ALU.add
                                  ).then_inc(self.y_out, 1)

            def step(n, j, i):
                peeled = isinstance(n, int)
                if peeled and n >= 1:
                    result(n - 1, (j + 3) % 4, (n - 1) // 4)
                if not peeled:
                    result(n - 1, (j + 3) % 4, i if j else i - 1)
                if not peeled or n + 3 < NBLK:
                    weights(n + 3, j + 3)
                if not peeled or n + 2 < NBLK:
                    product(n + 2, j + 2)
                if not peeled or n + 1 < NBLK:
                    rest(n + 1, j + 1)
            for n in range(3):
                weights(n, n)
            for n in range(2):
                product(n, n)
            rest(0, 0)
            self.steps(dve, step)
            result(NBLK - 1, (NBLK - 1) % 4, (NBLK - 1) // 4)

        TQ = TH // 4
        for part in range(PARTS):
            for j in range(4):
                dve.wait_ge(self.gathered[part * 4 + j], 16 * 2 * TQ)
                t0 = part * TH + j * TQ
                x = self.X[:].rearrange("p q a (b c) -> p (q a b) c", b=2)[:, t0:t0 + TQ]
                for k in range(2):
                    y = self.GY[:, k, t0:t0 + TQ]
                    share = mx[:, part, 4 + k, j * TQ:(j + 1) * TQ].unsqueeze(2).to_broadcast([P, TQ, C])
                    then(dve.tensor_tensor(y, y, share, ALU.mult))
                    then(dve.tensor_tensor(x, x, y, ALU.add))


def stage_mixture(nc, sem, A, K, X, L, WR, XD, YD, zeroed):
    with ExitStack() as st:
        mix = Mixture(nc, sem, st, A, K, X, L, WR, XD, YD)
        with nc.Block() as block:
            @block.sync
            def _(sp):
                mix.sync(sp)

            @block.gpsimd
            def _(pool):
                mix.pool(pool, zeroed)

            @block.tensor
            def _(pe):
                mix.tensor(pe)

            @block.scalar
            def _(act):
                mix.scalar(act)

            @block.vector
            def _(dve):
                mix.vector(dve)


def stage_linear(nc, sem, A, K, X, WR):
    SCALE = 1.0 / 8.0
    BC = 4
    NC3 = B // BC
    with ExitStack() as st:
        def sb(name, shape, dt=F32):
            return st.enter_context(nc.sbuf_tensor("l_" + name, shape, dt))
        ps = st.enter_context(nc.psum_tensor("l_ps", [P, 8, BANK], F32))
        xn = sb("xn", [P, B, 2, C])
        xT = sb("xT", [P, B, P])
        sx = sb("sx", [P, B])
        wraw = sb("wraw", [P, 2 * H3, C])
        wv = sb("wv", [P, H3, 2, C])
        praw = sb("praw", [P, 4, C])
        wq = sb("wq", [P, H3, 2, C])
        pw = sb("pw", [P, 4, 2, C], F32R)
        pbias = sb("pbias", [P, 1])
        bq = sb("bq", [P, H3])
        bv = sb("bv", [P, H3])
        lb = sb("lb", [P, 32])
        ls = sb("ls", [P, 1])
        gain = sb("gain", [P, H3, B])
        vg = sb("vg", [P, 4, BC * P])
        vh = sb("vh", [P, 2, H3, BC * P], F32R)
        vl = sb("vl", [P, 2, H3, BC * P], F32R)
        oT = sb("oT", [P, 2, BC, 2, H3, 16])
        loaded, own_v, own_p, normed, zeroed, w_ready = (sem("l_" + n) for n in ("ld", "ov", "op", "nm", "z", "wr"))
        xt_mm, xt_ev, g_mm, g_ready, sx_ready = (sem("l_" + n) for n in ("xm", "xe", "gm", "gr", "sx"))
        v_mm, v_ev, vh_done, vl_done, o_mm, o_ev, t_mm, t_ev = (
            sem("l_" + n) for n in ("vm", "ve", "vh", "vl", "om", "oe", "tm", "te"))
        w_loaded = sem("l_wl")

        def out(g):
            k = NT // G
            pairs = []
            for par in range(2):
                src = ln.xm[:, g * QG:(g + 1) * QG, par, :].rearrange("p q (b c) -> p q b c", b=2)
                dst = xn[:, g * 2 * QG:(g + 1) * 2 * QG, par, :].rearrange("p (q b) c -> p q b c", b=2)
                r = ln.r[:, g * k:(g + 1) * k].rearrange("p (q a b) -> p q a b", a=2, b=2)[:, :, par, :]
                pairs.append((dst, src, r.unsqueeze(3).to_broadcast([P, QG, 2, C])))
            return pairs
        ln = LayerNorm(nc, sem, st, "l_", X, out, normed,
                       room=(xT[:].rearrange("p b n -> p (b n)").rearrange("p (q a c) -> p q a c", q=Q, a=2),
                             oT[:].rearrange("p g b a h m -> p g (b a h m)")))

        with nc.Block() as block:
            @block.sync
            def _(sp):
                for k in range(2):
                    rows = slice(k * C, (k + 1) * C)
                    sp.dma_start(wraw[rows].rearrange("p a c -> p (a c)"), A["L3_attn_qkv_w"]).then_inc(loaded, 16)
                    bias = A["L3_attn_qkv_b"].rearrange("(s h d) -> s d h", s=2, d=C)
                    sp.dma_start(bq[rows], bias[0], allow_slow_non_contiguous=True).then_inc(loaded, 16)
                    sp.dma_start(bv[rows], bias[1], allow_slow_non_contiguous=True).then_inc(loaded, 16)
                    sp.dma_start(lb[rows], A["L3_attn_lunchbox"]).then_inc(loaded, 16)
                sp.dma_start(praw[:], A["L3_attn_proj_w"].rearrange("(j p) o -> p j o", p=P)).then_inc(loaded, 16)
                sp.wait_ge(zeroed, 1)
                sp.dma_start(pbias[0:C], A["L3_attn_proj_b"].rearrange("(o a) -> o a", a=1)).then_inc(loaded, 16)
                load_weights(sp, A, "L3_ffn", WR, w_loaded)

            @block.gpsimd
            def _(pool):
                then = counter(pool, own_p)
                pool.memset(pbias[:], 0.0).then_inc(zeroed, 1)
                ln.pool(pool)
                then(pool.memset(wv[:], 0.0))
                pool.wait_ge(loaded, 160)
                for k in range(2):
                    rows = slice(k * C, (k + 1) * C)
                    pool.tensor_copy(wv[rows, :, k, :], wraw[rows, H3:2 * H3, :]).then_inc(w_ready, 1)
                pool.wait_ge(w_ready, 2)
                pool.tensor_copy(wq[:], wraw[:, 0:H3, :].unsqueeze(2).to_broadcast([P, H3, 2, C])).then_inc(w_ready, 1)
                then(pool.tensor_copy(pw[:, :, 0, :], praw[:]))
                pool.tensor_tensor(pw[:, :, 1, :], praw[:], pw[:, :, 0, :].bitcast(F32), ALU.subtract).then_inc(w_ready, 1)
                for k in range(NC3):
                    for h in range(H3):
                        n = k * H3 + h
                        pool.wait_ge(vh_done, n + 1)
                        pool.tensor_tensor(vl[:, k % 2, h], vg[:, n % 4], vh[:, k % 2, h].bitcast(F32),
                                           ALU.subtract).then_inc(vl_done, 1)

            @block.tensor
            def _(pe):
                for k in range(NC3):
                    pe.wait_ge(normed, k // 2 + 1)
                    if k >= 2:
                        pe.wait_ge(xt_ev, k - 1)
                    for u in range(4):
                        ins = pe.transpose(ps[:, k % 2, u * P:(u + 1) * P],
                                           xn[:, 4 * k + u].rearrange("p a c -> p (a c)"), K["ident"][:])
                    ins.then_inc(xt_mm, 1)
                pe.wait_ge(w_ready, 4)
                pe.wait_ge(sx_ready, 1)
                for h in range(H3):
                    ins = pe.matmul(ps[:, 2, h * B:(h + 1) * B], wq[:, h].rearrange("p a c -> p (a c)"), sx[:],
                                    start=True, stop=True)
                ins.then_inc(g_mm, 1)

                def values(k):
                    for h in range(H3):
                        n = k * H3 + h
                        if n >= 2:
                            pe.wait_ge(v_ev, n - 1)
                        else:
                            pe.wait_ge(xt_ev, NC3)
                        pe.matmul(ps[:, n % 2, :], wv[:, h].rearrange("p a c -> p (a c)"),
                                  xT[:, BC * k:BC * (k + 1)].rearrange("p b n -> p (b n)"), start=True, stop=True
                                  ).then_inc(v_mm, 1)

                def project(k):
                    if k >= 2:
                        pe.wait_ge(o_ev, 4 * (k - 1))
                    for half in range(2):
                        o = ps[:, 3 + 2 * (k % 2) + half, :]
                        pe.wait_ge(vl_done, k * H3 + (half + 1) * H3 // 2)
                        for jj in range(4):
                            for part, v in enumerate((vh, vl)):
                                v = v[:, k % 2].rearrange("p h n -> p (h n)")
                                ins = pe.matmul(o, pw[:, jj].rearrange("p a c -> p (a c)"),
                                                v[:, half * 2048 + jj:(half + 1) * 2048:4],
                                                start=(jj == 0 and part == 0), stop=(jj == 3 and part == 1))
                        ins.then_inc(o_mm, 1)

                def turn(k):
                    pe.wait_ge(o_ev, 4 * (k + 1))
                    if k >= 1:
                        pe.wait_ge(t_ev, 2 * k)
                    for b in range(BC):
                        for par in range(2):
                            ins = pe.matmul(ps[:, 7, (2 * b + par) * C:(2 * b + par + 1) * C],
                                            oT[:, k % 2, b, par].rearrange("p h m -> p (h m)"), K["fold"][:],
                                            start=True, stop=True)
                    ins.then_inc(t_mm, 1)

                values(0)
                for k in range(NC3):
                    if k + 1 < NC3:
                        values(k + 1)
                    project(k)
                    if k >= 1:
                        turn(k - 1)
                turn(NC3 - 1)

            @block.scalar
            def _(act):
                ln.scalar(act)
                for k in range(NC3):
                    act.wait_ge(xt_mm, k + 1)
                    act.copy(xT[:, 4 * k:4 * k + 4].rearrange("p b n -> p (b n)"), ps[:, k % 2, :]).then_inc(xt_ev, 1)

                def high(k, h):
                    n = k * H3 + h
                    act.wait_ge(v_ev, n + 1)
                    if k >= 2:
                        act.wait_ge(o_mm, 2 * (k - 1))
                    act.copy(vh[:, k % 2, h], vg[:, n % 4]).then_inc(vh_done, 1)

                def out_rows(k, half):
                    act.wait_ge(o_mm, 2 * k + half + 1)
                    if k >= 2:
                        act.wait_ge(t_mm, k - 1)
                    src = ps[:, 3 + 2 * (k % 2) + half, :].rearrange("p (h b m a) -> p a h b m", h=4, b=BC, a=2)
                    for par in range(2):
                        act.activation(oT[:, k % 2, :, par, 4 * half:4 * half + 4, :].rearrange("p b h m -> p h b m"),
                                       src[:, par], ACT.Identity, bias=pbias[:]).then_inc(o_ev, 1)

                for k in range(NC3):
                    for h in range(H3):
                        high(k, h)
                        if k >= 1 and h in (3, 7):
                            out_rows(k - 1, h // 4)
                for half in range(2):
                    out_rows(NC3 - 1, half)

            @block.vector
            def _(dve):
                then = counter(dve, own_v)
                ln.vector(dve, then)
                dve.wait_ge(loaded, 160)
                then(dve.tensor_reduce(ls[:], lb[:], AX.X, ALU.add))
                then(dve.tensor_scalar(ls[:], ls[:], SCALE, None, ALU.mult))
                then(dve.tensor_scalar(bq[:], bq[:], float(N), None, ALU.mult))
                dve.wait_ge(xt_ev, NC3)
                dve.tensor_reduce(sx[:], xT[:], AX.X, ALU.add).then_inc(sx_ready, 1)
                dve.wait_ge(g_mm, 1)
                then(dve.tensor_tensor(gain[:], ps[:, 2, 0:H3 * B].rearrange("p (h b) -> p h b", b=B),
                                       bq[:].unsqueeze(2).to_broadcast([P, H3, B]), ALU.add))
                then(dve.tensor_scalar(gain[:], gain[:], ls[:], None, ALU.mult))

                def residual(k):
                    dve.wait_ge(t_mm, k + 1)
                    for u in range(2):
                        x = X[:, 2 * k + u].rearrange("p a (b c) -> p a b c", b=2)
                        t = ps[:, 7, u * 4 * C:(u + 1) * 4 * C].rearrange("p (b a c) -> p a b c", b=2, a=2)
                        dve.tensor_tensor(x, x, t, ALU.add).then_inc(t_ev, 1)

                for k in range(NC3):
                    for h in range(H3):
                        n = k * H3 + h
                        dve.wait_ge(v_mm, n + 1)
                        if n >= 4:
                            dve.wait_ge(vl_done, n - 3)
                        dve.scalar_tensor_tensor(
                            out=vg[:, n % 4].rearrange("p (b n) -> p b n", b=BC),
                            in0=ps[:, n % 2, :].rearrange("p (b n) -> p b n", b=BC), scalar=bv[:, h:h + 1],
                            in1=gain[:, h, BC * k:BC * (k + 1)].unsqueeze(2).to_broadcast([P, BC, P]),
                            op0=ALU.add, op1=ALU.mult).then_inc(v_ev, 1)
                    if k >= 2:
                        residual(k - 2)
                residual(NC3 - 2)
                residual(NC3 - 1)


def stage_out(nc, sem, K, X, out):
    with ExitStack() as st:
        ps = st.enter_context(nc.psum_tensor("o_ps", [P, 4, BANK], F32))
        Y = st.enter_context(nc.sbuf_tensor("o_y", [P, Q, N], F32))
        mm, ev, stored = sem("o_mm"), sem("o_ev"), sem("o_st")
        out_v = out.rearrange("(q b) c y w -> (b c) q (y w)", b=2)
        with nc.Block() as block:
            @block.tensor
            def _(pe):
                for k in range(Q // 2):
                    if k >= 4:
                        pe.wait_ge(ev, k - 3)
                    for u in range(4):
                        ins = pe.transpose(ps[:, k % 4, u * P:(u + 1) * P], X[:, 2 * k + u // 2, u % 2, :], K["ident"][:])
                    ins.then_inc(mm, 1)

            def move(eng, copy, k):
                eng.wait_ge(mm, k + 1)
                copy(Y[:, 2 * k:2 * k + 2].rearrange("p q (n a) -> p q a n", a=2),
                     ps[:, k % 4, :].rearrange("p (q a n) -> p q a n", q=2, a=2)).then_inc(ev, 1)

            @block.vector
            def _(dve):
                for k in range(Q // 2):
                    move(dve, dve.tensor_copy, k)

            @block.sync
            def _(sp):
                for g in range(G):
                    sp.wait_ge(ev, 2 * (g + 1))
                    sp.dma_start(out_v[:, g * QG:(g + 1) * QG, :], Y[:, g * QG:(g + 1) * QG, :]).then_inc(stored, 16)
                sp.wait_ge(stored, 16 * G)


def build(nc, A, out):
    with ExitStack() as ctx:
        def sb(name, shape, dt=F32):
            return ctx.enter_context(nc.sbuf_tensor(name, shape, dt))

        used = []

        def sem(name):
            used.append(nc.alloc_semaphore(name=name))
            return used[-1]

        def reuse():
            nc.clear_and_free_semaphores(used)
            nc.all_engine_barrier()
            used.clear()
        X = sb("X", [P, Q, 2, 2 * C])
        K = {"ident": sb("ident", [P, P]), "fold": sb("fold", [P, C]), "iota": sb("iota", [P, 32]),
             "row0": sb("row0", [P, P]), "fill": sb("fill", [P, TH * P // BS]), "reset": sb("reset", [P, E * TH]),
             "upper": sb("upper", [P, P]), "ones": sb("ones", [P, P])}
        XD = [nc.dram_tensor(f"blocks_x{h}", (NBLK * BS, P), F32, kind="Internal").ap() for h in range(PARTS)]
        YD = [nc.dram_tensor(f"blocks_y{h}", (NBLK * BS, C), F32, kind="Internal").ap() for h in range(PARTS)]
        zeroed = nc.alloc_semaphore(name="zeroed")
        with ExitStack() as st:
            def tmp(name, shape, dt=F32):
                return st.enter_context(nc.sbuf_tensor(name, shape, dt))
            Xc = tmp("Xc", [P, Q, N])
            wproj = tmp("wproj", [P, 2, C])
            FM = tmp("FM", [P, Q, 2, 2 * C])
            V = tmp("V", [P, Q, 2, 2 * C + 4])
            QKf = tmp("QKf", [P, Q, 2, 4 * C])
            with ExitStack() as st2:
                xn = st2.enter_context(nc.sbuf_tensor("xn0", [P, Q, N], F32))
                wqkv = st2.enter_context(nc.sbuf_tensor("wqkv", [P, 3, 2, C], F32))
                brow = st2.enter_context(nc.sbuf_tensor("brow", [P, 3, 2, C], F32))
                rowk = st2.enter_context(nc.sbuf_tensor("rowk", [KS * WW, HD, 2, 8], F32))
                epsv = st2.enter_context(nc.sbuf_tensor("epsv", [P, C], F32))
                stage_norm(nc, sem, A, K, Xc, xn, wqkv, brow, wproj, rowk, epsv)
                stage_qkv(nc, sem, A, K, xn, wqkv, brow, rowk, epsv, QKf, V, FM,
                          S=X[:].rearrange("p (g q) a c -> p g (q a c)", g=2))
            WR = ctx.enter_context(nc.sbuf_tensor("WR", [P, E, WC], F32, side="right"))
            zeros = ctx.enter_context(nc.sbuf_tensor("zeros", [P, 4 * P], F32, side="right"))
            stage_attend(nc, sem, A, K, Xc, QKf, V, FM, wproj, X, WR, XD, zeros, zeroed)
        reuse()
        stage_pool(nc, sem, A, K, X)
        for L in ("L2_ffn", "L3_ffn"):
            stage_mixture(nc, sem, A, K, X, L, WR, XD, YD, (zeroed, 16 * PARTS))
            reuse()
            if L == "L2_ffn":
                stage_linear(nc, sem, A, K, X, WR)
        stage_out(nc, sem, K, X, out)


def shape_constants():
    pos = np.zeros((5, 4, P), np.float32)
    for r in range(P):
        for j in range(4):
            n = (r % C) * 4 + j
            jj, ii = np.float32(n % WW) / np.float32(WW - 1), np.float32(n // WW) / np.float32(HH - 1)
            pos[:, j, r] = (jj, ii, np.float32(1) - jj, np.float32(1) - ii, 1)
    pairs = np.kron(np.eye(P // 2), np.full((2, 2), 0.5)).astype(np.float32)
    mask = np.kron(np.eye(P // HD), np.ones((HD, HD))).astype(np.float32)
    selx = np.zeros((KS, KS, WW, KS, WW), np.float32)
    for dy in range(KS):
        for ix in range(WW):
            for jx in range(WW):
                if 0 <= jx - ix + KS // 2 < KS:
                    selx[dy, jx - ix + KS // 2, ix, dy, jx] = 1
    sely = np.zeros((KS, WW, 2, 2 * HH - 1, WW // 2), np.float32)
    for dy in range(KS):
        for jx in range(WW):
            sely[dy, jx, jx % 2, dy - KS // 2 + HH - 1, jx // 2] = 1
    return {
        "k_pos": pos, "k_pairs": pairs, "k_mask": mask, "k_ident": np.eye(P, dtype=np.float32),
        "k_selx": selx.reshape(KS * KS, WW, KS * WW), "k_sely": sely.reshape(KS * WW, 2, -1),
        "k_fold": np.concatenate([np.eye(C), np.eye(C)]).astype(np.float32),
        "k_iota": np.tile(np.arange(32, dtype=np.float32), (P, 1)),
        "k_fill": np.tile(np.arange(TH * P // BS, dtype=np.float32) * BS, (P, 1)),
        "k_reset": np.tile((np.arange(E * TH) % TH > 0).astype(np.float32), (P, 1)),
        "k_upper": np.triu(np.ones((P, P), np.float32), 1),
    }


_INS = ['x', 'L0_conv_W', 'L0_conv_b', 'L1_conv_Wq', 'L1_conv_bq', 'L1_conv_Wkv', 'L1_conv_bkv', 'L1_conv_Wproj',
        'L1_conv_bproj', 'L1_conv_dwc_w', 'L1_conv_dwc_b', 'L1_conv_scale_param', 'L2_attn_fc_w', 'L2_attn_fc_b',
        'L2_attn_score_w', 'L2_ffn_gate_w', 'L2_ffn_gate_b', 'L2_ffn_w1', 'L2_ffn_w2', 'L2_ffn_w3', 'L3_attn_qkv_w',
        'L3_attn_qkv_b', 'L3_attn_lunchbox', 'L3_attn_proj_w', 'L3_attn_proj_b', 'L3_ffn_gate_w', 'L3_ffn_gate_b',
        'L3_ffn_w1', 'L3_ffn_w2', 'L3_ffn_w3']


def kernel(**inputs):
    import concourse.bacc as bacc
    from concourse.bass_utils import run_bass_kernel_spmd

    nc = bacc.Bacc("TRN2", target_bir_lowering=False, num_devices=1)
    arrays, A = {}, {}
    for name, a in [(n, inputs[n]) for n in _INS] + list(shape_constants().items()):
        a = np.ascontiguousarray(a)
        arrays[f"in_{name}"] = a
        A[name] = nc.dram_tensor(f"in_{name}", a.shape, mybir.dt.from_np(a.dtype), kind="ExternalInput").ap()
    out = nc.dram_tensor("out_x", (B, C, HH, WW), F32, kind="ExternalOutput").ap()
    build(nc, A, out)
    r = run_bass_kernel_spmd(nc, [arrays], core_ids=[0])
    return r.results[0]["out_x"]
```

```python
from contextlib import ExitStack

import numpy as np

import concourse.bass as bass
from concourse import mybir

F32 = mybir.dt.float32
F32R = mybir.dt.float32r
ALU = mybir.AluOpType
ACT = mybir.ActivationFunctionType
AX = mybir.AxisListType

B, C, HH, WW = 32, 64, 16, 16
N = HH * WW
P = 128
Q = B // 2
NT = Q * 2 * 2
NH, HD = 8, C // 8
KS = 5
E, HID = 16, 128
H3 = 8
G = 4
QG = Q // G
BANK = 512
BIG = 1e38


def counter(eng, sem):
    n = [0]

    def then(ins):
        n[0] += 1
        ins.then_inc(sem, 1)
        eng.wait_ge(sem, n[0])
    return then


def bcast(ap, shape):
    return ap.to_broadcast(shape)


def stage_norm(nc, sem, A, K, Xc, xn, wqkv, brow, rows2, wproj, rowk, epsv):
    with ExitStack() as st:
        def sb(name, shape, dt=F32):
            return st.enter_context(nc.sbuf_tensor(name, shape, dt))
        ps = st.enter_context(nc.psum_tensor("n_ps", [P, 8, BANK], F32))
        posw = sb("n_posw", [5, C])
        w1 = sb("n_w1", [P, 2, C])
        w2 = sb("n_w2", [P, 2, C])
        taps = sb("n_taps", [KS * KS, HD])
        selx = sb("n_selx", [KS * KS, WW, KS * WW])
        pos = sb("n_pos", [5, 4, P])
        pairs = sb("n_pairs", [P, P])
        stats = sb("n_stats", [P, Q, 6])
        mv = sb("n_mv", [P, Q, 2])
        gm = sb("n_gm", [P, Q, 2])
        dm = sb("n_dm", [P, Q])
        vg = sb("n_vg", [P, Q])
        sd = sb("n_sd", [P, Q])
        rs = sb("n_rs", [P, Q])
        nmr = sb("n_nmr", [P, Q])
        sp_ = sb("n_sp", [P, 8, C])
        braw = sb("n_braw", [P, 3, 2, C])
        upper = sb("n_upper", [P, P])
        small, big_w, x_in = sem("n_small"), sem("n_bigw"), [sem(f"n_x{g}") for g in range(G)]
        pe_ready, mv_ready, gm_ready, var_ready, sd_ready = (
            sem("n_pe"), sem("n_mv"), sem("n_gm"), sem("n_var"), sem("n_sd"))
        scale_in, bias_in, exp_in, exp_out, ln_in, ln_out = (sem("n_" + n) for n in ("sc", "bi", "ei", "eo", "li", "lo"))
        wt_ready, rowk_ps, later, norm_ready = sem("n_wt"), sem("n_rkp"), sem("n_later"), sem("n_nr")
        own_v, own_p, zeroed = sem("n_ownv"), sem("n_ownp"), sem("n_zero")
        x_v = A["x"].rearrange("(q b) c y w -> (b c) q (y w)", b=2)

        with nc.Block() as block:
            @block.sync
            def _(sp):
                sp.dma_start(sp_[:, 0, :], A["L1_conv_scale_param"].rearrange("a b c -> (a b) c").to_broadcast([P, C])
                             ).then_inc(scale_in, 16)
                for g in range(G):
                    sp.dma_start(Xc[:, g * QG:(g + 1) * QG, :], x_v[:, g * QG:(g + 1) * QG, :]).then_inc(x_in[g], 16)
                sp.wait_ge(zeroed, 1)
                for k, src in enumerate((A["L1_conv_bq"][0:C], A["L1_conv_bkv"][0:C], A["L1_conv_bkv"][C:2 * C])):
                    for row in (0, 32):
                        src2 = src.rearrange("(a b c) -> a b c", a=1, b=1).to_broadcast([1, 2, C])
                        sp.dma_start(braw[row:row + 1, k], src2).then_inc(bias_in, 16)
                for name in ("iota", "fill", "reset"):
                    sp.dma_start(K[name][:], A["k_" + name]).then_inc(later, 16)
                sp.dma_start(upper[:], A["k_upper"]).then_inc(later, 16)
                sp.wait_ge(later, 64)

            @block.gpsimd
            def _(pool):
                then = counter(pool, own_p)
                pool.memset(brow[:].bitcast(F32), 0.0).then_inc(zeroed, 1)
                pool.memset(wqkv[:], 0.0).then_inc(zeroed, 1)
                pool.memset(wproj[:], 0.0).then_inc(zeroed, 1)
                pool.memset(K["ones"][:].bitcast(F32), 1.0)
                pool.wait_ge(later, 64)
                pool.tensor_copy(K["upper"][:], upper[:])
                then(pool.memset(rows2[:].bitcast(F32), 0.0))
                pool.memset(rows2[0:1, :].bitcast(F32), 1.0)
                pool.memset(rows2[32:33, :].bitcast(F32), 1.0)

            @block.scalar
            def _(act):
                act.dma_start(pos[:], A["k_pos"]).then_inc(small, 16)
                act.dma_start(posw[0:4, :], A["L0_conv_W"].rearrange("c k -> k c"), allow_slow_non_contiguous=True
                              ).then_inc(small, 16)
                act.dma_start(posw[4:5, :], A["L0_conv_b"].rearrange("(a c) -> a c", a=1)).then_inc(small, 16)
                act.dma_start(pairs[:], A["k_pairs"]).then_inc(big_w, 16)
                act.dma_start(K["ident"][:], A["k_ident"]).then_inc(big_w, 16)
                for half in range(2):
                    act.dma_start(w1[0:C, half, :], A["L1_conv_Wq"]).then_inc(big_w, 16)
                    act.dma_start(w1[C:P, half, :], A["L1_conv_Wkv"][0:C, :]).then_inc(big_w, 16)
                    act.dma_start(w2[0:C, half, :], A["L1_conv_Wkv"][C:2 * C, :]).then_inc(big_w, 16)
                    act.dma_start(w2[C:P, half, :], A["L1_conv_Wproj"]).then_inc(big_w, 16)
                act.dma_start(taps[:], A["L1_conv_dwc_w"].rearrange("d a y x -> (a y x) d"),
                              allow_slow_non_contiguous=True).then_inc(big_w, 16)
                act.dma_start(selx[:], A["k_selx"]).then_inc(big_w, 16)
                act.wait_ge(exp_in, 1)
                act.activation(sp_[:, 2, :], sp_[:, 1, :], ACT.Exp).then_inc(exp_out, 1)
                act.wait_ge(ln_in, 1)
                act.activation(sp_[:, 5, :], sp_[:, 3, :], ACT.Ln).then_inc(ln_out, 1)
                act.wait_ge(var_ready, 1)
                act.activation(sd[:], vg[:], ACT.Sqrt).then_inc(sd_ready, 1)
                act.wait_ge(norm_ready, 1)
                for q in range(1, Q, 2):
                    act.activation(xn[:, q, :], Xc[:, q, :], ACT.Identity, bias=nmr[:, q:q + 1], scale=rs[:, q:q + 1])

            @block.tensor
            def _(pe):
                pe.wait_ge(small, 48)
                for j in range(4):
                    ins = pe.matmul(ps[:, 0, j * C:(j + 1) * C], pos[:, j, :], posw[:], start=True, stop=True)
                ins.then_inc(pe_ready, 1)
                pe.wait_ge(big_w, 16 * 12)
                pe.transpose(ps[:, 1, 0:P], w1[:].rearrange("p a c -> p (a c)"), K["ident"][:])
                pe.transpose(ps[:, 1, P:2 * P], w2[:].rearrange("p a c -> p (a c)"), K["ident"][:]).then_inc(wt_ready, 1)
                for ix in range(WW):
                    ins = pe.matmul(ps[0:KS * WW, 2, ix * 8:ix * 8 + 8], selx[:, ix, :], taps[:], start=True, stop=True)
                ins.then_inc(rowk_ps, 1)
                pe.wait_ge(mv_ready, 1)
                pe.matmul(ps[:, 3, 0:2 * Q], pairs[:], mv[:].rearrange("p q k -> p (q k)"),
                          start=True, stop=True).then_inc(gm_ready, 1)

            @block.vector
            def _(dve):
                then = counter(dve, own_v)
                dve.wait_ge(scale_in, 16)
                then(dve.tensor_scalar(sp_[:, 4, :], sp_[:, 0, :], -1.0, None, ALU.mult))
                dve.tensor_tensor(sp_[:, 1, :], sp_[:, 0, :], sp_[:, 4, :], ALU.min).then_inc(exp_in, 1)
                dve.wait_ge(pe_ready, 1)
                for g in range(G):
                    dve.wait_ge(x_in[g], 16)
                    xg = Xc[:, g * QG:(g + 1) * QG, :]
                    then(dve.tensor_tensor(xg, xg, ps[:, 0, 0:N].unsqueeze(1).to_broadcast([P, QG, N]), ALU.add))
                    for q in range(g * QG, (g + 1) * QG):
                        ins = dve.bn_stats(stats[:, q, :], Xc[:, q, :])
                then(ins)
                for q in range(Q):
                    ins = dve.bn_aggr(mv[:, q, :], stats[:, q, :])
                ins.then_inc(mv_ready, 1)
                dve.wait_ge(exp_out, 1)
                dve.tensor_scalar(sp_[:, 3, :], sp_[:, 2, :], 1.0, None, ALU.add).then_inc(ln_in, 1)
                dve.wait_ge(ln_in, 1)
                then(dve.tensor_scalar(sp_[:, 4, :], sp_[:, 3, :], -1.0, None, ALU.add))
                then(dve.tensor_scalar(sp_[:, 6, :], sp_[:, 4, :], 0.0, None, ALU.is_equal))
                dve.wait_ge(ln_out, 1)
                then(dve.tensor_tensor(sp_[:, 5, :], sp_[:, 5, :], sp_[:, 6, :], ALU.add))
                then(dve.tensor_tensor(sp_[:, 4, :], sp_[:, 4, :], sp_[:, 6, :], ALU.add))
                then(dve.reciprocal(sp_[:, 7, :], sp_[:, 4, :]))
                then(dve.tensor_tensor(sp_[:, 5, :], sp_[:, 5, :], sp_[:, 2, :], ALU.mult))
                then(dve.tensor_tensor(sp_[:, 5, :], sp_[:, 5, :], sp_[:, 7, :], ALU.mult))
                then(dve.scalar_tensor_tensor(out=sp_[:, 6, :], in0=sp_[:, 0, :], scalar=0.0, in1=sp_[:, 5, :],
                                              op0=ALU.max, op1=ALU.add))
                then(dve.reciprocal(sp_[:, 7, :], sp_[:, 6, :]))
                dve.tensor_scalar(epsv[:], sp_[:, 7, :], 1e-6, None, ALU.mult)
                dve.wait_ge(gm_ready, 1)
                then(dve.tensor_copy(gm[:].rearrange("p q k -> p (q k)"), ps[:, 3, 0:2 * Q]))
                then(dve.tensor_tensor(dm[:], mv[:, :, 0], gm[:, :, 0], ALU.subtract))
                then(dve.tensor_tensor(dm[:], dm[:], dm[:], ALU.mult))
                then(dve.tensor_tensor(vg[:], dm[:], gm[:, :, 1], ALU.add))
                dve.tensor_scalar(vg[:], vg[:], 1e-5, None, ALU.add).then_inc(var_ready, 1)
                dve.wait_ge(wt_ready, 1)
                dve.wait_ge(zeroed, 3)
                for b2 in range(2):
                    rows = slice(b2 * C, b2 * C + C)
                    for k in range(2):
                        dve.tensor_tensor(wqkv[rows, k, b2, :], ps[rows, 1, k * C:(k + 1) * C], sp_[rows, 7, :], ALU.mult)
                    dve.tensor_copy(wqkv[rows, 2, b2, :], ps[rows, 1, 2 * C:3 * C])
                    dve.tensor_copy(wproj[rows, b2, :], ps[rows, 1, 3 * C:4 * C])
                dve.wait_ge(bias_in, 96)
                for row in (slice(0, 1), slice(32, 33)):
                    b4 = braw[row, 0:2].rearrange("p k b c -> p (k b) c")
                    then(dve.tensor_tensor(b4, b4, sp_[row, 7:8, :].to_broadcast([1, 4, C]), ALU.mult))
                    then(dve.tensor_copy(brow[row], braw[row]))
                then(dve.tensor_tensor(brow[row], braw[row], brow[row].bitcast(F32), ALU.subtract))
                dve.wait_ge(rowk_ps, 1)
                dve.tensor_copy(rowk[:], ps[0:KS * WW, 2, 0:P].rearrange("k (b a d) -> k d a b", a=2, d=8))
                dve.wait_ge(sd_ready, 1)
                then(dve.reciprocal(rs[:], sd[:]))
                dve.scalar_tensor_tensor(out=nmr[:], in0=gm[:, :, 0], scalar=-1.0, in1=rs[:],
                                         op0=ALU.mult, op1=ALU.mult).then_inc(norm_ready, 1)
                dve.wait_ge(norm_ready, 1)
                for q in range(0, Q, 2):
                    dve.tensor_scalar(xn[:, q, :], Xc[:, q, :], rs[:, q:q + 1], nmr[:, q:q + 1], ALU.mult, ALU.add)


def stage_qkv(nc, sem, A, K, xn, wqkv, brow, rows2, rowk, epsv, QKf, V, FM, S):
    with ExitStack() as st:
        def sb(name, shape, dt=F32):
            return st.enter_context(nc.sbuf_tensor(name, shape, dt))
        ps = st.enter_context(nc.psum_tensor("q_ps", [P, 8, BANK], F32))
        QK = sb("q_qk", [P, Q, 2, 4 * C])
        S6 = sb("q_s6", [P, 2, QG * 2 * 4 * C])
        T = sb("q_t", [P, 2, 2 * HD, P])
        sely = sb("q_sely", [KS * WW, 2, 31 * 8])
        dwb = sb("q_dwb", [P, HD])
        n2 = sb("q_n2", [P, Q * 2 * 4])
        n6 = sb("q_n6", [P, Q * 2 * 4])
        loaded, own_v = sem("q_loaded"), sem("q_own")
        mm, qk_ev, v_ev = sem("q_mm"), sem("q_evac"), sem("q_vev")
        grp_ready, squared, cubed, sixth, norms, roots = (
            sem("q_grp"), sem("q_squared"), sem("q_cubed"), sem("q_sixth"), sem("q_norms"), sem("q_roots"))
        band_ps, band_sb, conv_mm, conv_ev, s_free, f_ready = (sem("q_" + n) for n in ("bp", "bs", "cm", "ce", "sf", "fr"))
        NT2 = 2 * Q

        def part(t, g):
            return t[:, g * QG:(g + 1) * QG].rearrange("p q a c -> p (q a c)")

        def rows(ap):
            return ap.rearrange("p (r c) -> p r c", c=C)

        with nc.Block() as block:
            @block.sync
            def _(sp):
                sp.dma_start(sely[:], A["k_sely"]).then_inc(loaded, 16)
                sp.dma_start(dwb[:], A["L1_conv_dwc_b"].rearrange("(a d) -> a d", a=1).to_broadcast([P, HD])
                             ).then_inc(loaded, 16)

            @block.tensor
            def _(pe):
                for i in range(NT2):
                    if i >= 8 and i % 2 == 0:
                        pe.wait_ge(qk_ev, i // 2 - 3)
                    if i >= 8 and i % 4 == 0:
                        pe.wait_ge(v_ev, i // 4 - 1)
                    for bank, c0, k in ((i // 2 % 4, i % 2 * 4 * C, slice(0, 2)), (4 + i // 4 % 2, i % 4 * 2 * C, slice(2, 3))):
                        w, b = (t[:, k].rearrange("p k b c -> p (k b c)") for t in (wqkv, brow))
                        o = ps[:, bank, c0:c0 + (k.stop - k.start) * 2 * C]
                        pe.matmul(o, xn[:, i // 2, i % 2:N:2], w, start=True, stop=False)
                        ins = pe.matmul(o, rows2[:], b, start=False, stop=True)
                    if i % 2 == 1:
                        ins.then_inc(mm, 1)
                pe.wait_ge(loaded, 32)
                for k in range(8):
                    pj, i4 = k // 4, (k % 4) * 4
                    if k >= 2:
                        pe.wait_ge(band_sb, k - 1)
                    for u in range(4):
                        s0 = (HH - 1 - (i4 + u)) * 8
                        ins = pe.matmul(ps[:, 6 + k % 2, u * P:(u + 1) * P], sely[:, pj, s0:s0 + P],
                                        rowk[:].rearrange("k d a b -> k (d a b)"), start=True, stop=True)
                    ins.then_inc(band_ps, 1)
                pe.wait_ge(v_ev, Q // 2)
                pe.wait_ge(band_sb, 8)
                for k in range(2 * HD):
                    d, pi = k // 2, k % 2
                    if k >= 2:
                        pe.wait_ge(conv_ev, k - 1)
                    for pj in range(2):
                        ins = pe.matmul(ps[:, 4 + k % 2, 0:B * NH], T[:, pj, 2 * d + pi, :],
                                        V[:, :, pj, d:2 * C:HD], start=(pj == 0), stop=(pj == 1))
                    ins.then_inc(conv_mm, 1)

            @block.scalar
            def _(act):
                def square(g):
                    if g >= 2:
                        act.wait_ge(cubed, g - 1)
                        act.wait_ge(norms, 2 * (g - 2) + 1)
                    act.activation(S[:, g % 2], part(QK, g), ACT.Square).then_inc(squared, 1)

                def sixths(g):
                    act.wait_ge(cubed, g + 1)
                    if g >= 2:
                        act.wait_ge(norms, 2 * (g - 2) + 2)
                    act.activation(S6[:, g % 2], part(QKf, g), ACT.Square).then_inc(sixth, 1)

                def root(g):
                    act.wait_ge(norms, 2 * g + 2)
                    r = slice(g * QG * 8, (g + 1) * QG * 8)
                    act.activation(n2[:, r], n2[:, r], ACT.Sqrt).then_inc(roots, 1)
                    act.activation(n6[:, r], n6[:, r], ACT.Sqrt).then_inc(roots, 1)

                def bands(k):
                    pj, i4 = k // 4, (k % 4) * 4
                    act.wait_ge(band_ps, k + 1)
                    act.copy(T[:, pj, :, i4 * 8:(i4 + 4) * 8].rearrange("p a (u b) -> p u a b", b=8),
                             ps[:, 6 + k % 2, :].rearrange("p (u a b) -> p u a b", u=4, b=8)).then_inc(band_sb, 1)

                def conv(k):
                    d, pi = k // 2, k % 2
                    act.wait_ge(conv_mm, k + 1)
                    act.activation(FM[:, :, pi, d:2 * C:HD], ps[:, 4 + k % 2, 0:B * NH].rearrange("p (q h) -> p q h", q=Q),
                                   ACT.Identity, bias=dwb[:, d:d + 1]).then_inc(conv_ev, 1)

                for g in range(G):
                    for j in range(g * QG // 2, (g + 1) * QG // 2):
                        act.wait_ge(mm, 2 * j + 2)
                        act.copy(V[:, 2 * j:2 * j + 2, :, 0:2 * C],
                                 ps[:, 4 + j % 2, :].rearrange("p (q a c) -> p q a c", q=2, a=2)).then_inc(v_ev, 1)
                    if g == G - 1:
                        act.wait_ge(loaded, 32)
                        bands(0)
                        bands(1)
                    act.wait_ge(qk_ev, (g + 1) * QG)
                    square(g)
                    if g == G - 1:
                        bands(2)
                    if g >= 1:
                        sixths(g - 1)
                    if g == G - 1:
                        bands(3)
                    if g >= 2:
                        root(g - 2)
                for k in range(4, 8):
                    bands(k)
                sixths(G - 1)
                conv(0)
                root(G - 2)
                for k in range(1, 4):
                    conv(k)
                root(G - 1)
                for k in range(4, 2 * HD):
                    conv(k)

            def cube(eng, g):
                eng.wait_ge(squared, g + 1)
                eng.tensor_tensor(part(QKf, g), S[:, g % 2], part(QK, g), ALU.mult).then_inc(cubed, 1)

            def scale(eng, g, k0):
                eng.wait_ge(f_ready, g + 1)
                eng.wait_ge(sixth, g + 1)
                v = QKf[:, g * QG:(g + 1) * QG].rearrange("p q a (k c) -> p (q a) k c", c=C)[:, :, k0:k0 + 2]
                f = n2[:, g * QG * 8:(g + 1) * QG * 8].rearrange("p (r k) -> p r k", k=4)[:, :, k0:k0 + 2]
                eng.tensor_tensor(v, v, f.unsqueeze(3).to_broadcast([P, 2 * QG, 2, C]), ALU.mult)

            @block.gpsimd
            def _(pool):
                pool.memset(V[:, :, :, 2 * C:2 * C + 4], 1.0)
                for g in range(G + 2):
                    if g < G - 1:
                        cube(pool, g)
                    if g >= 2:
                        scale(pool, g - 2, 2)

            @block.vector
            def _(dve):
                then = counter(dve, own_v)
                for g in range(G + 3):
                    if g < G:
                        for q in range(g * QG, (g + 1) * QG):
                            dve.wait_ge(mm, q + 1)
                            dve.scalar_tensor_tensor(out=rows(QK[:, q].rearrange("p a c -> p (a c)")), in0=rows(ps[:, q % 4, :]),
                                                     scalar=0.0, in1=epsv[:].unsqueeze(1).to_broadcast([P, 8, C]),
                                                     op0=ALU.max, op1=ALU.add).then_inc(qk_ev, 1)
                    if 0 <= g - 1 < G:
                        r = slice((g - 1) * QG * 8, g * QG * 8)
                        if g == G:
                            dve.wait_ge(cubed, G - 1)
                            cube(dve, G - 1)
                        dve.wait_ge(squared, g)
                        dve.tensor_reduce(n2[:, r], rows(S[:, (g - 1) % 2]), AX.X, ALU.add).then_inc(norms, 1)
                        dve.wait_ge(sixth, g)
                        dve.tensor_reduce(n6[:, r], rows(S6[:, (g - 1) % 2]), AX.X, ALU.add).then_inc(norms, 1)
                    if 0 <= g - 2 < G:
                        r = slice((g - 2) * QG * 8, (g - 1) * QG * 8)
                        dve.wait_ge(roots, 2 * (g - 1))
                        then(dve.reciprocal(n6[:, r], n6[:, r]))
                        dve.tensor_tensor(n2[:, r], n2[:, r], n6[:, r], ALU.mult).then_inc(f_ready, 1)
                        scale(dve, g - 2, 0)


def stage_attend(nc, sem, A, K, Xc, QKf, V, FM, wproj, X, WR, XD, zeros, zeroed, weights_in):
    with ExitStack() as st:
        def sb(name, shape, dt=F32):
            return st.enter_context(nc.sbuf_tensor(name, shape, dt))
        ps = st.enter_context(nc.psum_tensor("a_ps", [P, 8, BANK], F32))
        W = P + 2 * NH
        QT = sb("a_qt", [P, Q, 2, P])
        mask = sb("a_mask", [P, P])
        BD = sb("a_bd", [P, Q, W])
        z = sb("a_z", [P, 2, 2, 2 * NH])
        y = sb("a_y", [P, 2, 2, P])
        yf = sb("a_yf", [P, 2, 2, P])
        oT = sb("a_ot", [P, 2, 2, P])
        bp = sb("a_bp", [P, 2, C])
        loaded, own_v = sem("a_loaded"), sem("a_own")
        qt_mm, qt_ev, kv_mm, kv_ev = (sem("a_qm"), sem("a_qe"), sem("a_km"), sem("a_ke"))
        nd_mm, y_ready, yf_ready, t_mm, o_ready, pr_mm, pr_ev = (
            sem("a_" + n) for n in ("nm", "yr", "yf", "tm", "or", "pm", "pe"))
        zeros_set = sem("a_zs")

        with nc.Block() as block:
            @block.sync
            def _(sp):
                sp.dma_start(mask[:], A["k_mask"]).then_inc(loaded, 16)
                for b2 in range(2):
                    sp.dma_start(bp[:, b2, :], A["L1_conv_bproj"].rearrange("(a c) -> a c", a=1).to_broadcast([P, C])
                                 ).then_inc(loaded, 16)
                load_weights(sp, A, "L2_ffn", WR, weights_in)
                sp.wait_ge(zeros_set, 1)
                for part in range(PARTS):
                    rows = XD[part].rearrange("(p a b) c -> p a (b c)", p=P, b=4)
                    sp.dma_start(rows, zeros[:].unsqueeze(1).to_broadcast(rows.shape)).then_inc(zeroed, 16)

            @block.tensor
            def _(pe):
                def kv(q):
                    if q >= 2:
                        pe.wait_ge(kv_ev, q - 1)
                    for par in range(2):
                        ins = pe.matmul(ps[:, 4 + q % 2, 0:2 * C + 1], QKf[:, q, par, 2 * C:4 * C],
                                        V[:, q, par, 0:2 * C + 1], start=(par == 0), stop=(par == 1))
                    ins.then_inc(kv_mm, 1)

                def qt(k):
                    if k >= 2:
                        pe.wait_ge(qt_ev, k - 1)
                    for u in range(4):
                        ins = pe.transpose(ps[:, 2 + k % 2, u * P:(u + 1) * P], QKf[:, 2 * k + u // 2, u % 2, 0:2 * C],
                                           K["ident"][:])
                    ins.then_inc(qt_mm, 1)

                for q in range(Q):
                    kv(q)
                    if q % 2 == 1:
                        qt(q // 2)

                def numden(q):
                    pe.wait_ge(kv_ev, q + 1)
                    pe.wait_ge(qt_ev, q // 2 + 1)
                    if q >= 2:
                        pe.wait_ge(y_ready, q - 1)
                    for par in range(2):
                        ins = pe.matmul(ps[:, q % 2, par * W:(par + 1) * W], QT[:, q, par, :], BD[:, q, :],
                                        start=True, stop=True)
                    ins.then_inc(nd_mm, 1)

                def turn(q):
                    if q == 0:
                        pe.wait_ge(qt_ev, Q // 2)
                    if q >= 2:
                        pe.wait_ge(o_ready, q - 1)
                    pe.wait_ge(yf_ready, q + 1)
                    for par in range(2):
                        ins = pe.transpose(ps[:, 2 + q % 2, par * P:(par + 1) * P], yf[:, q % 2, par], K["ident"][:])
                    ins.then_inc(t_mm, 1)

                def project(q):
                    if q >= 2:
                        pe.wait_ge(pr_ev, q - 1)
                    pe.wait_ge(o_ready, q + 1)
                    for par in range(2):
                        o = ps[:, 6 + q % 2, par * P:(par + 1) * P]
                        pe.matmul(o, Xc[:, q, par:N:2], K["ident"][:], start=True, stop=False)
                        ins = pe.matmul(o, oT[:, q % 2, par], wproj[:].rearrange("p b c -> p (b c)"),
                                        start=False, stop=True)
                    ins.then_inc(pr_mm, 1)

                for i in range(Q + 3):
                    if i < Q:
                        numden(i)
                    if 0 <= i - 2 < Q:
                        turn(i - 2)
                    if 0 <= i - 3 < Q:
                        project(i - 3)

            @block.scalar
            def _(act):
                for k in range(Q // 2):
                    act.wait_ge(qt_mm, k + 1)
                    act.copy(QT[:, 2 * k:2 * k + 2].rearrange("p a b n -> p (a b n)"), ps[:, 2 + k % 2, :]
                             ).then_inc(qt_ev, 1)
                for q in range(Q):
                    act.wait_ge(t_mm, q + 1)
                    if q >= 2:
                        act.wait_ge(pr_mm, q - 1)
                    act.copy(oT[:, q % 2].rearrange("p a n -> p (a n)"), ps[:, 2 + q % 2, 0:2 * P]).then_inc(o_ready, 1)

            @block.gpsimd
            def _(pool):
                pool.memset(zeros[:], 0.0).then_inc(zeros_set, 1)
                for q in range(Q):
                    pool.wait_ge(y_ready, q + 1)
                    if q >= 2:
                        pool.wait_ge(t_mm, q - 1)
                    pool.tensor_tensor(yf[:, q % 2], y[:, q % 2], FM[:, q], ALU.add).then_inc(yf_ready, 1)

            @block.vector
            def _(dve):
                then = counter(dve, own_v)
                dve.wait_ge(loaded, 48)
                for q in range(Q):
                    dve.wait_ge(kv_mm, q + 1)
                    dve.tensor_tensor(BD[:, q, 0:P], ps[:, 4 + q % 2, 0:P], mask[:], ALU.mult)
                    dve.tensor_tensor(BD[:, q, P:W], mask[:, 0:P:HD], ps[:, 4 + q % 2, P:P + 1].to_broadcast([P, 2 * NH]),
                                      ALU.mult).then_inc(kv_ev, 1)

                def out(q):
                    dve.wait_ge(pr_mm, q + 1)
                    dve.tensor_tensor(X[:, q], ps[:, 6 + q % 2, 0:2 * P].rearrange("p (a n) -> p a n", a=2),
                                      bp[:].rearrange("p b c -> p (b c)").unsqueeze(1).to_broadcast([P, 2, P]),
                                      ALU.add).then_inc(pr_ev, 1)

                for q in range(Q):
                    dve.wait_ge(nd_mm, q + 1)
                    nd = ps[:, q % 2, 0:2 * W].rearrange("p (a w) -> p a w", w=W)
                    then(dve.tensor_scalar(z[:, q % 2], nd[:, :, P:W], 1e-6, None, ALU.add))
                    then(dve.reciprocal(z[:, q % 2], z[:, q % 2]))
                    if q >= 2:
                        dve.wait_ge(yf_ready, q - 1)
                    dve.tensor_tensor(y[:, q % 2].rearrange("p a (h d) -> p a h d", d=HD),
                                      nd[:, :, 0:P].rearrange("p a (h d) -> p a h d", d=HD),
                                      z[:, q % 2].unsqueeze(3).to_broadcast([P, 2, 2 * NH, HD]),
                                      ALU.mult).then_inc(y_ready, 1)
                    if q >= 4:
                        out(q - 4)
                for q in range(Q - 4, Q):
                    out(q)


class LayerNorm:

    def __init__(self, nc, sem, st, tag, X, out, done, room=None, sq=None):
        self.X, self.out, self.done = X, out, done
        self.xm = st.enter_context(nc.sbuf_tensor(tag + "xm", [P, Q, 2, 2 * C], F32))[:] if room is None else room
        self.sq = st.enter_context(nc.sbuf_tensor(tag + "sq", [P, 2, QG * 4 * C], F32))[:] if sq is None else sq
        self.mean = st.enter_context(nc.sbuf_tensor(tag + "s1", [P, NT], F32))
        self.var = st.enter_context(nc.sbuf_tensor(tag + "s2", [P, NT], F32))
        self.r = st.enter_context(nc.sbuf_tensor(tag + "r", [P, NT], F32))
        self.mean_done, self.centered, self.squared, self.var_done, self.sd_done = (
            sem(tag + n) for n in ("mea", "cen", "sqd", "var", "sd"))

    def flat(self, t, g):
        g %= t.shape[1] // QG
        return t[:, g * QG:(g + 1) * QG].rearrange("p q a c -> p (q a c)")

    def rows(self, t, g):
        return self.flat(t, g).rearrange("p (r c) -> p r c", c=C)

    def cols(self, t, g):
        return t[:, g * NT // G:(g + 1) * NT // G]

    def pool(self, pool):
        for g in range(G):
            pool.wait_ge(self.mean_done, g + 1)
            pool.tensor_tensor(self.rows(self.xm, g), self.rows(self.X, g),
                               self.cols(self.mean, g).unsqueeze(2).to_broadcast([P, NT // G, C]),
                               ALU.add).then_inc(self.centered, 1)

    def center(self, dve, g):
        dve.wait_ge(self.mean_done, g + 1)
        dve.tensor_tensor(self.rows(self.xm, g), self.rows(self.X, g),
                          self.cols(self.mean, g).unsqueeze(2).to_broadcast([P, NT // G, C]),
                          ALU.add).then_inc(self.centered, 1)

    def square(self, act, g):
        act.wait_ge(self.centered, g + 1)
        if g >= 2:
            act.wait_ge(self.var_done, g - 1)
        act.activation(self.sq[:, g % 2], self.flat(self.xm, g), ACT.Square).then_inc(self.squared, 1)

    def root(self, act, g):
        act.wait_ge(self.var_done, g + 1)
        act.activation(self.cols(self.var, g), self.cols(self.var, g), ACT.Sqrt).then_inc(self.sd_done, 1)

    def scalar(self, act):
        for g in range(G + 1):
            if g < G:
                self.square(act, g)
            if g >= 1:
                self.root(act, g - 1)

    def sum(self, dve, then, g):
        s = self.cols(self.mean, g)
        then(dve.tensor_reduce(s, self.rows(self.X, g), AX.X, ALU.add))
        dve.tensor_scalar(s, s, -1.0 / C, None, ALU.mult).then_inc(self.mean_done, 1)

    def variance(self, dve, then, g):
        s = self.cols(self.var, g)
        dve.wait_ge(self.squared, g + 1)
        then(dve.tensor_reduce(s, self.sq[:, g % 2].rearrange("p (r c) -> p r c", c=C), AX.X, ALU.add))
        dve.tensor_scalar(s, s, 1.0 / C, 1e-5, ALU.mult, ALU.add).then_inc(self.var_done, 1)

    def normalize(self, dve, then, g):
        dve.wait_ge(self.sd_done, g + 1)
        then(dve.reciprocal(self.cols(self.r, g), self.cols(self.var, g)))
        for o, i, r in self.out(g):
            ins = dve.tensor_tensor(o, i, r, ALU.mult)
        ins.then_inc(self.done, 1)

    def part_scalar(self, act, part):
        for g in (2 * part, 2 * part + 1):
            self.square(act, g)
        for g in (2 * part, 2 * part + 1):
            self.root(act, g)

    def part_vector(self, dve, then, part, more=lambda g: None):
        groups = (2 * part, 2 * part + 1)
        for step in (self.sum, lambda dve, then, g: self.center(dve, g), self.variance, self.normalize):
            for g in groups:
                step(dve, then, g)
        for g in groups:
            more(g)

    def vector(self, dve, then):
        for g in range(G + 3):
            if g < G:
                self.sum(dve, then, g)
            if 0 <= g - 2 < G:
                self.variance(dve, then, g - 2)
            if 0 <= g - 3 < G:
                self.normalize(dve, then, g - 3)


def load_weights(sp, A, L, WR, loaded):
    for k in range(2):
        for n, w in enumerate(("_w1", "_w2")):
            sp.dma_start(WR[k * C:(k + 1) * C, :, n * HID:(n + 1) * HID], A[L + w].rearrange("e d h -> d e h")
                         ).then_inc(loaded, 16)
    sp.dma_start(WR[:, :, 2 * HID:WC], A[L + "_w3"].rearrange("e h o -> h e o")).then_inc(loaded, 16)


def plain_norm_out(ln_of, xn):
    def out(g):
        ln, k = ln_of(), NT // G
        return [(ln.rows(ln.xm if xn is None else xn, g), ln.rows(ln.xm, g), ln.r[:, g * k:(g + 1) * k].unsqueeze(2).to_broadcast([P, k, C]))]
    return out


def stage_pool(nc, sem, A, K, X, LW):
    with ExitStack() as st:
        def sb(name, shape, dt=F32):
            return st.enter_context(nc.sbuf_tensor(name, shape, dt))
        ps = st.enter_context(nc.psum_tensor("p_ps", [P, 8, BANK], F32))
        H = sb("p_h", [P, Q, 2, 2 * C])
        HT = sb("p_ht", [P, Q * 2, P])
        QT = sb("p_qt", [P, Q * 2, P])
        AE = sb("p_ae", [P, 2, C * B])
        BH = sb("p_bh", [P, 2, C * B])
        wf = sb("p_wf", [C, 2, C])
        wbd = sb("p_wbd", [P, 2, C])
        fb = sb("p_fb", [P, 1])
        sw = sb("p_sw", [P, 2])
        e = sb("p_e", [P, 2, B])
        m = sb("p_m", [P, 2, B + 1])
        dd = sb("p_d", [P, 2, 2, B])
        ex = sb("p_ex", [P, 2, 2, B])
        s = sb("p_s", [P, 2, B + 1])
        rs = sb("p_rs", [P, 2, B])
        co = sb("p_co", [P, 2, 2, B])
        loaded, later, own_v, zeroed = sem("p_loaded"), sem("p_later"), sem("p_own"), sem("p_zero")
        normed, ht_mm, ht_ev, w_mm, w_ev, fc_mm, tanh_done, e_mm = (
            sem("p_" + n) for n in ("normed", "htm", "hte", "wm", "we", "fc", "tanh", "em"))
        exp_in, exp_out, a_ready, spread, scanned = (sem("p_" + n) for n in ("xi", "xo", "ar", "sp", "sc"))
        weighed = [sem(f"p_wg{par}") for par in range(2)]
        ln = LayerNorm(nc, sem, st, "p_", X, plain_norm_out(lambda: ln, H), normed)

        def by_batch(t, par):
            return t[:, :, par, :].rearrange("p q (b c) -> p c q b", b=2)

        with nc.Block() as block:
            def weigh(eng, par):
                cb = co[:, par, 1, :].rearrange("p (q b) -> p q b", b=2).unsqueeze(1).to_broadcast([P, C, Q, 2])
                eng.tensor_tensor(BH[:, par].rearrange("p (c q b) -> p c q b", q=Q, b=2),
                                  by_batch(H, par), cb, ALU.mult).then_inc(weighed[par], 1)

            def add(eng, par):
                eng.wait_ge(scanned, par + 1)
                eng.tensor_tensor(by_batch(X, par), by_batch(X, par),
                                  BH[:, par].rearrange("p (c q b) -> p c q b", q=Q, b=2), ALU.add)

            @block.sync
            def _(sp):
                for k in range(2):
                    sp.dma_start(wf[:, k, :], A["L2_attn_fc_w"]).then_inc(loaded, 16)
                    sp.dma_start(fb[k * C:(k + 1) * C, :], A["L2_attn_fc_b"].rearrange("(c a) -> c a", a=1)
                                 ).then_inc(loaded, 16)
                sp.wait_ge(zeroed, 1)
                for k in range(2):
                    sp.dma_start(sw[k * C:(k + 1) * C, k:k + 1], A["L2_attn_score_w"].rearrange("(c a) -> c a", a=1)
                                 ).then_inc(loaded, 16)
                load_linear(sp, A, LW, later, (zeroed, 3))

            @block.gpsimd
            def _(pool):
                pool.memset(sw[:], 0.0).then_inc(zeroed, 1)
                pool.memset(wbd[:], 0.0).then_inc(zeroed, 1)
                pool.memset(LW["pbias"][:], 0.0).then_inc(zeroed, 1)
                ln.pool(pool)
                pool.wait_ge(a_ready, 1)
                weigh(pool, 1)
                add(pool, 0)

            @block.tensor
            def _(pe):
                pe.wait_ge(loaded, 96)
                pe.transpose(ps[:, 7, 0:C], wf[:].rearrange("p a c -> p (a c)"), K["ident"][0:C, 0:C]).then_inc(w_mm, 1)
                for k in range(Q // 2):
                    pe.wait_ge(normed, k * 2 // QG + 1)
                    if k >= 2:
                        pe.wait_ge(ht_ev, k - 1)
                    for u in range(4):
                        ins = pe.transpose(ps[:, k % 2, u * P:(u + 1) * P], H[:, 2 * k + u // 2, u % 2, :], K["ident"][:])
                    ins.then_inc(ht_mm, 1)
                pe.wait_ge(w_ev, 2)
                for k in range(Q // 2):
                    pe.wait_ge(ht_ev, k + 1)
                    if k >= 2:
                        pe.wait_ge(tanh_done, k - 1)
                    pe.matmul(ps[:, 2 + k % 2, :], wbd[:].rearrange("p b c -> p (b c)"),
                              HT[:, 4 * k:4 * k + 4].rearrange("p a n -> p (a n)"), start=True, stop=True
                              ).then_inc(fc_mm, 1)
                for k in range(2 * Q):
                    pe.wait_ge(tanh_done, k // 4 + 1)
                    ins = pe.matmul(ps[:, 4, 2 * k:2 * k + 2], QT[:, k, :], sw[:], start=True, stop=True)
                ins.then_inc(e_mm, 1)

            @block.scalar
            def _(act):
                ln.scalar(act)
                for k in range(Q // 2):
                    act.wait_ge(ht_mm, k + 1)
                    act.copy(HT[:, 4 * k:4 * k + 4].rearrange("p a n -> p (a n)"), ps[:, k % 2, :]).then_inc(ht_ev, 1)
                for k in range(Q // 2):
                    act.wait_ge(fc_mm, k + 1)
                    act.activation(QT[:, 4 * k:4 * k + 4].rearrange("p a n -> p (a n)"), ps[:, 2 + k % 2, :],
                                   ACT.Tanh, bias=fb[:]).then_inc(tanh_done, 1)
                act.wait_ge(exp_in, 2)
                act.activation(ex[:], dd[:], ACT.Exp).then_inc(exp_out, 1)
                act.wait_ge(a_ready, 1)
                for par in range(2):
                    act.copy(AE[:, par].rearrange("p (c b) -> p c b", b=B),
                             co[:, par, 0:1, :].to_broadcast([P, C, B])).then_inc(spread, 1)

            @block.vector
            def _(dve):
                then = counter(dve, own_v)
                ln.vector(dve, then)
                dve.wait_ge(w_mm, 1)
                dve.wait_ge(zeroed, 2)
                for b2 in range(2):
                    rows = slice(b2 * C, b2 * C + C)
                    dve.tensor_copy(wbd[rows, b2, :], ps[rows, 7, 0:C]).then_inc(w_ev, 1)
                dve.memset(m[:, :, 0:1], -3e38)
                dve.memset(s[:, :, 0:1], 0.0)
                dve.wait_ge(e_mm, 1)
                then(dve.tensor_copy(e[:].rearrange("p a (q b) -> p a q b", b=2),
                                     ps[:, 4, 0:NT].rearrange("p (q a b) -> p a q b", a=2, b=2)))
                for par in range(2):
                    ins = dve.tensor_tensor_scan(m[:, par, 1:B + 1], e[:, par], e[:, par], -3e38, ALU.max, ALU.max)
                then(ins)
                dve.tensor_tensor(dd[:, :, 0, :], m[:, :, 0:B], m[:, :, 1:B + 1], ALU.subtract).then_inc(exp_in, 1)
                dve.tensor_tensor(dd[:, :, 1, :], e[:], m[:, :, 1:B + 1], ALU.subtract).then_inc(exp_in, 1)
                dve.wait_ge(exp_out, 1)
                for par in range(2):
                    ins = dve.tensor_tensor_scan(s[:, par, 1:B + 1], ex[:, par, 0], ex[:, par, 1], 0.0,
                                                 ALU.mult, ALU.add)
                then(ins)
                then(dve.reciprocal(rs[:], s[:, :, 1:B + 1]))
                dve.tensor_tensor(co[:, :, 1, :], ex[:, :, 1, :], rs[:], ALU.mult)
                then(dve.tensor_tensor(co[:, :, 0, :], ex[:, :, 0, :], rs[:], ALU.mult))
                dve.tensor_tensor(co[:, :, 0, :], co[:, :, 0, :], s[:, :, 0:B], ALU.mult).then_inc(a_ready, 1)
                weigh(dve, 0)
                dve.wait_ge(weighed[0], 1)
                for par in range(2):
                    dve.wait_ge(spread, par + 1)
                    dve.wait_ge(weighed[par], 1)
                    dve.tensor_tensor_scan(BH[:, par], AE[:, par], BH[:, par], 0.0, ALU.mult, ALU.add
                                           ).then_inc(scanned, 1)
                add(dve, 1)


BS = 256
PARTS = 2
TH = NT // PARTS
UNIT = 2
NU = -(-(2 * TH * P // BS + E - 1) // UNIT)
NBLK = NU * UNIT
WC = 2 * HID + C


class Mixture:

    def __init__(self, nc, sem, kept, A, K, X, L, WR, XD, YD, GY_last):
        def sb(name, shape, dt=F32):
            return kept.enter_context(nc.sbuf_tensor(L + name, shape, dt))

        self.nc, self.A, self.K, self.X, self.L, self.WR, self.XD, self.YD = nc, A, K, X, L, WR, XD, YD
        self.mx = sb("mx", [P, PARTS, 6, TH])
        self.slot = sb("slot", [P, PARTS, 2, TH], mybir.dt.int32)
        self.owner = sb("owner", [P, PARTS, NU, UNIT], mybir.dt.int32)
        self.gw, self.gb, self.gwr = sb("gw", [P, E]), sb("gb", [P, E]), sb("gwr", [P, 2, E], F32R)
        self.HL = [None] * PARTS
        self.GY = [None] * (PARTS - 1) + [GY_last]

        def sems(*names):
            return [sem(L + n) for n in names]
        self.g_loaded, self.gw_split, self.normed = sems("gl", "gs", "nm")
        self.hi, self.lo, self.tr_mm, self.tr_ev, self.lg_mm, self.exp_in, self.exp_out = sems(
            "hi", "lo", "tm", "te", "lm", "xi", "xo")
        self.counted, self.ranked, self.owned, self.slotted = sems("cn", "rk", "ow", "sl")
        self.scattered = sems(*(f"sc{h}" for h in range(PARTS)))
        self.gathered = sems(*(f"ga{j}" for j in range(PARTS * 4)))
        self.ln = LayerNorm(nc, sem, kept, L, X, plain_norm_out(lambda: self.ln, None), self.normed, room=0, sq=0)

    def routing_room(self, st, tag, parts, ps, xm=None, sq=None, **lent):
        def sb(name, shape, dt=F32):
            if name in lent:
                return lent[name]
            return st.enter_context(self.nc.sbuf_tensor(self.L + tag + name, shape, dt))
        self.ps = ps
        self.ln.xm = sb("xm", [P, Q // PARTS, 2, 2 * C])[:] if xm is None else xm
        self.ln.sq = sb("sq", [P, 2, QG * 4 * C])[:] if sq is None else sq
        for part in parts:
            self.HL[part] = sb(f"hl{part}", [P, TH, 2, C])
        self.XS = sb("xs", [P, 4, 4 * P], F32R)
        self.lg, self.key, self.one1 = sb("lg", [P, TH, E]), sb("key", [P, TH, E]), sb("one1", [P, TH, E])
        self.tot, self.cum, self.off = sb("tot", [P, E, TH], F32R), sb("cum", [P, E, TH]), sb("off", [P, E, TH])
        self.nbk = sb("nbk", [P, E, TH * P // BS])
        self.blk = sb("blk", [P, 4, E])
        self.own = sb("own", [P, NBLK, E])
        self.ownf = sb("ownf", [P, NBLK])
        self.slotf = sb("slotf", [P, TH])

    def blocks_room(self, st, sem, outlives):
        def sb(name, shape, dt=F32):
            return st.enter_context(self.nc.sbuf_tensor(self.L + name, shape, dt))

        def sems(*names):
            return [sem(self.L + n) for n in names]
        self.GY = [(outlives or st).enter_context(self.nc.sbuf_tensor(f"{self.L}gy{h}", [P, 2, TH, C], F32))
                   for h in range(PARTS - 1)] + self.GY[-1:]
        self.xb = sb("xb", [P, 4, 4, P])
        self.xt = sb("xt", [P, 2, UNIT * BS], F32R)
        self.wb = sb("wb", [P, 4, UNIT, WC])
        self.wr = sb("wr", [P, 4, 2, UNIT, WC], F32R)
        self.gate = sb("gate", [P, 2, UNIT * BS])
        self.hid = sb("hid", [P, 2, UNIT * BS])
        self.hh = sb("hh", [P, 2, UNIT * BS], F32R)
        self.hlo = sb("hlo", [P, 2, UNIT * BS], F32R)
        self.yb = sb("yb", [P, 4, 4 * C])
        self.own_v, = sems("ov")
        self.x_in, self.w_in, self.stored = (sems(*(f"{n}{j}" for j in range(4))) for n in ("xl", "wl", "ys"))
        self.turned, self.xt_out, self.up1, self.up2, self.down = sems("bt", "bx", "b1", "b2", "bd")
        self.w_hi, self.w_lo, self.silu, self.prod, self.h_hi, self.h_lo, self.y_out = sems(
            "wh", "wo", "si", "pr", "hh_", "ho", "yo")

    def free(self, eng, sem, part, n, depth):
        if isinstance(n, int) and n < depth:
            if part:
                eng.wait_ge(sem, part * NU)
        else:
            eng.wait_ge(sem, part * NU + n - depth + 1)

    def steps(self, eng, body):
        for n in range(8):
            body(n, n % 4, n // 4)
        last = (NU - 3) // 4
        with eng.Fori(2, last) as i:
            for j in range(4):
                body(i * 4 + j, j, i)
        for n in range(4 * last, NU):
            body(n, n % 4, n // 4)

    def filled(self, part, j, i):
        return 16 * (part * ((NU + 3 - j % 4) // 4) + i + j // 4 + 1)

    def unit_rows(self, t, n):
        rows = t.rearrange("(n b p s) c -> n p b (s c)", b=UNIT, p=P, s=BS // P)
        return rows[bass.ds(n, 1)].rearrange("n p b c -> p (n b) c")

    def load_gate(self, sp):
        for k in range(2):
            sp.dma_start(self.gw[k * C:(k + 1) * C, :], self.A[self.L + "_gate_w"]).then_inc(self.g_loaded, 16)
        sp.dma_start(self.gb[:], self.A[self.L + "_gate_b"].rearrange("(a c) -> a c", a=1).to_broadcast([P, E])
                     ).then_inc(self.g_loaded, 16)

    def sync(self, sp):
        for part in range(PARTS):
            def fetch(n, j, i):
                self.free(sp, self.w_lo, part, n, 4)
                owners = self.owner[0:1, part, bass.ds(n, 1)].rearrange("p n b -> p (n b)")
                _, experts = self.nc.values_load_multi_w_load_instructions(
                    owners, engines=[mybir.EngineType.SP], min_val=0, max_val=E - 1)
                for b in range(UNIT):
                    sp.dma_start(self.wb[:, j, b:b + 1], self.WR[:, bass.ds(experts[b], 1)]).then_inc(self.w_in[j], 16)
            sp.wait_ge(self.owned, part + 1)
            self.steps(sp, fetch)
        for j in range(4):
            sp.wait_ge(self.stored[j], 16 * PARTS * ((NU + 3 - j) // 4))

    def scatter(self, pool, part):
        for k in range(2):
            pool.wait_ge(self.slotted, 2 * part + k + 1)
            for t in range(TH):
                pool.indirect_dma_start(self.XD[part], bass.IndirectOffsetOnAxis(self.slot[:, part, k, t:t + 1], 0),
                                        self.HL[part][:, t].rearrange("p a c -> p (a c)"), None
                                        ).then_inc(self.scattered[part], 16)

    def gather(self, pool, part):
        if part < PARTS - 1:
            for j in range(4):
                pool.wait_ge(self.stored[j], 16 * (part + 1) * ((NU + 3 - j) // 4))
        for t in range(TH):
            for k in range(2):
                pool.indirect_dma_start(self.GY[part][:, k, t], None, self.YD[part],
                                        bass.IndirectOffsetOnAxis(self.slot[:, part, k, t:t + 1], 0)
                                        ).then_inc(self.gathered[part * 4 + t // (TH // 4)], 16)

    def route_tensor(self, pe, part, between=lambda: None):
        ps, K = self.ps, self.K
        TG, KG = NT // G, NT // G // 4
        for g in (2 * part, 2 * part + 1):
            pe.wait_ge(self.lo, g + 1)
            for k in range(g * KG, (g + 1) * KG):
                if k >= 2:
                    pe.wait_ge(self.tr_ev, k - 1)
                for u in range(4):
                    ins = pe.transpose(ps[:, k % 2, u * P:(u + 1) * P],
                                       self.HL[part][:, (4 * k + u) % TH].rearrange("p a c -> p (a c)"), K["ident"][:])
                ins.then_inc(self.tr_mm, 1)
            pe.wait_ge(self.gw_split, 2)
            for t in range(g * TG, (g + 1) * TG):
                pe.wait_ge(self.tr_ev, t // 4 + 1)
                ins = pe.matmul(ps[:, 2 + t // TG, t % TG * 2 * E:(t % TG + 1) * 2 * E],
                                self.XS[:, t // 4 % 4, t % 4 * P:(t % 4 + 1) * P],
                                self.gwr[:].rearrange("p a e -> p (a e)"), start=True, stop=True)
                if t % 4 == 3:
                    ins.then_inc(self.lg_mm, 1)
        between()
        pe.wait_ge(self.counted, part + 1)
        m = self.tot[:].rearrange("p e t -> p (e t)")
        pe.matmul(ps[:, 6, :], K["upper"][:], m, start=True, stop=True)
        pe.matmul(ps[:, 7, :], K["ones"][:], m, start=True, stop=True).then_inc(self.ranked, 1)
        pe.wait_ge(self.slotted, 2 * part + 2)

    def tensor(self, pe):
        ps, K = self.ps, self.K
        for part in range(PARTS):
            def turn(n, j, i):
                self.free(pe, self.xt_out, part, n, 2)
                pe.wait_ge(self.x_in[j % 4], self.filled(part, j, i))
                for s in range(4):
                    ins = pe.transpose(ps[:, j % 2, s * P:(s + 1) * P], self.xb[:, j % 4, s], K["ident"][:])
                ins.then_inc(self.turned, 1)

            def up(n, j):
                count = part * NU + n + 1
                pe.wait_ge(self.xt_out, count)
                pe.wait_ge(self.w_lo, count)
                self.free(pe, self.silu, part, n, 2)
                x = self.xt[:, j % 2]
                for bank, c0, done in ((2, 0, self.up1), (4, HID, self.up2)):
                    if bank == 4:
                        self.free(pe, self.prod, part, n, 2)
                    for b in range(UNIT):
                        slots = slice(b * BS, (b + 1) * BS)
                        for k in range(2):
                            ins = pe.matmul(ps[:, bank + j % 2, slots], self.wr[:, j % 4, k, b, c0:c0 + HID], x[:, slots],
                                            start=(k == 0), stop=(k == 1))
                    ins.then_inc(done, 1)

            def down(n, j):
                self.free(pe, self.y_out, part, n, 2)
                pe.wait_ge(self.h_lo, part * NU + n + 1)
                for s in range(4):
                    o = ps[:, 6 + j % 2, s * P:(s + 1) * P].rearrange("p (a c) -> p a c", a=2)
                    for k, h in enumerate((self.hh, self.hlo)):
                        ins = pe.matmul(o, h[:, j % 2, s * P:(s + 1) * P], self.wr[:, j % 4, :, s * P // BS, 2 * HID:WC],
                                        start=(k == 0), stop=(k == 1))
                ins.then_inc(self.down, 1)

            def step(n, j, i):
                if not isinstance(n, int) or n + 3 < NU:
                    turn(n + 3, j + 3, i)
                if not isinstance(n, int) or n + 2 < NU:
                    up(n + 2, j + 2)
                down(n, j)
            for n in range(3):
                turn(n, n, 0)
            for n in range(2):
                up(n, n)
            self.steps(pe, step)

    def route_scalar(self, act, part, between=lambda: None):
        ln, ps = self.ln, self.ps
        KG = NT // G // 4
        groups = (2 * part, 2 * part + 1)
        ln.part_scalar(act, part)
        for g in groups:
            act.wait_ge(self.normed, g + 1)
            act.copy(self.HL[part][:, g % 2 * 4 * KG:(g % 2 + 1) * 4 * KG, 0, :].bitcast(F32R), ln.rows(ln.xm, g)
                     ).then_inc(self.hi, 1)
        for k in range(2 * part * KG, 2 * (part + 1) * KG):
            act.wait_ge(self.tr_mm, k + 1)
            if k >= 4:
                act.wait_ge(self.lg_mm, k - 3)
            act.copy(self.XS[:, k % 4], ps[:, k % 2, :]).then_inc(self.tr_ev, 1)
        between()
        act.wait_ge(self.exp_in, part + 1)
        act.activation(self.mx[:, part, 3], self.mx[:, part, 2], ACT.Exp).then_inc(self.exp_out, 1)

    def scalar(self, act):
        ps = self.ps
        for part in range(PARTS):
            def weights(n, j, i):
                act.wait_ge(self.w_in[j % 4], UNIT * self.filled(part, j, i))
                self.free(act, self.down, part, n, 4)
                act.copy(self.wr[:, j % 4, 0], self.wb[:, j % 4]).then_inc(self.w_hi, 1)

            def load(n, j):
                self.free(act, self.turned, part, n, 4)
                act.dma_start(self.xb[:, j % 4].rearrange("p (b s) c -> p b (s c)", b=UNIT),
                              self.unit_rows(self.XD[part], n)).then_inc(self.x_in[j % 4], 16)

            def tokens(n, j):
                act.wait_ge(self.turned, part * NU + n + 1)
                self.free(act, self.up2, part, n, 2)
                act.copy(self.xt[:, j % 2], ps[:, j % 2, :]).then_inc(self.xt_out, 1)

            def silu(n, j):
                act.wait_ge(self.up1, part * NU + n + 1)
                self.free(act, self.prod, part, n, 2)
                act.activation(self.gate[:, j % 2], ps[:, 2 + j % 2, :], ACT.Silu).then_inc(self.silu, 1)

            def halve(n, j):
                act.wait_ge(self.prod, part * NU + n + 1)
                self.free(act, self.down, part, n, 2)
                act.copy(self.hh[:, j % 2], self.hid[:, j % 2]).then_inc(self.h_hi, 1)

            def store(n, j):
                act.wait_ge(self.y_out, part * NU + n + 1)
                act.dma_start(self.unit_rows(self.YD[part], n), self.yb[:, j % 4].rearrange("p (b c) -> p b c", b=UNIT)
                              ).then_inc(self.stored[j % 4], 16)

            def step(n, j, i):
                peeled = isinstance(n, int)
                if not peeled or n + 4 < NU:
                    load(n + 4, j + 4)
                if not peeled or n + 3 < NU:
                    weights(n + 3, j + 3, i)
                    tokens(n + 3, j + 3)
                if not peeled or n + 2 < NU:
                    silu(n + 2, j + 2)
                if not peeled or n + 1 < NU:
                    halve(n + 1, j + 1)
                if not peeled or n >= 1:
                    store(n - 1, j + 3)
            act.wait_ge(self.scattered[part], 16 * 2 * TH)
            for n in range(4):
                load(n, n)
            for n in range(3):
                weights(n, n, 0)
                tokens(n, n)
            for n in range(2):
                silu(n, n)
            halve(0, 0)
            self.steps(act, step)
            store(NU - 1, (NU - 1) % 4)

    def split_gate(self, dve):
        dve.wait_ge(self.g_loaded, 48)
        dve.tensor_copy(self.gwr[:, 0], self.gw[:]).then_inc(self.gw_split, 1)
        dve.wait_ge(self.gw_split, 1)
        dve.tensor_tensor(self.gwr[:, 1], self.gw[:], self.gwr[:, 0].bitcast(F32), ALU.subtract
                          ).then_inc(self.gw_split, 1)

    def route_vector(self, dve, then, part, between=lambda: None):
        nc, ln, ps, K, mx = self.nc, self.ln, self.ps, self.K, self.mx
        full = [P, TH, E]
        lg, key, one1, blk = self.lg, self.key, self.one1, self.blk
        iota = K["iota"][:, 0:E].unsqueeze(1).to_broadcast(full)
        TG = NT // G

        def low(g):
            dve.wait_ge(self.hi, g + 1)
            hl = self.HL[part][:, g % 2 * TG:(g % 2 + 1) * TG]
            dve.tensor_tensor(hl[:, :, 1, :], ln.rows(ln.xm, g), hl[:, :, 0, :], ALU.subtract).then_inc(self.lo, 1)

        def by_tile(t):
            return t.rearrange("p e t -> p t e")

        ln.part_vector(dve, then, part, low)
        between()
        m = mx[:, part]

        def wide(k):
            return m[:, k].unsqueeze(2).to_broadcast(full)
        dve.wait_ge(self.lg_mm, (part + 1) * TH // 4)
        both = ps[:, 2 + 2 * part:4 + 2 * part, :].rearrange("p g (t a e) -> p g t a e", a=2, e=E)
        by_group = lg[:].rearrange("p (g t) e -> p g t e", g=2)
        then(dve.tensor_tensor(by_group, both[:, :, :, 0],
                               self.gb[:].unsqueeze(1).unsqueeze(1).to_broadcast([P, 2, TG, E]), ALU.add))
        then(dve.tensor_tensor(by_group, by_group, both[:, :, :, 1], ALU.add))
        for k, one in ((0, one1), (1, key)):
            then(dve.tensor_reduce(m[:, k], lg[:], AX.X, ALU.max))
            then(dve.tensor_tensor(key[:], lg[:], wide(k), ALU.is_equal))
            then(dve.scalar_tensor_tensor(out=key[:], in0=key[:], scalar=-64.0, in1=iota,
                                          op0=ALU.mult, op1=ALU.add))
            then(dve.tensor_reduce(m[:, 5], key[:], AX.X, ALU.min))
            if k == 1:
                dve.tensor_tensor(m[:, 2], m[:, 1], m[:, 0], ALU.subtract).then_inc(self.exp_in, 1)
            then(dve.tensor_tensor(one[:], key[:], wide(5), ALU.is_equal))
            if k == 0:
                then(dve.scalar_tensor_tensor(out=lg[:], in0=one1[:], scalar=-BIG, in1=lg[:],
                                              op0=ALU.mult, op1=ALU.add))
        dve.tensor_tensor(by_tile(self.tot[:]), one1[:], key[:], ALU.add).then_inc(self.counted, 1)
        dve.wait_ge(self.exp_out, part + 1)
        then(dve.tensor_scalar(m[:, 4], m[:, 3], 1.0, None, ALU.add))
        then(dve.reciprocal(m[:, 4], m[:, 4]))
        then(dve.tensor_tensor(m[:, 5], m[:, 3], m[:, 4], ALU.mult))
        dve.wait_ge(self.ranked, part + 1)
        flat = "p e t -> p (e t)"
        then(dve.tensor_tensor_scan(self.cum[:].rearrange(flat), K["reset"][:], ps[:, 7, :], 0.0,
                                    ALU.mult, ALU.add))
        n_e = self.cum[:, :, TH - 1:TH]
        nb = self.nbk.shape[2]
        then(dve.tensor_tensor(self.nbk[:], n_e.to_broadcast([P, E, nb]),
                               K["fill"][:, 0:nb].unsqueeze(1).to_broadcast([P, E, nb]), ALU.is_gt))
        then(dve.tensor_reduce(blk[:, 0], self.nbk[:], AX.X, ALU.add))
        then(dve.tensor_tensor_scan(blk[:, 1], K["ones"][:, 0:E].bitcast(F32), blk[:, 0], 0.0, ALU.mult, ALU.add))
        then(dve.tensor_tensor(blk[:, 2], blk[:, 1], blk[:, 0], ALU.subtract))
        then(dve.tensor_scalar(blk[:, 3], blk[:, 2], float(BS), None, ALU.mult))
        then(dve.tensor_tensor(self.off[:].rearrange(flat), self.cum[:].rearrange(flat), ps[:, 7, :], ALU.subtract))
        then(dve.tensor_tensor(self.off[:], self.off[:], blk[:, 3].unsqueeze(2).to_broadcast([P, E, TH]), ALU.add))
        then(dve.tensor_tensor(self.off[:].rearrange(flat), self.off[:].rearrange(flat), ps[:, 6, :], ALU.add))
        for k, one in ((0, one1), (1, key)):
            then(dve.tensor_tensor(lg[:], one[:], by_tile(self.off[:]), ALU.mult))
            then(dve.tensor_reduce(self.slotf[:], lg[:], AX.X, ALU.add))
            dve.tensor_copy(self.slot[:, part, k], self.slotf[:]).then_inc(self.slotted, 1)
            dve.wait_ge(self.slotted, 2 * part + k + 1)
        wide_b = [P, NBLK, E]
        then(dve.tensor_tensor(self.own[:], blk[:, 1].unsqueeze(1).to_broadcast(wide_b),
                               K["iota"][:, 0:NBLK].unsqueeze(2).to_broadcast(wide_b), ALU.is_le))
        then(dve.tensor_reduce(self.ownf[:], self.own[:], AX.X, ALU.add))
        then(dve.tensor_scalar(self.ownf[:], self.ownf[:], float(E - 1), None, ALU.min))
        dve.tensor_copy(self.owner[:, part].rearrange("p n b -> p (n b)"), self.ownf[:]).then_inc(self.owned, 1)

    def vector(self, dve, then):
        ps = self.ps
        for part in range(PARTS):
            def weights(n, j):
                dve.wait_ge(self.w_hi, part * NU + n + 1)
                dve.tensor_tensor(self.wr[:, j % 4, 1], self.wb[:, j % 4], self.wr[:, j % 4, 0].bitcast(F32),
                                  ALU.subtract).then_inc(self.w_lo, 1)

            def product(n, j):
                dve.wait_ge(self.silu, part * NU + n + 1)
                dve.wait_ge(self.up2, part * NU + n + 1)
                self.free(dve, self.h_lo, part, n, 2)
                dve.tensor_tensor(self.hid[:, j % 2], self.gate[:, j % 2], ps[:, 4 + j % 2, :], ALU.mult
                                  ).then_inc(self.prod, 1)

            def rest(n, j):
                dve.wait_ge(self.h_hi, part * NU + n + 1)
                dve.tensor_tensor(self.hlo[:, j % 2], self.hid[:, j % 2], self.hh[:, j % 2].bitcast(F32),
                                  ALU.subtract).then_inc(self.h_lo, 1)

            def result(n, j, i):
                dve.wait_ge(self.down, part * NU + n + 1)
                if not isinstance(n, int) or n >= 4:
                    dve.wait_ge(self.stored[j % 4], self.filled(part, j, i) - 16)
                elif part:
                    dve.wait_ge(self.stored[j % 4], 16 * ((NU + 3 - j) // 4))
                y = ps[:, 6 + j % 2, :].rearrange("p (s a c) -> p s c a", s=4, a=2)
                dve.tensor_reduce(self.yb[:, j % 4].rearrange("p (s c) -> p s c", c=C), y, AX.X, ALU.add
                                  ).then_inc(self.y_out, 1)

            def step(n, j, i):
                peeled = isinstance(n, int)
                if peeled and n >= 1:
                    result(n - 1, (j + 3) % 4, (n - 1) // 4)
                if not peeled:
                    result(n - 1, (j + 3) % 4, i if j else i - 1)
                if not peeled or n + 3 < NU:
                    weights(n + 3, j + 3)
                if not peeled or n + 2 < NU:
                    product(n + 2, j + 2)
                if not peeled or n + 1 < NU:
                    rest(n + 1, j + 1)
            for n in range(3):
                weights(n, n)
            for n in range(2):
                product(n, n)
            rest(0, 0)
            self.steps(dve, step)
            result(NU - 1, (NU - 1) % 4, (NU - 1) // 4)

    def combine(self, dve, then, part):
        for j in range(4):
            self.combine_quarter(dve, then, part, j)

    def combine_quarter(self, dve, then, part, j):
        TQ = TH // 4
        dve.wait_ge(self.gathered[part * 4 + j], 16 * 2 * TQ)
        t0 = part * TH + j * TQ
        x = self.X[:].rearrange("p q a (b c) -> p (q a b) c", b=2)[:, t0:t0 + TQ]
        for k in range(2):
            y = self.GY[part][:, k, j * TQ:(j + 1) * TQ]
            share = self.mx[:, part, 4 + k, j * TQ:(j + 1) * TQ].unsqueeze(2).to_broadcast([P, TQ, C])
            then(dve.tensor_tensor(y, y, share, ALU.mult))
            then(dve.tensor_tensor(x, x, y, ALU.add))


def stage_mixture(nc, sem, mix, first, ready, weights_in, outlives=None):
    with ExitStack() as st:
        ps = st.enter_context(nc.psum_tensor(mix.L + "ps", [P, 8, BANK], F32))
        mix.blocks_room(st, sem, outlives)
        mix.routing_room(st, "m", range(first, PARTS), ps[:], xm=mix.GY[0][:, 0].rearrange("p t c -> p (t c)").rearrange(
            "p (q a c) -> p q a c", a=2, c=2 * C),
            own=mix.GY[0][:, 1].rearrange("p t c -> p (t c)")[:, 0:NBLK * E].rearrange("p (n e) -> p n e", e=E))
        with nc.Block() as block:
            @block.sync
            def _(sp):
                if not first:
                    mix.load_gate(sp)
                sp.wait_ge(*weights_in)
                mix.sync(sp)

            @block.gpsimd
            def _(pool):
                pool.wait_ge(*ready)
                for part in range(first, PARTS):
                    mix.scatter(pool, part)
                for part in range(PARTS - 1):
                    mix.gather(pool, part)

            @block.tensor
            def _(pe):
                for part in range(first, PARTS):
                    mix.route_tensor(pe, part)
                mix.tensor(pe)

            @block.scalar
            def _(act):
                for part in range(first, PARTS):
                    mix.route_scalar(act, part)
                mix.scalar(act)

            @block.vector
            def _(dve):
                then = counter(dve, mix.own_v)
                for part in range(first, PARTS):
                    mix.route_vector(dve, then, part, (lambda: None) if part else (lambda: mix.split_gate(dve)))
                mix.vector(dve, then)
                if outlives is None:
                    for part in range(PARTS - 1):
                        mix.combine(dve, then, part)


def load_linear(sp, A, LW, loaded, zeroed):
    for k in range(2):
        rows = slice(k * C, (k + 1) * C)
        sp.dma_start(LW["wraw"][rows].rearrange("p a c -> p (a c)"), A["L3_attn_qkv_w"]).then_inc(loaded, 16)
        bias = A["L3_attn_qkv_b"].rearrange("(s h d) -> s d h", s=2, d=C)
        sp.dma_start(LW["bq"][rows], bias[0], allow_slow_non_contiguous=True).then_inc(loaded, 16)
        sp.dma_start(LW["bv"][rows], bias[1], allow_slow_non_contiguous=True).then_inc(loaded, 16)
        sp.dma_start(LW["lb"][rows], A["L3_attn_lunchbox"]).then_inc(loaded, 16)
    sp.dma_start(LW["praw"][:], A["L3_attn_proj_w"].rearrange("(j p) o -> p j o", p=P)).then_inc(loaded, 16)
    sp.wait_ge(*zeroed)
    sp.dma_start(LW["pbias"][0:C], A["L3_attn_proj_b"].rearrange("(o a) -> o a", a=1)).then_inc(loaded, 16)
    sp.wait_ge(loaded, 160)


def stage_linear(nc, sem, A, K, X, WR, weights_in, LW, mix, mix_next):
    SCALE = 1.0 / 8.0
    BC = 4
    NC3 = B // BC
    KP = NC3 // PARTS
    BP = B // PARTS
    with ExitStack() as st:
        def sb(name, shape, dt=F32):
            return st.enter_context(nc.sbuf_tensor("l_" + name, shape, dt))
        ps = st.enter_context(nc.psum_tensor("l_ps", [P, 8, BANK], F32))
        xn = sb("xn", [P, B // PARTS, 2, C])
        xT = sb("xT", [P, B // PARTS, P])
        sx = sb("sx", [P, B])
        wv = sb("wv", [P, H3, 2, C])
        wq = sb("wq", [P, H3, 2, C])
        pw = sb("pw", [P, 4, 2, C], F32R)
        wraw, praw, pbias, bq, bv, lb = (LW[n] for n in ("wraw", "praw", "pbias", "bq", "bv", "lb"))
        ls = sb("ls", [P, 1])
        gain = sb("gain", [P, H3, B])
        vg = sb("vg", [P, 4, BC * P])
        vh = sb("vh", [P, 2, H3, BC * P], F32R)
        vl = sb("vl", [P, 2, H3, BC * P], F32R)
        oT = sb("oT", [P, 2, BC, 2, H3, 16])
        own_v, normed, w_ready = (sem("l_" + n) for n in ("ov", "nm", "wr"))
        xt_mm, xt_ev, g_mm, sx_ready = (sem("l_" + n) for n in ("xm", "xe", "gm", "sx"))
        v_mm, v_ev, vh_done, vl_done, o_mm, o_ev, t_mm, t_ev = (
            sem("l_" + n) for n in ("vm", "ve", "vh", "vl", "om", "oe", "tm", "te"))

        def out(g):
            k = NT // G
            pairs = []
            for par in range(2):
                src = ln.xm[:, g % 2 * QG:(g % 2 + 1) * QG, par, :].rearrange("p q (b c) -> p q b c", b=2)
                dst = xn[:, g % 2 * 2 * QG:(g % 2 + 1) * 2 * QG, par, :].rearrange("p (q b) c -> p q b c", b=2)
                r = ln.r[:, g * k:(g + 1) * k].rearrange("p (q a b) -> p q a b", a=2, b=2)[:, :, par, :]
                pairs.append((dst, src, r.unsqueeze(3).to_broadcast([P, QG, 2, C])))
            return pairs
        ln = LayerNorm(nc, sem, st, "l_", X, out, normed,
                       room=xT[:].rearrange("p b n -> p (b n)").rearrange("p (q a c) -> p q a c", a=2, c=2 * C))

        def lend(t, a, b):
            return t[:, a * TH * E:(a + 1) * TH * E].rearrange("p (x y) -> p x y", x=b)
        vgf, oTf = vg[:].rearrange("p k n -> p (k n)"), oT[:].rearrange("p g b a h m -> p (g b a h m)")
        mix_next.routing_room(st, "l", range(1), ps[:], sq=ln.sq, xs=vh[:, 0, 0:4],
                              **{name: lend(vgf, k, TH) for k, name in enumerate(("lg", "key", "one1"))},
                              **{name: lend(oTf, k, E) for k, name in enumerate(("cum", "off"))},
                              tot=vh[:, 0, 4].rearrange("p (e t) -> p e t", e=E),
                              xm=xn[:].rearrange("p b a c -> p (b a c)").rearrange("p (q a c) -> p q a c", a=2, c=2 * C))

        with nc.Block() as block:
            @block.sync
            def _(sp):
                mix_next.load_gate(sp)
                load_weights(sp, A, "L3_ffn", WR, weights_in)

            @block.gpsimd
            def _(pool):
                mix.gather(pool, PARTS - 1)
                mix_next.scatter(pool, 0)

            @block.tensor
            def _(pe):
                def channel_major(k):
                    pe.wait_ge(normed, k // 2 + 1)
                    if k >= 2:
                        pe.wait_ge(xt_ev, k - 1)
                    for u in range(4):
                        ins = pe.transpose(ps[:, k % 2, u * P:(u + 1) * P],
                                           xn[:, (4 * k + u) % BP].rearrange("p a c -> p (a c)"), K["ident"][:])
                    ins.then_inc(xt_mm, 1)

                def sums(part):
                    pe.wait_ge(w_ready, 4)
                    pe.wait_ge(sx_ready, part + 1)
                    for h in range(H3):
                        ins = pe.matmul(ps[:, 2, h * BP:(h + 1) * BP], wq[:, h].rearrange("p a c -> p (a c)"),
                                        sx[:, part * BP:(part + 1) * BP], start=True, stop=True)
                    ins.then_inc(g_mm, 1)

                def value(n):
                    k, h = n // H3, n % H3
                    if n >= 2:
                        pe.wait_ge(v_ev, n - 1)
                    if k % KP == 0 and h < 2:
                        pe.wait_ge(xt_ev, k + KP)
                    pe.matmul(ps[:, n % 2, :], wv[:, h].rearrange("p a c -> p (a c)"),
                              xT[:, BC * (k % KP):BC * (k % KP + 1)].rearrange("p b n -> p (b n)"), start=True, stop=True
                              ).then_inc(v_mm, 1)

                def project(k, step):
                    half, jj = step // 4, step % 4
                    if jj == 0:
                        if k >= 2:
                            pe.wait_ge(o_ev, 4 * (k - 1))
                        pe.wait_ge(vl_done, k * H3 + (half + 1) * H3 // 2)
                    for part, v in enumerate((vh, vl)):
                        v = v[:, k % 2].rearrange("p h n -> p (h n)")
                        ins = pe.matmul(ps[:, 3 + 2 * (k % 2) + half, :], pw[:, jj].rearrange("p a c -> p (a c)"),
                                        v[:, half * 2048 + jj:(half + 1) * 2048:4],
                                        start=(jj == 0 and part == 0), stop=(jj == 3 and part == 1))
                    if jj == 3:
                        ins.then_inc(o_mm, 1)

                def turn(k, step):
                    b, par = step // 2, step % 2
                    if step == 0:
                        pe.wait_ge(o_ev, 4 * (k + 1))
                        if k >= 1:
                            pe.wait_ge(t_ev, 2 * k)
                    ins = pe.transpose(ps[:, (7, 2)[b // 2], step % 4 * P:(step % 4 + 1) * P],
                                       oT[:, k % 2, b, par].rearrange("p h m -> p (h m)"), K["ident"][:])
                    if step == 7:
                        ins.then_inc(t_mm, 1)

                def tokens(part):
                    for k in range(part * KP, (part + 1) * KP):
                        channel_major(k)

                def next_tokens():
                    pe.wait_ge(mix_next.tr_ev, 2 * KP)
                    tokens(1)

                tokens(0)
                for part in range(PARTS):
                    sums(part)
                    for k in range(part * KP - 1, (part + 1) * KP + 1):
                        for step in range(H3):
                            if k + 1 < (part + 1) * KP:
                                value((k + 1) * H3 + step)
                            if part * KP <= k < (part + 1) * KP:
                                project(k, step)
                            if k - 1 >= part * KP:
                                turn(k - 1, step)
                    if part == 0:
                        pe.wait_ge(v_ev, KP * H3)
                        pe.wait_ge(o_ev, 4 * KP)
                        pe.wait_ge(t_ev, 2 * KP)
                        mix_next.route_tensor(pe, 0, next_tokens)

            @block.scalar
            def _(act):
                def high(k, h):
                    n = k * H3 + h
                    act.wait_ge(v_ev, n + 1)
                    if k >= 2:
                        act.wait_ge(o_mm, 2 * (k - 1))
                    act.copy(vh[:, k % 2, h], vg[:, n % 4]).then_inc(vh_done, 1)

                def out_rows(k, half):
                    act.wait_ge(o_mm, 2 * k + half + 1)
                    if k >= 2:
                        act.wait_ge(t_mm, k - 1)
                    src = ps[:, 3 + 2 * (k % 2) + half, :].rearrange("p (h b m a) -> p a h b m", h=4, b=BC, a=2)
                    for par in range(2):
                        act.activation(oT[:, k % 2, :, par, 4 * half:4 * half + 4, :].rearrange("p b h m -> p h b m"),
                                       src[:, par], ACT.Identity, bias=pbias[:]).then_inc(o_ev, 1)

                def tokens(part):
                    ln.part_scalar(act, part)
                    for k in range(part * KP, (part + 1) * KP):
                        act.wait_ge(xt_mm, k + 1)
                        act.copy(xT[:, 4 * (k % KP):4 * (k % KP) + 4].rearrange("p b n -> p (b n)"), ps[:, k % 2, :]).then_inc(xt_ev, 1)

                tokens(0)
                for part in range(PARTS):
                    for k in range(part * KP, (part + 1) * KP):
                        for h in range(H3):
                            high(k, h)
                            if k % KP and h in (3, 7):
                                out_rows(k - 1, h // 4)
                    for half in range(2):
                        out_rows((part + 1) * KP - 1, half)
                    if part == 0:
                        mix_next.route_scalar(act, 0, lambda: tokens(1))

            @block.vector
            def _(dve):
                then = counter(dve, own_v)

                def prepare():
                    then(dve.memset(wv[:], 0.0))
                    for k in range(2):
                        rows = slice(k * C, (k + 1) * C)
                        dve.tensor_copy(wv[rows, :, k, :], wraw[rows, H3:2 * H3, :]).then_inc(w_ready, 1)
                    dve.tensor_copy(wq[:], wraw[:, 0:H3, :].unsqueeze(2).to_broadcast([P, H3, 2, C])).then_inc(w_ready, 1)
                    then(dve.tensor_copy(pw[:, :, 0, :], praw[:]))
                    dve.tensor_tensor(pw[:, :, 1, :], praw[:], pw[:, :, 0, :].bitcast(F32), ALU.subtract).then_inc(w_ready, 1)
                    then(dve.tensor_reduce(ls[:], lb[:], AX.X, ALU.add))
                    then(dve.tensor_scalar(ls[:], ls[:], SCALE, None, ALU.mult))
                    then(dve.tensor_scalar(bq[:], bq[:], float(N), None, ALU.mult))

                def gains(part):
                    b = slice(part * BP, (part + 1) * BP)
                    dve.wait_ge(xt_ev, (part + 1) * KP)
                    dve.tensor_reduce(sx[:, b], xT[:], AX.X, ALU.add).then_inc(sx_ready, 1)
                    dve.wait_ge(g_mm, part + 1)
                    then(dve.tensor_tensor(gain[:, :, b], ps[:, 2, 0:H3 * BP].rearrange("p (h b) -> p h b", b=BP),
                                           bq[:].unsqueeze(2).to_broadcast([P, H3, BP]), ALU.add))
                    then(dve.tensor_scalar(gain[:, :, b], gain[:, :, b], ls[:], None, ALU.mult))

                def value(n):
                    k, h = n // H3, n % H3
                    dve.wait_ge(v_mm, n + 1)
                    if n >= 4:
                        dve.wait_ge(vl_done, n - 3)
                    dve.scalar_tensor_tensor(
                        out=vg[:, n % 4].rearrange("p (b n) -> p b n", b=BC),
                        in0=ps[:, n % 2, :].rearrange("p (b n) -> p b n", b=BC), scalar=bv[:, h:h + 1],
                        in1=gain[:, h, BC * k:BC * (k + 1)].unsqueeze(2).to_broadcast([P, BC, P]),
                        op0=ALU.add, op1=ALU.mult).then_inc(v_ev, 1)

                def low(n):
                    dve.wait_ge(vh_done, n + 1)
                    dve.tensor_tensor(vl[:, n // H3 % 2, n % H3], vg[:, n % 4], vh[:, n // H3 % 2, n % H3].bitcast(F32),
                                      ALU.subtract).then_inc(vl_done, 1)

                def residual(k):
                    dve.wait_ge(t_mm, k + 1)
                    for half in range(2):
                        for u in range(2):
                            x = X[:, 2 * k + u].rearrange("p a (b c) -> p a b c", b=2)
                            t = ps[:, (7, 2)[u], :].rearrange("p (b a h c) -> p h a b c", b=2, a=2, h=2)[:, half]
                            ins = dve.tensor_tensor(x, x, t, ALU.add)
                            if half:
                                ins.then_inc(t_ev, 1)
                        if not half:
                            then(ins)

                def last_tokens():
                    mix.combine(dve, then, PARTS - 1)
                    ln.part_vector(dve, then, 1)

                for part in range(PARTS):
                    if part == 0:
                        ln.part_vector(dve, then, 0)
                        prepare()
                    else:
                        mix_next.split_gate(dve)
                        mix_next.route_vector(dve, then, 0, last_tokens)
                    gains(part)
                    value(part * KP * H3)
                    for n in range(part * KP * H3, (part + 1) * KP * H3):
                        if (n + 1) % (KP * H3):
                            value(n + 1)
                        low(n)
                        k = n // H3
                        if n % H3 == H3 - 1 and k % KP >= 2:
                            residual(k - 2)
                    residual((part + 1) * KP - 2)
                    residual((part + 1) * KP - 1)


def stage_out(nc, sem, K, X, out, mix):
    with ExitStack() as st:
        ps = st.enter_context(nc.psum_tensor("o_ps", [P, 4, BANK], F32))
        Y = st.enter_context(nc.sbuf_tensor("o_y", [P, Q, N], F32))
        mm, ev, stored, added = (sem("o_" + n) for n in ("mm", "ev", "st", "ad"))
        out_v = out.rearrange("(q b) c y w -> (b c) q (y w)", b=2)
        with nc.Block() as block:
            @block.gpsimd
            def _(pool):
                mix.gather(pool, PARTS - 1)

            @block.tensor
            def _(pe):
                for k in range(Q // 2):
                    if k >= 4:
                        pe.wait_ge(ev, k - 3)
                    pe.wait_ge(added, 4 * (k + 1))
                    for u in range(4):
                        ins = pe.transpose(ps[:, k % 4, u * P:(u + 1) * P], X[:, 2 * k + u // 2, u % 2, :], K["ident"][:])
                    ins.then_inc(mm, 1)

            def move(eng, copy, k):
                eng.wait_ge(mm, k + 1)
                copy(Y[:, 2 * k:2 * k + 2].rearrange("p q (n a) -> p q a n", a=2),
                     ps[:, k % 4, :].rearrange("p (q a n) -> p q a n", q=2, a=2)).then_inc(ev, 1)

            @block.scalar
            def _(act):
                for k in range(Q // 2):
                    move(act, act.copy, k)

            @block.vector
            def _(dve):
                then = counter(dve, added)
                for part in range(PARTS):
                    mix.combine(dve, then, part)

            @block.sync
            def _(sp):
                for k in range(Q // 2):
                    sp.wait_ge(ev, k + 1)
                    sp.dma_start(out_v[:, 2 * k:2 * k + 2, :], Y[:, 2 * k:2 * k + 2, :]).then_inc(stored, 16)
                sp.wait_ge(stored, 16 * (Q // 2))


def build(nc, A, out):
    with ExitStack() as ctx:
        def sb(name, shape, dt=F32):
            return ctx.enter_context(nc.sbuf_tensor(name, shape, dt))

        used = []

        def sem(name):
            used.append(nc.alloc_semaphore(name=name))
            return used[-1]

        def reuse(keep=()):
            nc.clear_and_free_semaphores([s for s in used if s not in keep])
            nc.all_engine_barrier()
            used[:] = keep
        X = sb("X", [P, Q, 2, 2 * C])
        K = {"ident": sb("ident", [P, P]), "iota": sb("iota", [P, NBLK]),
             "fill": sb("fill", [P, TH * P // BS]), "reset": sb("reset", [P, E * TH]),
             "upper": sb("upper", [P, P], F32R), "ones": sb("ones", [P, P], F32R)}
        XD = [nc.dram_tensor(f"blocks_x{h}", (NBLK * BS, P), F32, kind="Internal").ap() for h in range(PARTS)]
        YD = [nc.dram_tensor(f"blocks_y{h}", (NBLK * BS, C), F32, kind="Internal").ap() for h in range(PARTS)]
        zeroed, weights_in = nc.alloc_semaphore(name="zeroed"), nc.alloc_semaphore(name="weights_in")
        with ExitStack() as st:
            def tmp(name, shape, dt=F32):
                return st.enter_context(nc.sbuf_tensor(name, shape, dt))
            Xc = tmp("Xc", [P, Q, N])
            wproj = tmp("wproj", [P, 2, C])
            FM = tmp("FM", [P, Q, 2, 2 * C])
            V = tmp("V", [P, Q, 2, 2 * C + 4])
            QKf = tmp("QKf", [P, Q, 2, 4 * C])
            with ExitStack() as st2:
                xn = st2.enter_context(nc.sbuf_tensor("xn0", [P, Q, N], F32))
                wqkv = st2.enter_context(nc.sbuf_tensor("wqkv", [P, 3, 2, C], F32))
                brow = st2.enter_context(nc.sbuf_tensor("brow", [P, 3, 2, C], F32R))
                rows2 = st2.enter_context(nc.sbuf_tensor("rows2", [P, P], F32R))
                rowk = st2.enter_context(nc.sbuf_tensor("rowk", [KS * WW, HD, 2, 8], F32))
                epsv = st2.enter_context(nc.sbuf_tensor("epsv", [P, C], F32))
                stage_norm(nc, sem, A, K, Xc, xn, wqkv, brow, rows2, wproj, rowk, epsv)
                stage_qkv(nc, sem, A, K, xn, wqkv, brow, rows2, rowk, epsv, QKf, V, FM,
                          S=X[:].rearrange("p (g q) a c -> p g (q a c)", g=2))
            WR = ctx.enter_context(nc.sbuf_tensor("WR", [P, E, WC], F32, side="right"))
            zeros = ctx.enter_context(nc.sbuf_tensor("zeros", [P, 4 * P], F32, side="right"))
            stage_attend(nc, sem, A, K, Xc, QKf, V, FM, wproj, X, WR, XD, zeros, zeroed, weights_in)
        reuse()
        LW = {name: sb("lw_" + name, [P] + shape) for name, shape in (
            ("wraw", [2 * H3, C]), ("praw", [4, C]), ("pbias", [1]), ("bq", [H3]), ("bv", [H3]), ("lb", [32]))}
        stage_pool(nc, sem, A, K, X, LW)
        GY_last = sb("gy_last", [P, 2, TH, C])
        mix1 = Mixture(nc, sem, ctx, A, K, X, "L2_ffn", WR, XD, YD, GY_last)
        stage_mixture(nc, sem, mix1, 0, (zeroed, 16 * PARTS), (weights_in, 80))
        reuse(keep=mix1.gathered)
        mix2 = Mixture(nc, sem, ctx, A, K, X, "L3_ffn", WR, XD, YD, GY_last)
        kept = list(used)
        stage_linear(nc, sem, A, K, X, WR, weights_in, LW, mix1, mix2)
        reuse(keep=[s for s in kept if s not in mix1.gathered])
        stage_mixture(nc, sem, mix2, 1, (zeroed, 16 * PARTS), (weights_in, 160), outlives=ctx)
        reuse(keep=mix2.gathered)
        stage_out(nc, sem, K, X, out, mix2)


def shape_constants():
    pos = np.zeros((5, 4, P), np.float32)
    for r in range(P):
        for j in range(4):
            n = (r % C) * 4 + j
            jj, ii = np.float32(n % WW) / np.float32(WW - 1), np.float32(n // WW) / np.float32(HH - 1)
            pos[:, j, r] = (jj, ii, np.float32(1) - jj, np.float32(1) - ii, 1)
    pairs = np.kron(np.eye(P // 2), np.full((2, 2), 0.5)).astype(np.float32)
    mask = np.kron(np.eye(P // HD), np.ones((HD, HD))).astype(np.float32)
    selx = np.zeros((KS, KS, WW, KS, WW), np.float32)
    for dy in range(KS):
        for ix in range(WW):
            for jx in range(WW):
                if 0 <= jx - ix + KS // 2 < KS:
                    selx[dy, jx - ix + KS // 2, ix, dy, jx] = 1
    sely = np.zeros((KS, WW, 2, 2 * HH - 1, WW // 2), np.float32)
    for dy in range(KS):
        for jx in range(WW):
            sely[dy, jx, jx % 2, dy - KS // 2 + HH - 1, jx // 2] = 1
    return {
        "k_pos": pos, "k_pairs": pairs, "k_mask": mask, "k_ident": np.eye(P, dtype=np.float32),
        "k_selx": selx.reshape(KS * KS, WW, KS * WW), "k_sely": sely.reshape(KS * WW, 2, -1),
        
        "k_iota": np.tile(np.arange(NBLK, dtype=np.float32), (P, 1)),
        "k_fill": np.tile(np.arange(TH * P // BS, dtype=np.float32) * BS, (P, 1)),
        "k_reset": np.tile((np.arange(E * TH) % TH > 0).astype(np.float32), (P, 1)),
        "k_upper": np.triu(np.ones((P, P), np.float32), 1),
    }


_INS = ['x', 'L0_conv_W', 'L0_conv_b', 'L1_conv_Wq', 'L1_conv_bq', 'L1_conv_Wkv', 'L1_conv_bkv', 'L1_conv_Wproj',
        'L1_conv_bproj', 'L1_conv_dwc_w', 'L1_conv_dwc_b', 'L1_conv_scale_param', 'L2_attn_fc_w', 'L2_attn_fc_b',
        'L2_attn_score_w', 'L2_ffn_gate_w', 'L2_ffn_gate_b', 'L2_ffn_w1', 'L2_ffn_w2', 'L2_ffn_w3', 'L3_attn_qkv_w',
        'L3_attn_qkv_b', 'L3_attn_lunchbox', 'L3_attn_proj_w', 'L3_attn_proj_b', 'L3_ffn_gate_w', 'L3_ffn_gate_b',
        'L3_ffn_w1', 'L3_ffn_w2', 'L3_ffn_w3']


def kernel(**inputs):
    import concourse.bacc as bacc
    from concourse.bass_utils import run_bass_kernel_spmd

    nc = bacc.Bacc("TRN2", target_bir_lowering=False, num_devices=1)
    arrays, A = {}, {}
    for name, a in [(n, inputs[n]) for n in _INS] + list(shape_constants().items()):
        a = np.ascontiguousarray(a)
        arrays[f"in_{name}"] = a
        A[name] = nc.dram_tensor(f"in_{name}", a.shape, mybir.dt.from_np(a.dtype), kind="ExternalInput").ap()
    out = nc.dram_tensor("out_x", (B, C, HH, WW), F32, kind="ExternalOutput").ap()
    build(nc, A, out)
    r = run_bass_kernel_spmd(nc, [arrays], core_ids=[0])
    return r.results[0]["out_x"]
```
